# Optimizing a Trainium2 kernel written in Bass

```python
import numpy as np
import jax
import jax.numpy as jnp

def _softmax(x, axis=-1):
    return jax.nn.softmax(x, axis=axis)

def _gelu(x):
    return jax.nn.gelu(x, approximate=True)

def _silu(x):
    return jax.nn.silu(x)

def _sigmoid(x):
    return jax.nn.sigmoid(x)

def _layernorm(x, axis=-1, eps=1e-05):
    m = jnp.mean(x, axis=axis, keepdims=True)
    v = jnp.var(x, axis=axis, keepdims=True)
    return (x - m) / jnp.sqrt(v + eps)

def _scatter_add(tgt, idx, src, axis=0):
    return tgt.at[idx].add(src)

def _segment_sum(src, seg, n):
    return jax.ops.segment_sum(src, seg, n)
kernel_name = 'mk_recurrent_d2_jaxref_r8_bc4d9f'

def setup_inputs(seed: int=0):
    np.random.seed(seed)
    _w = jnp.asarray

    def _L0_attn_setup():
        import math
        import jax, jax.numpy as jnp
        import numpy as np
        HEADS = 16
        DIM_HEAD = 64
        NUM_NULL_KV = 2
        ATTN_SCALE = 8.0
        LN_EPS = 1e-05

        def _alibi_slopes(heads):
            start = 2.0 ** (-2.0 ** (-(math.log2(heads) - 3.0)))
            return np.array([start * start ** i for i in range(heads)], dtype=np.float32)

        def _l2norm(t):
            return t / jnp.maximum(jnp.linalg.norm(t, axis=-1, keepdims=True), 1e-12)
        key = jax.random.key(seed)
        ks = jax.random.split(key, 5)
        b, n, dim = (4, 256, 128)
        return {'x': jax.random.normal(ks[0], (b, n, dim), dtype=jnp.float32), 'gamma': jnp.ones((dim,), dtype=jnp.float32), 'w_q': jax.random.normal(ks[1], (dim, HEADS * DIM_HEAD), dtype=jnp.float32) * 0.02, 'w_kv': jax.random.normal(ks[2], (dim, 2 * HEADS * DIM_HEAD), dtype=jnp.float32) * 0.02, 'null_kv': jax.random.normal(ks[3], (HEADS, 2 * NUM_NULL_KV, DIM_HEAD), dtype=jnp.float32), 'q_scale': jnp.ones((DIM_HEAD,), dtype=jnp.float32), 'k_scale': jnp.ones((DIM_HEAD,), dtype=jnp.float32), 'w_out': jax.random.normal(ks[4], (HEADS * DIM_HEAD, dim), dtype=jnp.float32) * 0.02}
    _L0_attn_in = _L0_attn_setup()

    def _L0_ffn_setup():
        import jax, jax.numpy as jnp
        import numpy as np
        B, T, D, DFF, E = (4, 256, 128, 512, 8)
        key = jax.random.key(seed)
        ks = jax.random.split(key, 4)
        s_in = 1.0 / np.sqrt(D)
        s_ff = 1.0 / np.sqrt(DFF)
        return {'x': jax.random.normal(ks[0], (B, T, D), dtype=jnp.float32), 'gate_W': jax.random.normal(ks[1], (D, E), dtype=jnp.float32) * s_in, 'gate_b': jnp.zeros((E,), dtype=jnp.float32), 'W1': jax.random.normal(ks[2], (E, D, DFF), dtype=jnp.float32) * s_in, 'b1': jnp.zeros((E, DFF), dtype=jnp.float32), 'W2': jax.random.normal(ks[3], (E, DFF, D), dtype=jnp.float32) * s_ff, 'b2': jnp.zeros((E, D), dtype=jnp.float32)}
    _L0_ffn_in = _L0_ffn_setup()

    def _L1_attn_setup():
        import jax, jax.numpy as jnp
        import numpy as np
        DIM_Q = 128
        DIM_K = 128
        DIM_V = 128
        OUT_DIM = 128
        B, N = (4, 256)

        def _layer_norm(h, gamma, beta, eps=1e-05):
            mu = jnp.mean(h, axis=-1, keepdims=True)
            var = jnp.mean(jnp.square(h - mu), axis=-1, keepdims=True)
            return (h - mu) * jax.lax.rsqrt(var + eps) * gamma + beta
        key = jax.random.key(seed)
        ks = jax.random.split(key, 8)
        s_in = 1.0 / np.sqrt(DIM_Q)
        s_v = 1.0 / np.sqrt(DIM_V)
        return {'x': jax.random.normal(ks[0], (B, N, DIM_Q), dtype=jnp.float32), 'Wq': jax.random.normal(ks[1], (DIM_Q, DIM_K), dtype=jnp.float32) * s_in, 'Wk': jax.random.normal(ks[2], (DIM_Q, DIM_K), dtype=jnp.float32) * s_in, 'Wv': jax.random.normal(ks[3], (DIM_Q, DIM_V), dtype=jnp.float32) * s_in, 'Wfc': jax.random.normal(ks[4], (DIM_V, OUT_DIM), dtype=jnp.float32) * s_v, 'bfc': jax.random.normal(ks[5], (OUT_DIM,), dtype=jnp.float32) * 0.02, 'gamma': jnp.ones((DIM_V,), dtype=jnp.float32), 'beta': jnp.zeros((DIM_V,), dtype=jnp.float32)}
    _L1_attn_in = _L1_attn_setup()

    def _L1_ffn_setup():
        import jax, jax.numpy as jnp
        import numpy as np
        B, S, D, F, E, K = (2, 256, 128, 512, 8, 2)
        key = jax.random.key(seed)
        ks = jax.random.split(key, 5)
        x = jax.random.normal(ks[0], (B, S, D), dtype=jnp.float32)
        Wg = jax.random.normal(ks[1], (D, E), dtype=jnp.float32) * 0.02
        W1 = jax.random.normal(ks[2], (E, D, F), dtype=jnp.float32) * 0.02
        b1 = jnp.zeros((E, F), dtype=jnp.float32)
        W2 = jax.random.normal(ks[3], (E, F, D), dtype=jnp.float32) * 0.02
        b2 = jnp.zeros((E, D), dtype=jnp.float32)
        return {'x': x, 'Wg': Wg, 'W1': W1, 'b1': b1, 'W2': W2, 'b2': b2}
    _L1_ffn_in = _L1_ffn_setup()
    _d = {'L0_attn_x': _L0_attn_in['x'], 'L0_attn_gamma': _L0_attn_in['gamma'], 'L0_attn_w_q': _L0_attn_in['w_q'], 'L0_attn_w_kv': _L0_attn_in['w_kv'], 'L0_attn_null_kv': _L0_attn_in['null_kv'], 'L0_attn_q_scale': _L0_attn_in['q_scale'], 'L0_attn_k_scale': _L0_attn_in['k_scale'], 'L0_attn_w_out': _L0_attn_in['w_out'], 'L0_ffn_gate_W': _L0_ffn_in['gate_W'], 'L0_ffn_gate_b': _L0_ffn_in['gate_b'], 'L0_ffn_W1': _L0_ffn_in['W1'], 'L0_ffn_b1': _L0_ffn_in['b1'], 'L0_ffn_W2': _L0_ffn_in['W2'], 'L0_ffn_b2': _L0_ffn_in['b2'], 'L1_attn_Wq': _L1_attn_in['Wq'], 'L1_attn_Wk': _L1_attn_in['Wk'], 'L1_attn_Wv': _L1_attn_in['Wv'], 'L1_attn_Wfc': _L1_attn_in['Wfc'], 'L1_attn_bfc': _L1_attn_in['bfc'], 'L1_attn_gamma': _L1_attn_in['gamma'], 'L1_attn_beta': _L1_attn_in['beta'], 'L1_ffn_Wg': _L1_ffn_in['Wg'], 'L1_ffn_W1': _L1_ffn_in['W1'], 'L1_ffn_b1': _L1_ffn_in['b1'], 'L1_ffn_W2': _L1_ffn_in['W2'], 'L1_ffn_b2': _L1_ffn_in['b2']}
    _x0 = _d['L0_attn_x']
    _d['L0_attn_x'] = jax.random.normal(jax.random.fold_in(jax.random.key(seed), 1), (16, 256, 128), dtype=_x0.dtype)
    del _x0
    return _d

def reference(L0_attn_x, L0_attn_gamma, L0_attn_w_q, L0_attn_w_kv, L0_attn_null_kv, L0_attn_q_scale, L0_attn_k_scale, L0_attn_w_out, L0_ffn_gate_W, L0_ffn_gate_b, L0_ffn_W1, L0_ffn_b1, L0_ffn_W2, L0_ffn_b2, L1_attn_Wq, L1_attn_Wk, L1_attn_Wv, L1_attn_Wfc, L1_attn_bfc, L1_attn_gamma, L1_attn_beta, L1_ffn_Wg, L1_ffn_W1, L1_ffn_b1, L1_ffn_W2, L1_ffn_b2):

    def _L0_attn_ref(x, gamma, w_q, w_kv, null_kv, q_scale, k_scale, w_out):
        import math
        import jax, jax.numpy as jnp
        import numpy as np
        HEADS = 16
        DIM_HEAD = 64
        NUM_NULL_KV = 2
        ATTN_SCALE = 8.0
        LN_EPS = 1e-05

        def _alibi_slopes(heads):
            start = 2.0 ** (-2.0 ** (-(math.log2(heads) - 3.0)))
            return np.array([start * start ** i for i in range(heads)], dtype=np.float32)

        def _l2norm(t):
            return t / jnp.maximum(jnp.linalg.norm(t, axis=-1, keepdims=True), 1e-12)
        b, n, dim = x.shape
        mu = jnp.mean(x, axis=-1, keepdims=True)
        var = jnp.mean(jnp.square(x - mu), axis=-1, keepdims=True)
        xn = (x - mu) * jax.lax.rsqrt(var + LN_EPS) * gamma
        q = (xn @ w_q).reshape(b, n, HEADS, DIM_HEAD).transpose(0, 2, 1, 3)
        kv = xn @ w_kv
        k, v = jnp.split(kv, 2, axis=-1)
        k = k.reshape(b, n, HEADS, DIM_HEAD).transpose(0, 2, 1, 3)
        v = v.reshape(b, n, HEADS, DIM_HEAD).transpose(0, 2, 1, 3)
        nkv = null_kv.reshape(HEADS, NUM_NULL_KV, 2, DIM_HEAD)
        nk = jnp.broadcast_to(nkv[:, :, 0][None], (b, HEADS, NUM_NULL_KV, DIM_HEAD))
        nv = jnp.broadcast_to(nkv[:, :, 1][None], (b, HEADS, NUM_NULL_KV, DIM_HEAD))
        k = jnp.concatenate([nk, k], axis=2)
        v = jnp.concatenate([nv, v], axis=2)
        q = _l2norm(q) * q_scale
        k = _l2norm(k) * k_scale
        sim = jnp.einsum('bhid,bhjd->bhij', q, k) * ATTN_SCALE
        j = n + NUM_NULL_KV
        rows = jnp.arange(n)
        cols = jnp.arange(j)
        dist = -jnp.abs(cols[None, :] - (rows[:, None] + NUM_NULL_KV)).astype(sim.dtype)
        slopes = jnp.asarray(_alibi_slopes(HEADS))
        sim = sim + dist[None, None] * slopes[None, :, None, None]
        causal_mask = cols[None, :] > rows[:, None] + NUM_NULL_KV
        neg = -jnp.finfo(sim.dtype).max
        sim = jnp.where(causal_mask[None, None], neg, sim)
        attn = jax.nn.softmax(sim, axis=-1)
        out = jnp.einsum('bhij,bhjd->bhid', attn, v)
        out = out.transpose(0, 2, 1, 3).reshape(b, n, HEADS * DIM_HEAD)
        return out @ w_out

    def _L0_ffn_ref(x, gate_W, gate_b, W1, b1, W2, b2):
        import jax, jax.numpy as jnp
        import numpy as np
        B, T, D, DFF, E = (4, 256, 128, 512, 8)
        b, t, d = x.shape
        num_experts = gate_W.shape[-1]
        logits = jnp.einsum('btd,de->bte', x, gate_W) + gate_b
        top1 = jnp.argmax(logits, axis=-1).reshape(-1)
        flat_x = x.reshape(b * t, d)
        out = jnp.zeros_like(flat_x)
        for e in range(num_experts):
            mask = (top1 == e).astype(x.dtype)[:, None]
            h = jax.nn.gelu(flat_x * mask @ W1[e] + b1[e], approximate=False)
            out = out + (h @ W2[e] + b2[e]) * mask
        return out.reshape(b, t, d)

    def _L1_attn_ref(x, Wq, Wk, Wv, Wfc, bfc, gamma, beta):
        import jax, jax.numpy as jnp
        import numpy as np
        DIM_Q = 128
        DIM_K = 128
        DIM_V = 128
        OUT_DIM = 128
        B, N = (4, 256)

        def _layer_norm(h, gamma, beta, eps=1e-05):
            mu = jnp.mean(h, axis=-1, keepdims=True)
            var = jnp.mean(jnp.square(h - mu), axis=-1, keepdims=True)
            return (h - mu) * jax.lax.rsqrt(var + eps) * gamma + beta
        q = jnp.einsum('bnd,dk->bnk', x, Wq)
        k = jnp.einsum('bnd,dk->bnk', x, Wk)
        v = jnp.einsum('bnd,dv->bnv', x, Wv)
        scale = 1.0 / np.sqrt(DIM_K)
        scores = jnp.einsum('bnk,bmk->bnm', q, k) * scale
        n = x.shape[1]
        causal = jnp.tril(jnp.ones((n, n), dtype=bool))
        scores = jnp.where(causal, scores, -jnp.inf)
        att = jax.nn.softmax(scores, axis=-1)
        out = jnp.einsum('bnm,bmv->bnv', att, v)
        out = _layer_norm(out + v, gamma, beta)
        return jnp.einsum('bnv,vo->bno', out, Wfc) + bfc

    def _L1_ffn_ref(x, Wg, W1, b1, W2, b2):
        import jax, jax.numpy as jnp
        import numpy as np
        B, S, D, F, E, K = (2, 256, 128, 512, 8, 2)
        b, s, d = x.shape
        e = Wg.shape[1]
        T = b * s
        C = 2 * K * T // e
        xt = x.reshape(T, d)
        logits = xt.astype(jnp.float32) @ Wg.astype(jnp.float32)
        gates = jax.nn.softmax(logits, axis=-1)
        idx1 = jnp.argmax(gates, axis=-1)
        mask1 = jax.nn.one_hot(idx1, e, dtype=gates.dtype)
        gate1 = jnp.sum(gates * mask1, axis=-1)
        logits2 = jnp.where(mask1 > 0, -jnp.inf, logits)
        idx2 = jnp.argmax(logits2, axis=-1)
        mask2 = jax.nn.one_hot(idx2, e, dtype=gates.dtype)
        gate2 = jnp.sum(gates * mask2, axis=-1)
        denom = gate1 + gate2 + 1e-09
        w1 = gate1 / denom
        w2 = gate2 / denom
        p1 = jnp.cumsum(mask1, axis=0) - mask1
        pos1 = jnp.sum(p1 * mask1, axis=-1).astype(jnp.int32)
        off = jnp.sum(mask1, axis=0)
        p2 = jnp.cumsum(mask2, axis=0) - mask2 + off[None, :]
        pos2 = jnp.sum(p2 * mask2, axis=-1).astype(jnp.int32)
        keep1 = (pos1 < C).astype(xt.dtype)
        keep2 = (pos2 < C).astype(xt.dtype)
        pos1 = jnp.clip(pos1, 0, C - 1)
        pos2 = jnp.clip(pos2, 0, C - 1)
        xe = jnp.zeros((e, C, d), dtype=xt.dtype)
        xe = xe.at[idx1, pos1].add(xt * keep1[:, None])
        xe = xe.at[idx2, pos2].add(xt * keep2[:, None])
        h = jax.nn.gelu(jnp.einsum('ecd,edf->ecf', xe, W1) + b1[:, None, :], approximate=False)
        ye = jnp.einsum('ecf,efd->ecd', h, W2) + b2[:, None, :]
        out = ye[idx1, pos1] * (w1 * keep1)[:, None] + ye[idx2, pos2] * (w2 * keep2)[:, None]
        return out.reshape(b, s, d)
    x = L0_attn_x
    xn = _layernorm(x, axis=-1)
    s = _L0_attn_ref(xn, L0_attn_gamma, L0_attn_w_q, L0_attn_w_kv, L0_attn_null_kv, L0_attn_q_scale, L0_attn_k_scale, L0_attn_w_out)
    g = _silu(_L0_ffn_ref(xn, L0_ffn_gate_W, L0_ffn_gate_b, L0_ffn_W1, L0_ffn_b1, L0_ffn_W2, L0_ffn_b2))
    x = x + s * g
    xn = _layernorm(x, axis=-1)
    s = _L1_attn_ref(xn, L1_attn_Wq, L1_attn_Wk, L1_attn_Wv, L1_attn_Wfc, L1_attn_bfc, L1_attn_gamma, L1_attn_beta)
    g = _silu(_L1_ffn_ref(xn, L1_ffn_Wg, L1_ffn_W1, L1_ffn_b1, L1_ffn_W2, L1_ffn_b2))
    x = x + s * g
    return x

_drawn_inputs = setup_inputs


def setup_inputs(seed=0):
    import zlib

    import numpy as np

    out = dict(_drawn_inputs(seed))
    spreads = {'L0_attn_gamma': (1.0, 0.6),
     'L0_attn_q_scale': (1.0, 0.6),
     'L0_attn_k_scale': (1.0, 0.6),
     'L0_ffn_gate_b': (0.0, 0.755),
     'L0_ffn_b1': (0.0, 0.8),
     'L0_ffn_b2': (0.0, 0.8),
     'L1_attn_gamma': (1.0, 0.6),
     'L1_attn_beta': (0.0, 0.8),
     'L1_ffn_b1': (0.0, 0.8),
     'L1_ffn_b2': (0.0, 0.1)}
    factors = {'L0_attn_w_q': 3.032,
     'L0_attn_null_kv': 3.38,
     'L1_attn_Wq': 8.0,
     'L1_attn_Wk': 8.0,
     'L1_attn_bfc': 21.698,
     'L1_ffn_W1': 2.792}
    for name, (base, spread) in spreads.items():
        noise = np.random.default_rng([zlib.crc32(name.encode()), seed]).standard_normal(out[name].shape)
        drawn = base * np.exp(spread * noise) if base else spread * noise
        out[name] = jnp.asarray(drawn.astype(out[name].dtype))
    for name, factor in factors.items():
        out[name] = (out[name] * factor).astype(out[name].dtype)
    return out
```

```python
import concourse.bass as bass
from concourse import mybir
from contextlib import ExitStack

F32, I32 = mybir.dt.float32, mybir.dt.int32
ACT, ALU, AX = mybir.ActivationFunctionType, mybir.AluOpType, mybir.AxisListType

NB, N, D = 16, 256, 128
P = 128
T = NB * N
NT = T // P
H, DH = 16, 64
HC = H // 2
NNULL = 2
E, DFF = 8, 512
FC = DFF // P
BLK = 256
CAP = 2 * 2 * T // E
NBLK0 = (T + E * (BLK - 1)) // BLK
NBLK1 = (2 * T + E * (BLK - 1)) // BLK
NBUF = 4
WCOLS = 2 * DFF + FC
LOADS = 3 * 16
EPS = 1e-5
NEG = -1e30
BIG = float(1 << 20)
RSQRT_MAGIC = float(0x5F3759DF)
NTHR = T // BLK

C_ID, C_TRI, C_NB, C_M1, C_W8, C_RS, C_THR, C_JJ = 0, 128, 256, 320, 576, 584, 840, 856
C_END = C_JJ + (NBLK1 + 1)

GROUPS = [(0, [8 * (g // 2) + g % 2 + 2 * k for k in range(4)]) for g in range(4)] + \
         [(1, [4 * (g // 2) + g % 2 + 2 * k for k in range(2)]) for g in range(8)]
NG = len(GROUPS)
NU, NQ = 12, 8


def proj_order(with_next):
    uses = []
    for g in range(NG):
        if with_next and g < NU // 2:
            uses += [("unit", 2 * g), ("unit", 2 * g + 1)]
        if g == 6:
            uses += [("out", 0, 0), ("out", 0, 1)]
        if with_next and g in QK_SLOTS:
            uses += [("qk", s) for s in QK_SLOTS[g]]
    return uses + [("out", 1, 0), ("out", 1, 1)]


QK_SLOTS = {6: (0, 1), 7: (2, 3), 10: (4, 5), 11: (6, 7)}
RING_START = NU + NQ
RING_STEP = len(proj_order(True))
UNITS = [(0, 0), (0, 1), (0, 2), (0, 3), (1, 0), (1, 1), (1, 2), (1, 3), (0, 4), (0, 5), (1, 4), (1, 5)]


def block_kernel(nc, a):
    xe = nc.dram_tensor("expert_rows", (NBLK1 * BLK, D), F32).ap()
    ye = nc.dram_tensor("expert_out", (NBLK1 * BLK, D), F32).ap()
    x_v = a["L0_attn_x"].rearrange("b (t p) d -> p (b t) d", p=P)
    out_v = a["out"].rearrange("b (t p) d -> p (b t) d", p=P)

    ctx = ExitStack()
    with ctx:
        def sb(name, shape, dt=F32):
            return ctx.enter_context(nc.sbuf_tensor(name, shape, dt))

        def sem(name):
            return ctx.enter_context(nc.semaphore(name))

        bank = [ctx.enter_context(nc.psum_tensor(f"bank{i}", [P, 512], F32)) for i in range(8)]
        RING, SBANK, OBANK, MISC, TRB = bank[0:2], bank[2:4], bank[4:6], bank[6], bank[7]

        const = sb("const", [P, C_END])
        ident, tri = const[:, C_ID:C_ID + P], const[:, C_TRI:C_TRI + P]
        nbias = const[:, C_NB:C_NB + 64]
        mask1 = const[:, C_M1:C_M1 + 256]
        ones = sb("ones", [P, P])
        XN = sb("XN", [P, NT, D])
        RA = sb("RA", [P, NT * D])
        RS_ = sb("RS_", [P, NT, D])
        small = sb("small", [P, 640])
        qscale, gamma0, gamma1, beta1 = (small[:, i:i + 1] for i in range(4))
        kscale = small[:, 4:5]
        gateb = small[:, 8:16]
        nkT = small[:, 16:48]
        bfc = small[:, 48:176]
        MV = small[:, 176:240].rearrange("p (n s) -> p n s", s=2)
        VE, RSTD, T1, T2 = (small[:, 240 + 32 * i:272 + 32 * i] for i in range(4))
        G1W, G2W = small[:, 368:400], small[:, 400:432]
        ST6 = small[:, 432:624].rearrange("p (n s) -> p n s", s=6)
        gw1, gw0 = small[:, 624:632], small[:, 632:640]
        slots = sb("slots", [P, 2, NT], I32)
        owner = sb("owner", [1, NBLK1 + 1], I32)

        ARENA = 39000
        arena = sb("arena", [P, ARENA])
        at = [0]

        def take(n, rows=P):
            at[0] += n
            assert at[0] <= ARENA, at[0]
            return arena[0:rows, at[0] - n:at[0]]

        raw = take(2 * 4 * 512).rearrange("p (t n) -> p t n", t=2)
        qkn = take(2 * 4 * 512).rearrange("p (t n) -> p t n", t=2)
        sq = take(2 * 512).rearrange("p (i n) -> p i n", i=2)
        qT = take(2 * HC * N).rearrange("p (i c n) -> p i c n", i=2, c=HC)
        kT = take(2 * HC * N).rearrange("p (i c n) -> p i c n", i=2, c=HC)
        Vt = take(2 * 2 * H * DH).rearrange("p (i t n) -> p i t n", i=2, t=2)
        alibi = take(H * N).rearrange("p (h n) -> p h n", h=H)
        wqkv = take(3 * H * DH)
        wo0 = take(HC * D).rearrange("p (c n) -> p c n", c=HC)
        nvb = take(H * DH, 2 * H)
        route0_at = at[0]
        Sb = take(2 * 512).rearrange("p (i n) -> p i n", i=2)
        Pb = take(2 * 512).rearrange("p (i n) -> p i n", i=2)
        PTb = take(2 * 512).rearrange("p (i n) -> p i n", i=2)
        On = take(H * DH)
        OnT = take(H * DH).rearrange("p (c n) -> p c n", c=HC)
        xa = take(2 * N).rearrange("p (i n) -> p i n", i=2)
        ss = take(64).rearrange("p (t n) -> p t n", t=2)
        rn = take(64).rearrange("p (t n) -> p t n", t=2)
        nw1, nw2, c15 = take(32), take(32), take(32)
        xh = take(64).rearrange("p (t n) -> p t n", t=2)
        nsn = take(64)
        nmn = take(32)
        nm = take(32)
        den = take(32)
        ntmp = take(64)
        pn = take(64)
        rden = take(32)
        pnT = take(P, 2 * H)
        nkp = take(P, 2 * H)
        attn_end = at[0]
        XN2 = raw_flat = arena[:, 0:NT * D].rearrange("p (t n) -> p t n", t=NT)
        XNT = arena[:, NT * D:2 * NT * D]
        zeros = arena[:, 2 * NT * D:2 * NT * D + 512]

        at[0] = 0
        GA = take(2 * NT * D).rearrange("p (k t n) -> p k t n", k=2, t=NT)
        XN1T = take(NT * D)
        AO = take(NT * D).rearrange("p (t n) -> p t n", t=NT)
        wb = take(NBUF * WCOLS).rearrange("p (i n) -> p i n", i=NBUF)
        b2b = take(NBUF * D).rearrange("p (i n) -> p i n", i=NBUF)
        xb = take(NBUF * 2 * D).rearrange("p (i t n) -> p i t n", i=NBUF, t=2)
        xbT = take(2 * BLK).rearrange("p (i n) -> p i n", i=2)
        hT = take(2 * FC * BLK).rearrange("p (i n) -> p i n", i=2)
        yb = take(2 * 2 * D).rearrange("p (i n) -> p i n", i=2)
        wq1, wk1, wv1, wfc = (take(D) for _ in range(4))
        xa1 = take(2 * N).rearrange("p (i n) -> p i n", i=2)
        qk1 = take(2 * 2 * N).rearrange("p (i n) -> p i n", i=2)
        v1 = take(3 * N).rearrange("p (i n) -> p i n", i=3)
        s1b = take(2 * 384).rearrange("p (i n) -> p i n", i=2)
        p1b = take(2 * 384).rearrange("p (i n) -> p i n", i=2)
        pt1 = take(384)
        nm1, den1, rd1 = (take(4) for _ in range(3))
        LG, EQ, M1, M2, R1, R2 = (take(256) for _ in range(6))
        TOT, INC = take(512), take(512)
        MX, KM, MX2, PZ = (take(32) for _ in range(4))
        CNT = take(64)
        CMP = take(320)
        route_end = at[0]
        LG0 = arena[:, route0_at:route0_at + 3400]

        S = {n: sem(n) for n in (
            "const_in", "x_in0", "x_in1", "gate_in", "gate1_in", "w_in", "zero_done", "xe_zero", "ones_ready", "c15_ready", "dve_step",
            "xn_ready", "xn2_ready", "tok_T", "tok_evac", "tok2_T", "tok2_evac", "logits_full", "mask_ready",
            "rank_full", "nk_ready", "nk_full", "nk_evac", "slots_ready", "scattered",
            "xa_in0", "xa_in1", "ring_full", "ring_evac", "sq_done", "ss_done", "seed_done", "newton", "qn_done",
            "sn_full", "s_full", "scores_seen", "ttr_done", "sn_step", "exp_done", "nsub_done", "pn_done", "den_step", "pt_full",
            "pt_evac", "pnT_full", "pnT_evac", "o_full", "on_done", "y_full", "y_evac",
            *[f"block_in{q}" for q in range(NBUF)], "xT_full", "xT_evac", "h_full", "gelu_done",
            "ye_full", "ye_evac", "stored0", "stored1", *[f"gathered{q}" for q in range(8)], "silu_done", "x_back", "x1_ready",
            "l1w_in", "qkv1_full", "qk1_evac", "v1_evac", "s1_full", "ttr1_done", "exp1_done", "pt1_full",
            "pt1_evac", "o1_full", "rd1_done", "o1_done", "xa1_in0", "xa1_in1", "ao_ready", "ao_T", "ao_evac",
            "fc_full", "attn1_done", "gate_exp", "out_ready", "out_done", "wexp")}

        class Chain:
            def __init__(self, eng, s):
                self.eng, self.s, self.n = eng, s, 0

            def __call__(self, ins):
                ins.then_inc(self.s, 1)
                self.n += 1
                self.eng.wait_ge(self.s, self.n)

        def ring_pos(with_next):
            return {u: i for i, u in enumerate(proj_order(with_next))}

        def ring_use(b, use, with_next=True):
            if isinstance(b, int) and b == -1:
                return use[1] if use[0] == "unit" else NU + use[1]
            return RING_START + b * RING_STEP + ring_pos(with_next)[use]

        def ring_bank(use, with_next=True, start=False):
            if start:
                return (use[1] if use[0] == "unit" else NU + use[1]) % 2
            return (RING_START + ring_pos(with_next)[use]) % 2

        def pairs(eng, first, last, body):
            n = (last - first + 1) // 2
            if n > 0:
                with eng.Fori(0, n) as i:
                    body(i * 2 + first, first % 2)
                    body(i * 2 + (first + 1), (first + 1) % 2)
            if (last - first + 1) % 2:
                body(last, last % 2)

        def rsqrt(eng, link, out, x, t1, t2, seed=True):
            if seed:
                link(eng.tensor_scalar(t1.bitcast(I32), x.bitcast(I32), 1, None, ALU.logical_shift_right))
                link(eng.tensor_scalar(out.bitcast(I32), t1.bitcast(I32), -1.0, RSQRT_MAGIC, ALU.mult, ALU.add))
            for _ in range(3):
                link(eng.tensor_tensor(t1, out, out, ALU.mult))
                link(eng.tensor_tensor(t2, t1, x, ALU.mult))
                link(eng.tensor_scalar(t1, t2, -0.5, 1.5, ALU.mult, ALU.add))
                link(eng.tensor_tensor(out, out, t1, ALU.mult))

        def layer_norm(v, link, src, dst, i0, n, done):
            for i in range(i0, i0 + n):
                ins = v.bn_stats(ST6[:, i], src[:, i])
            link(ins)
            for i in range(i0, i0 + n):
                ins = v.bn_aggr(MV[:, i], ST6[:, i])
            link(ins)
            s = slice(i0, i0 + n)
            link(v.tensor_scalar(VE[:, s], MV[:, s, 1], EPS, None, ALU.add))
            rsqrt(v, link, RSTD[:, s], VE[:, s], T1[:, s], T2[:, s])
            for i in range(i0, i0 + n):
                v.tensor_scalar(dst[:, i], src[:, i], MV[:, i, 0:1], RSTD[:, i:i + 1],
                                ALU.subtract, ALU.mult).then_inc(done, 1)

        def route(v, link, layer, mem, M1, M2):
            LG, EQ, R1, R2, TOT, INC, MX, KM, MX2, PZ, CNT, CMP = mem
            c = lambda lo, n: const[:, lo:lo + n]
            te = lambda x: x.rearrange("p (t e) -> p t e", e=E)
            et = lambda x: x.rearrange("p (e t) -> p e t", e=E)
            w8 = c(C_W8, E).unsqueeze(1).to_broadcast([P, NT, E])
            up = lambda x: x.unsqueeze(2).to_broadcast([P, NT, E])
            nch = 1 + layer

            def first_max(M, lg, mx):
                link(v.tensor_reduce(mx, te(lg), AX.X, ALU.max))
                link(v.tensor_tensor(te(EQ), te(lg), up(mx), ALU.is_equal))
                link(v.tensor_tensor(te(EQ), te(EQ), w8, ALU.mult))
                link(v.tensor_reduce(KM, te(EQ), AX.X, ALU.max))
                v.tensor_tensor(te(M), te(EQ), up(KM), ALU.is_equal).then_inc(S["mask_ready"], 1)

            base = 0 if layer == 0 else 1
            first_max(M1, LG, MX)
            if layer:
                v.wait_ge(S["mask_ready"], base + 1)
                link(v.scalar_tensor_tensor(out=R2, in0=M1, scalar=3.0 * NEG, in1=LG, op0=ALU.mult, op1=ALU.add))
                first_max(M2, R2, MX2)
                link(v.tensor_tensor(te(R1), te(LG), up(MX), ALU.subtract))
                v.tensor_copy(R2, R1).then_inc(S["gate_exp"], 1)
                v.wait_ge(S["wexp"], 1)
                link(v.tensor_reduce(PZ, te(R1), AX.X, ALU.add))
                link(v.reciprocal(KM, PZ))
                link(v.tensor_tensor(te(R1), te(R1), up(KM), ALU.mult))
                link(v.tensor_tensor(EQ, R1, M1, ALU.mult))
                link(v.tensor_reduce(G1W, te(EQ), AX.X, ALU.add))
                v.wait_ge(S["mask_ready"], base + 2)
                link(v.tensor_tensor(EQ, R1, M2, ALU.mult))
                link(v.tensor_reduce(G2W, te(EQ), AX.X, ALU.add))
                link(v.scalar_tensor_tensor(out=PZ, in0=G1W, scalar=1e-9, in1=G2W, op0=ALU.add, op1=ALU.add))
                link(v.reciprocal(KM, PZ))
                link(v.tensor_tensor(G1W, G1W, KM, ALU.mult))
                link(v.tensor_tensor(G2W, G2W, KM, ALU.mult))
            v.wait_ge(S["rank_full"], layer + 1)
            for k in range(nch):
                tot, inc = TOT[:, 256 * k:256 * k + 256], INC[:, 256 * k:256 * k + 256]
                link(v.tensor_copy(et(tot), te(SBANK[1][:, 256 * k:256 * k + 256]).rearrange("p t e -> p e t")))
                link(v.tensor_tensor_scan(inc, c(C_RS, 256), tot, 0.0, ALU.mult, ALU.add))
                link(v.tensor_copy(CNT[:, 8 * k:8 * k + 8], et(inc)[:, :, NT - 1]))
                link(v.tensor_tensor(inc, inc, tot, ALU.subtract))
            cnt = CNT[:, 0:8]
            if layer:
                inc = INC[:, 256:512]
                link(v.tensor_tensor(et(inc), et(inc), CNT[:, 0:8].unsqueeze(2).to_broadcast([P, E, NT]), ALU.add))
                cnt = CNT[:, 16:24]
                link(v.tensor_tensor(cnt, CNT[:, 0:8], CNT[:, 8:16], ALU.add))
                link(v.tensor_scalar(cnt, cnt, float(CAP), None, ALU.min))
            cm = CMP[:, 0:E * NTHR].rearrange("p (e k) -> p e k", e=E)
            link(v.tensor_tensor(cm, cnt.unsqueeze(2).to_broadcast([P, E, NTHR]),
                                 c(C_THR, NTHR).unsqueeze(1).to_broadcast([P, E, NTHR]), ALU.is_gt))
            nblk, bend, bst = CNT[:, 24:32], CNT[:, 32:40], CNT[:, 40:48]
            link(v.tensor_reduce(nblk, cm, AX.X, ALU.add))
            link(v.tensor_tensor_scan(bend, ones[:, 0:E], nblk, 0.0, ALU.mult, ALU.add))
            link(v.tensor_tensor(bst, bend, nblk, ALU.subtract))
            link(v.tensor_scalar(bst, bst, float(BLK), None, ALU.mult))
            nj = NBLK1 + 1
            cj = CMP[0:1, 0:nj * E].rearrange("p (j e) -> p j e", e=E)
            link(v.tensor_tensor(cj, const[0:1, C_JJ:C_JJ + nj].unsqueeze(2).to_broadcast([1, nj, E]),
                                 bend[0:1].unsqueeze(1).to_broadcast([1, nj, E]), ALU.is_ge))
            link(v.tensor_reduce(EQ[0:1, 0:nj], cj, AX.X, ALU.add))
            link(v.tensor_scalar(EQ[0:1, 0:nj], EQ[0:1, 0:nj], float(E - 1), None, ALU.min))
            link(v.tensor_copy(owner[:, :], EQ[0:1, 0:nj]))
            for k in range(nch):
                M = (M1, M2)[k]
                inc = INC[:, 256 * k:256 * k + 256]
                link(v.tensor_tensor(te(R1), te(SBANK[0][:, 256 * k:256 * k + 256]),
                                     et(inc).rearrange("p e t -> p t e"), ALU.add))
                link(v.tensor_tensor(EQ, R1, M, ALU.mult))
                link(v.tensor_reduce(PZ, te(EQ), AX.X, ALU.add))
                link(v.tensor_tensor(te(EQ), te(M), bst.unsqueeze(1).to_broadcast([P, NT, E]), ALU.mult))
                link(v.tensor_reduce(KM, te(EQ), AX.X, ALU.add))
                link(v.tensor_tensor(KM, KM, PZ, ALU.add))
                if layer:
                    link(v.tensor_scalar(MX, PZ, float(CAP), None, ALU.is_lt))
                    W = (G1W, G2W)[k]
                    link(v.tensor_tensor(W, W, MX, ALU.mult))
                    link(v.tensor_scalar(MX, MX, -BIG, BIG, ALU.mult, ALU.add))
                    link(v.tensor_tensor(KM, KM, MX, ALU.add))
                v.tensor_copy(slots[:, k, :], KM).then_inc(S["slots_ready"], 1)

        def scatter_rows(pool, layer):
            pool.wait_ge(S["slots_ready"], (1, 3)[layer])
            for k in range(1 + layer):
                for i in range(NT):
                    pool.indirect_dma_start(
                        xe[:, :], bass.IndirectOffsetOnAxis(ap=slots[:, k, i:i + 1], axis=0), XN[:, i, :], None,
                        bounds_check=NBLK1 * BLK - 1, oob_is_err=False).then_inc(S["scattered"], 16)

        def gather_rows(pool, layer):
            rows = (NBLK0, NBLK1)[layer] * BLK
            for i in range(NT):
                for k in range(1 + layer):
                    pool.indirect_dma_start(
                        GA[:, k, i, :], None, ye[0:rows, :], bass.IndirectOffsetOnAxis(ap=slots[:, k, i:i + 1], axis=0),
                        bounds_check=rows - 1, oob_is_err=False).then_inc(S[f"gathered{i // 4}"], 16)

        def quads(eng, first, last, body):
            n = (last - first + 1) // NBUF
            if n > 0:
                with eng.Fori(0, n) as i:
                    for q in range(NBUF):
                        body(i * NBUF + (first + q), q, i + first // NBUF)
            for j in range(first + n * NBUF, last + 1):
                body(j, j % NBUF, j // NBUF)

        def ffn_sync(sp, layer, nblk, base):
            W, B2 = a[f"wp_{layer}"], a[f"b2_{layer}"]

            def load_block(j, q):
                e = sp.value_load(owner[0:1, bass.ds(j, 1)], min_val=0, max_val=E - 1)
                src = xe[bass.ds(j * BLK, BLK), :].rearrange("(t p) d -> p t d", p=P)
                sp.dma_start(xb[:, q], src).then_inc(S[f"block_in{q}"], 16)
                sp.dma_start(wb[:, q], W[bass.ds(e, 1)].rearrange("e p n -> p (e n)")).then_inc(S[f"block_in{q}"], 16)
                sp.dma_start(b2b[:, q], B2[bass.ds(e, 1)].to_broadcast([P, D])).then_inc(S[f"block_in{q}"], 16)

            def step(j, q, more=True):
                p = q % 2
                sp.wait_ge(S["ye_evac"], j + (base + 1))
                dst = ye[bass.ds(j * BLK, BLK), :].rearrange("(t p) d -> p t d", p=P)
                sp.dma_start(dst, yb[:, p].rearrange("p (t d) -> p t d", t=2)).then_inc(S[f"stored{p}"], 16)
                if more:
                    load_block(j + NBUF, q)

            for j in range(NBUF):
                load_block(j, j)
            m = (nblk - NBUF) // NBUF * NBUF
            quads(sp, 0, m - 1, lambda j, q, i: step(j, q))
            for j in range(m, nblk):
                step(j, j % NBUF, more=j + NBUF < nblk)

        def ffn_tensor(pe, nblk, base, counts):
            XT, HB, YB = bank[0:2], bank[2:6], bank[6:8]

            def turn(j, q, i):
                pe.wait_ge(S[f"block_in{q}"], (i + (counts[q] + 1)) * LOADS)
                for t in range(2):
                    mm = pe.transpose(XT[q % 2][:, t * P:(t + 1) * P], xb[:, q, t, :], ident)
                mm.then_inc(S["xT_full"], 1)

            def up(j, q):
                pe.wait_ge(S["xT_evac"], j + (base + 1))
                for c in range(FC):
                    mm = pe.matmul(HB[2 * (q % 2) + c // 2][:, (c % 2) * BLK:(c % 2 + 1) * BLK],
                                   wb[:, q, c * P:(c + 1) * P], xbT[:, q % 2, :], start=True, stop=True)
                mm.then_inc(S["h_full"], 1)

            def down(j, q):
                p = q % 2
                pe.wait_ge(S["gelu_done"], j + (base + 1))
                if base or not isinstance(j, int) or j >= 2:
                    pe.wait_ge(S["ye_evac"], j + (base - 1))
                for t in range(2):
                    for c in range(FC):
                        mm = pe.matmul(YB[p][:, t * D:(t + 1) * D], hT[:, p, c * BLK + t * P:c * BLK + (t + 1) * P],
                                       wb[:, q, DFF + c * D:DFF + (c + 1) * D], start=(c == 0), stop=(c == FC - 1))
                mm.then_inc(S["ye_full"], 1)

            def step(j, q, i, more=2):
                if more >= 2:
                    turn(j + 2, (q + 2) % NBUF, i + (q + 2) // NBUF)
                if more >= 1:
                    up(j + 1, (q + 1) % NBUF)
                down(j, q)

            turn(0, 0, 0)
            turn(1, 1, 0)
            up(0, 0)
            for j in range(NBUF):
                step(j, j, 0)
            m = (nblk - 2) // NBUF * NBUF
            quads(pe, NBUF, m - 1, step)
            for j in range(m, nblk):
                step(j, j % NBUF, j // NBUF, more=min(2, nblk - 1 - j))

        def ffn_scalar(act, nblk, base, counts):
            HB = bank[2:6]

            def gelu(j, q, i):
                p = q % 2
                act.wait_ge(S["h_full"], j + (base + 1))
                act.wait_ge(S[f"block_in{q}"], (i + (counts[q] + 1)) * LOADS)
                for c in range(FC):
                    ins = act.activation(hT[:, p, c * BLK:(c + 1) * BLK], HB[2 * p + c // 2][:, (c % 2) * BLK:(c % 2 + 1) * BLK],
                                         ACT.Gelu, bias=wb[:, q, 2 * DFF + c:2 * DFF + c + 1])
                ins.then_inc(S["gelu_done"], 1)

            quads(act, 0, nblk - 1, gelu)

        def ffn_vector(v, nblk, base, counts):
            XT, YB = bank[0:2], bank[6:8]
            before = (base + 1) // 2, base // 2

            def evac_x(j, p):
                v.wait_ge(S["xT_full"], j + (base + 1))
                v.tensor_copy(xbT[:, p, :], XT[p][:, 0:BLK]).then_inc(S["xT_evac"], 1)

            def add_b2(j, q, i):
                p = q % 2
                v.wait_ge(S["ye_full"], j + (base + 1))
                v.wait_ge(S[f"block_in{q}"], (i + (counts[q] + 1)) * LOADS)
                if not isinstance(j, int) or j >= 2 or base:
                    v.wait_ge(S[f"stored{p}"], (i * 2 + (q // 2 + before[p])) * 16)
                v.tensor_tensor(yb[:, p, :].rearrange("p (t d) -> p t d", t=2),
                                YB[p][:, 0:2 * D].rearrange("p (t d) -> p t d", t=2),
                                b2b[:, q].unsqueeze(1).to_broadcast([P, 2, D]), ALU.add).then_inc(S["ye_evac"], 1)

            def step(j, q, i, more=True):
                if more:
                    evac_x(j + 2, q % 2)
                add_b2(j, q, i)

            evac_x(0, 0)
            evac_x(1, 1)
            for j in range(NBUF):
                step(j, j, 0)
            m = (nblk - 2) // NBUF * NBUF
            quads(v, NBUF, m - 1, step)
            for j in range(m, nblk):
                step(j, j % NBUF, j // NBUF, more=j + 2 < nblk)

        loads0 = (0,) * NBUF
        loads1 = tuple((NBLK0 + NBUF - 1 - q) // NBUF for q in range(NBUF))

        def stores(layer):
            return (NBLK0 + 1) // 2 + layer * ((NBLK1 + 1) // 2), NBLK0 // 2 + layer * (NBLK1 // 2)

        M1_0 = LG0[:, 256 * 2:256 * 3]
        mem0 = [LG0[:, 0:256], LG0[:, 256:512], LG0[:, 768:1024], LG0[:, 1024:1280], LG0[:, 1280:1792],
                LG0[:, 1792:2304], LG0[:, 2304:2336], LG0[:, 2336:2368], LG0[:, 2368:2400], LG0[:, 2400:2432],
                LG0[:, 2432:2496], LG0[:, 2496:2816]]
        mem1 = [LG, EQ, R1, R2, TOT, INC, MX, KM, MX2, PZ, CNT, CMP]
        RB = lambda b: bass.ds(b * N, N)

        block = ctx.enter_context(nc.Block())

        @block.sync
        def _(sp):
            sp.dma_start(const[:, :], a["const"]).then_inc(S["const_in"], 16)
            for h in range(2):
                s = slice(h * NT // 2, (h + 1) * NT // 2)
                sp.dma_start(RS_[:, s], x_v[:, s]).then_inc(S[f"x_in{h}"], 16)
            sp.dma_start(gateb, a["L0_ffn_gate_b"].unsqueeze(0).to_broadcast([P, E])).then_inc(S["gate_in"], 16)
            sp.dma_start(gamma0, a["L0_attn_gamma"].unsqueeze(1)).then_inc(S["gate_in"], 16)
            sp.dma_start(gw0, a["L0_ffn_gate_W"]).then_inc(S["gate_in"], 16)
            for h in range(2):
                sp.dma_start(qscale[64 * h:64 * h + 64], a["L0_attn_q_scale"].unsqueeze(1)).then_inc(S["w_in"], 16)
                sp.dma_start(kscale[64 * h:64 * h + 64], a["L0_attn_k_scale"].unsqueeze(1)).then_inc(S["w_in"], 16)
            sp.dma_start(nkp, a["nkp"]).then_inc(S["w_in"], 16)
            sp.dma_start(wqkv[:, 0:H * DH], a["L0_attn_w_q"]).then_inc(S["w_in"], 16)
            sp.dma_start(wqkv[:, H * DH:3 * H * DH], a["L0_attn_w_kv"]).then_inc(S["w_in"], 16)
            sp.dma_start(alibi, a["alibi"]).then_inc(S["w_in"], 16)
            sp.dma_start(nvb, a["nvb"]).then_inc(S["w_in"], 16)
            sp.dma_start(wo0, a["L0_attn_w_out"].rearrange("(c p) n -> p c n", p=P)).then_inc(S["w_in"], 16)
            sp.wait_ge(S["zero_done"], 1)
            sp.dma_start(xe.rearrange("(p r) d -> p (r d)", p=P).rearrange("p (r c) -> p r c", c=512 if (NBLK1 * 2 * D) % 512 == 0 else 256),
                         zeros[:, 0:(512 if (NBLK1 * 2 * D) % 512 == 0 else 256)].unsqueeze(1).to_broadcast(
                             [P, NBLK1 * 2 * D // (512 if (NBLK1 * 2 * D) % 512 == 0 else 256), (512 if (NBLK1 * 2 * D) % 512 == 0 else 256)])).then_inc(S["xe_zero"], 16)

            def load_xa(b, p):
                sp.dma_start(xa[:, p], RA[:, RB(b)]).then_inc(S[f"xa_in{p}"], 16)

            sp.wait_ge(S["tok2_evac"], NT // 4)
            load_xa(0, 0)
            load_xa(1, 1)

            def attn_step(b, p):
                sp.wait_ge(S["ring_evac"], ring_use(b, ("unit", NU - 1)) + 1)
                load_xa(b + 3, 1 - p)

            sp.wait_ge(S["ring_evac"], NU)
            load_xa(2, 0)
            m = (NB - 3) // 2
            pairs(sp, 0, 2 * m - 1, attn_step)
            for b in range(2 * m, NB - 3):
                attn_step(b, b % 2)

            sp.wait_ge(S["y_evac"], 2 * NB)
            sp.wait_ge(S["scattered"], 16 * NT)
            sp.dma_start(RA[:, :].rearrange("p (t d) -> p t d", d=D), x_v).then_inc(S["x_back"], 16)
            for w, name in ((wq1, "L1_attn_Wq"), (wk1, "L1_attn_Wk"), (wv1, "L1_attn_Wv"), (wfc, "L1_attn_Wfc")):
                sp.dma_start(w, a[name]).then_inc(S["l1w_in"], 16)
            sp.dma_start(gamma1, a["L1_attn_gamma"].unsqueeze(1)).then_inc(S["l1w_in"], 16)
            sp.dma_start(beta1, a["L1_attn_beta"].unsqueeze(1)).then_inc(S["l1w_in"], 16)
            sp.dma_start(bfc, a["L1_attn_bfc"].unsqueeze(0).to_broadcast([P, D])).then_inc(S["l1w_in"], 16)
            sp.dma_start(gw1, a["L1_ffn_Wg"]).then_inc(S["gate1_in"], 16)
            ffn_sync(sp, 0, NBLK0, 0)

            sp.wait_ge(S["tok_evac"], 2 * (NT // 4))

            def load_xa1(b, p):
                sp.dma_start(xa1[:, p], XN1T[:, RB(b)]).then_inc(S[f"xa1_in{p}"], 16)

            load_xa1(0, 0)
            load_xa1(1, 1)

            def attn1_step(b, p):
                sp.wait_ge(S["qkv1_full"], b + 1)
                load_xa1(b + 2, p)

            pairs(sp, 0, NB - 3, attn1_step)

            sp.wait_ge(S["scattered"], 16 * 3 * NT)
            ffn_sync(sp, 1, NBLK1, NBLK0)
            for q in range(8):
                s = slice(4 * q, 4 * q + 4)
                sp.wait_ge(S["out_ready"], q + 1)
                sp.dma_start(out_v[:, s], RA[:, 512 * q:512 * q + 512].rearrange("p (t d) -> p t d", d=D))\
                  .then_inc(S["out_done"], 16)
            sp.wait_ge(S["out_done"], 16 * 8)

        @block.gpsimd
        def _(pool):
            pool.memset(zeros, 0.0).then_inc(S["zero_done"], 1)
            pool.memset(ones[:, :], 1.0).then_inc(S["ones_ready"], 1)
            pool.memset(c15, 1.5).then_inc(S["c15_ready"], 1)
            pool.wait_ge(S["c15_ready"], 1)

            def square(a_, i, p_use, first):
                t, k = UNITS[i]
                pool.wait_ge(S["ring_evac"], p_use + 1)
                if i >= 2:
                    pool.wait_ge(S["ss_done"], a_ * NQ + (i - 1))
                r = raw[:, t, 512 * k:512 * k + 512]
                pool.tensor_tensor(sq[:, i % 2], r, r, ALU.mult).then_inc(S["sq_done"], 1)

            def unit_len(a_, t):
                pool.wait_ge(S["seed_done"], a_ * 2 + (t + 1))
                y, n = rn[:, t], 0
                for _ in range(3):
                    for out, i0, i1, op in ((nw1, y, y, ALU.mult), (nw2, nw1, xh[:, t], ALU.mult),
                                            (nw1, nw2, c15, ALU.add), (y, y, nw1, ALU.mult)):
                        pool.tensor_tensor(out, i0, i1, op).then_inc(S["newton"], 1)
                        n += 1
                        pool.wait_ge(S["newton"], a_ * 24 + (12 * t + n))

            def normalise(a_, t):
                for k in range(4):
                    pool.tensor_tensor(qkn[:, t, 512 * k:512 * k + 512].rearrange("p (h d) -> p h d", d=DH),
                                       raw[:, t, 512 * k:512 * k + 512].rearrange("p (h d) -> p h d", d=DH),
                                       rn[:, t, 8 * k:8 * k + 8].unsqueeze(2).to_broadcast([P, 8, DH]),
                                       ALU.mult).then_inc(S["qn_done"], 1)

            def lengths(a_, use):
                for i in range(6):
                    square(a_, i, use(i), False)
                unit_len(a_, 0)
                normalise(a_, 0)
                for i in range(6, 8):
                    square(a_, i, use(i), False)
                unit_len(a_, 1)
                normalise(a_, 1)

            lengths(0, lambda i: ring_use(-1, ("unit", i)))
            pool.wait_ge(S["xe_zero"], 16)
            scatter_rows(pool, 0)

            def step(b, p):
                lengths(b + 1, lambda i: ring_use(b, ("unit", i)))

            pairs(pool, 0, NB - 2, step)

            for p in range(2):
                pool.wait_ge(S[f"stored{p}"], 16 * stores(0)[p])
            gather_rows(pool, 0)
            scatter_rows(pool, 1)
            pool.wait_ge(S["silu_done"], 8)
            pool.wait_ge(S["x1_ready"], 8)
            pool.memset(GA[:, :, :, :].rearrange("p k t n -> p (k t n)"), 0.0).then_inc(S["zero_done"], 1)
            pool.wait_ge(S["zero_done"], 2)
            for p in range(2):
                pool.wait_ge(S[f"stored{p}"], 16 * stores(1)[p])
            gather_rows(pool, 1)

        @block.tensor
        def _(pe):
            def gate_logits(layer, first, gw, XT):
                def logits(g):
                    pe.wait_ge(S["tok_evac"], first + g + 1)
                    for i in range(4 * g, 4 * g + 4):
                        mm = pe.matmul(MISC[:, E * i:E * i + E], XT[:, P * i:P * i + P], gw, start=True, stop=True)
                    return mm
                for g in range(NT // 4):
                    pe.wait_ge(S["xn_ready"], layer * NT + 4 * g + 4)
                    if g >= 2:
                        pe.wait_ge(S["tok_evac"], first + g - 1)
                    for i in range(4):
                        mm = pe.transpose(RING[g % 2][:, P * i:P * i + P], XN[:, 4 * g + i, :], ident)
                    mm.then_inc(S["tok_T"], 1)
                    if layer == 0:
                        pe.wait_ge(S["xn2_ready"], 4 * g + 4)
                        if g >= 2:
                            pe.wait_ge(S["tok2_evac"], g - 1)
                        for i in range(4):
                            mm = pe.transpose(OBANK[g % 2][:, P * i:P * i + P], XN2[:, 4 * g + i, :], ident)
                        mm.then_inc(S["tok2_T"], 1)
                    if g:
                        logits(g - 1)
                logits(NT // 4 - 1).then_inc(S["logits_full"], 1)

            def ranks(layer, M1, M2):
                pe.wait_ge(S["mask_ready"], (1, 3)[layer])
                for k, M in enumerate((M1, M2)[:1 + layer]):
                    pe.matmul(SBANK[0][:, 256 * k:256 * k + 256], tri, M, start=True, stop=True)
                    mm = pe.matmul(SBANK[1][:, 256 * k:256 * k + 256], ones[:, :], M, start=True, stop=True)
                mm.then_inc(S["rank_full"], 1)

            pe.wait_ge(S["const_in"], 16)
            pe.wait_ge(S["ones_ready"], 1)
            pe.wait_ge(S["gate_in"], 48)
            gate_logits(0, 0, gw0, XNT)
            pe.wait_ge(S["nk_ready"], 1)
            pe.transpose(TRB[:, 0:2 * H], nkp, ident[0:2 * H, 0:2 * H]).then_inc(S["nk_full"], 1)
            ranks(0, M1_0, None)
            pe.wait_ge(S["tok2_evac"], NT // 4)

            def unit(a_, p, u, use, b_):
                t, k = UNITS[u]
                if not (isinstance(b_, int) and b_ == -1 and u < 2):
                    pe.wait_ge(S["ring_evac"], ring_use(b_, ("unit", u)) - 1)
                pe.matmul(RING[use][:, :], xa[:, p, t * P:(t + 1) * P], wqkv[:, 512 * k:512 * k + 512],
                          start=True, stop=True).then_inc(S["ring_full"], 1)

            def turn_qk(a_, s, use, b_):
                t, k = s // 4, s % 4
                pe.wait_ge(S["ring_evac"], ring_use(b_, ("qk", s)) - 1)
                pe.wait_ge(S["qn_done"], a_ * NQ + (s + 1))
                for c in range(4):
                    mm = pe.transpose(RING[use][:, P * c:P * c + P], qkn[:, t, 512 * k + P * c:512 * k + P * c + P],
                                      ident)
                mm.then_inc(S["ring_full"], 1)

            def scores(b, p, g):
                t, heads = GROUPS[g]
                n = P * (t + 1)
                for k, h in enumerate(heads):
                    r = 64 * (h % 2)
                    mm = pe.matmul(SBANK[g % 2][:, n * k:n * k + n], qT[r:r + 64, p, h // 2, t * P:(t + 1) * P],
                                   kT[r:r + 64, p, h // 2, 0:n], start=True, stop=True)
                mm.then_inc(S["s_full"], 1)

            def head_start(b, p, b_, with_next_prev=True):
                pe.wait_ge(S["ring_evac"], ring_use(b_, ("qk", NQ - 1)) + 1)
                for t in range(2):
                    for c in range(HC):
                        mm = pe.matmul(MISC[:, 32 * t + 4 * c:32 * t + 4 * c + 4], qT[:, p, c, t * P:(t + 1) * P],
                                       nkT[:, 4 * c:4 * c + 4], start=True, stop=True)
                mm.then_inc(S["sn_full"], 1)
                scores(b, p, 0)
                scores(b, p, 1)

            def turn_p(b, g):
                pe.wait_ge(S["exp_done"], b * NG + (g + 1))
                for k in range(4):
                    mm = pe.transpose(TRB[:, P * k:P * k + P], Pb[:, g % 2, P * k:P * k + P], ident)
                mm.then_inc(S["pt_full"], 1)

            def weigh(b, p, g):
                t, heads = GROUPS[g]
                pe.wait_ge(S["pt_evac"], b * NG + (g + 1))
                for k, h in enumerate(heads):
                    for j in range(t + 1):
                        o = OBANK[h // 8][:, DH * (h % 8):DH * (h % 8) + DH]
                        pe.matmul(o, PTb[:, g % 2, P * ((t + 1) * k + j):P * ((t + 1) * k + j) + P],
                                  Vt[:, p, j, DH * h:DH * h + DH], start=(h % 8 == 0 and j == 0), stop=False,
                                  skip_group_check=True)

            def turn_null(b, t):
                pe.wait_ge(S["pn_done"], b * 2 + (t + 1))
                pe.transpose(MISC[0:2 * H, 0:P], pn[:, 32 * t:32 * t + 32], ident).then_inc(S["pnT_full"], 1)

            def weigh_null(b, t):
                pe.wait_ge(S["pnT_evac"], b * 2 + (t + 1))
                for o in range(2):
                    mm = pe.matmul(OBANK[o][:, :], pnT, nvb[:, 512 * o:512 * o + 512], start=False, stop=True,
                                   skip_group_check=True)
                mm.then_inc(S["o_full"], 1)

            def turn_o(b, t, wn):
                pe.wait_ge(S["on_done"], b * 2 + (t + 1))
                for o in range(2):
                    pe.wait_ge(S["ring_evac"], ring_use(b, ("out", t, o), wn) - 1)
                    for c in range(4):
                        mm = pe.transpose(RING[ring_bank(("out", t, o), wn)][:, P * c:P * c + P],
                                          On[:, 512 * o + P * c:512 * o + P * c + P], ident)
                    mm.then_inc(S["ring_full"], 1)

            def project(b, t, wn):
                pe.wait_ge(S["ring_evac"], ring_use(b, ("out", t, 1), wn) + 1)
                for c in range(HC):
                    mm = pe.matmul(MISC[:, 0:D], OnT[:, c], wo0[:, c], start=(c == 0), stop=(c == HC - 1))
                mm.then_inc(S["y_full"], 1)

            def step(b, p, wn=True):
                for g in range(NG):
                    if g + 2 < NG:
                        pe.wait_ge(S["ttr_done"], b * NG + (g + 1))
                        scores(b, p, g + 2)
                    if wn and g < NU // 2:
                        for u in (2 * g, 2 * g + 1):
                            if u == 0:
                                pe.wait_ge(S[f"xa_in{1 - p}"], xa_count(p))
                            unit(b + 1, 1 - p, u, ring_bank(("unit", u)), b)
                    if g == 4:
                        turn_null(b, 0)
                    if g == 5:
                        pe.wait_ge(S["on_done"], b * 2 + 1)
                    if g:
                        weigh(b, p, g - 1)
                    if g == 4:
                        weigh_null(b, 0)
                    if g == 6:
                        turn_o(b, 0, wn)
                    if g == 7:
                        pe.wait_ge(S["sn_full"], b + 1)
                        project(b, 0, wn)
                    if wn and g in QK_SLOTS:
                        for s in QK_SLOTS[g]:
                            turn_qk(b + 1, s, ring_bank(("qk", s)), b)
                    turn_p(b, g)
                turn_null(b, 1)
                weigh(b, p, NG - 1)
                weigh_null(b, 1)
                if wn:
                    head_start(b + 1, 1 - p, b)
                    pe.wait_ge(S["sn_step"], (b + 1) * 2 + 1)
                turn_o(b, 1, wn)
                project(b, 1, wn)

            xa_loop = {}

            def xa_count(p):
                return xa_loop["i"] * 16 + (16 if p == 0 else 32)

            pe.wait_ge(S["w_in"], 16 * 10)
            pe.wait_ge(S["xa_in0"], 16)
            for u in range(NU):
                unit(0, 0, u, ring_bank(("unit", u), start=True), -1)
            for s in range(NQ):
                turn_qk(0, s, ring_bank(("qk", s), start=True), -1)
            pe.wait_ge(S["nk_evac"], 1)
            head_start(0, 0, -1)
            with pe.Fori(0, (NB - 2) // 2) as i:
                xa_loop["i"] = i
                step(i * 2, 0)
                step(i * 2 + 1, 1)
            for b in range(NB - 2, NB):
                xa_loop["i"] = b // 2
                step(b, b % 2, wn=b + 1 < NB)

            pe.wait_ge(S["y_evac"], 2 * NB)
            ffn_tensor(pe, NBLK0, 0, loads0)

            pe.wait_ge(S["gate1_in"], 16)
            pe.wait_ge(S["ye_evac"], NBLK0)
            gate_logits(1, NT // 4, gw1, XN1T)
            ranks(1, M1, M2)
            pe.wait_ge(S["l1w_in"], 16 * 7)

            QK, VB, SC, PT, OB = bank[0], bank[1], bank[4], bank[5], bank[6]

            def qkv1(b, p, n):
                pe.wait_ge(S[f"xa1_in{p}"], n)
                pe.matmul(QK[:, 0:N], wq1, xa1[:, p], start=True, stop=True)
                pe.matmul(QK[:, N:2 * N], wk1, xa1[:, p], start=True, stop=True)
                for t in range(2):
                    mm = pe.matmul(VB[:, t * D:(t + 1) * D], xa1[:, p, t * P:(t + 1) * P], wv1, start=True, stop=True)
                mm.then_inc(S["qkv1_full"], 1)

            def scores1(b, p):
                pe.wait_ge(S["qk1_evac"], b + 1)
                pe.matmul(SC[:, 0:P], qk1[:, p, 0:P], qk1[:, p, N:N + P], start=True, stop=True)
                pe.matmul(SC[:, P:P + N], qk1[:, p, P:N], qk1[:, p, N:2 * N], start=True, stop=True)\
                  .then_inc(S["s1_full"], 1)

            def weigh1(b, p):
                pe.wait_ge(S["exp1_done"], b + 1)
                for k in range(3):
                    mm = pe.transpose(PT[:, P * k:P * k + P], p1b[:, p, P * k:P * k + P], ident)
                mm.then_inc(S["pt1_full"], 1)
                pe.wait_ge(S["pt1_evac"], b + 1)
                for t, k, j in ((0, 0, 0), (1, 1, 0), (1, 2, 1)):
                    mm = pe.matmul(OB[:, t * D:(t + 1) * D], pt1[:, P * k:P * k + P],
                                   v1[:, p, j * D:(j + 1) * D], start=(j == 0), stop=(j == t))
                mm.then_inc(S["o1_full"], 1)

            def step1(b, p, i, more=2):
                if more >= 2:
                    pe.wait_ge(S["v1_evac"], b + 2)
                    pe.wait_ge(S["qk1_evac"], b + 2)
                    qkv1(b + 2, p, (i + 2) * 16)
                if more >= 1:
                    pe.wait_ge(S["ttr1_done"], b + 1)
                    scores1(b + 1, 1 - p)
                pe.wait_ge(S["v1_evac"], b + 1)
                weigh1(b, p)

            qkv1(0, 0, 16)
            pe.wait_ge(S["v1_evac"], 1)
            pe.wait_ge(S["qk1_evac"], 1)
            qkv1(1, 1, 16)
            scores1(0, 0)
            with pe.Fori(0, (NB - 2) // 2) as i:
                step1(i * 2, 0, i)
                step1(i * 2 + 1, 1, i)
            for b in range(NB - 2, NB):
                step1(b, b % 2, b // 2, more=NB - 1 - b)

            def fc(g):
                pe.wait_ge(S["ao_evac"], g + 1)
                if g >= 2:
                    pe.wait_ge(S["attn1_done"], g - 1)
                for i in range(4):
                    mm = pe.matmul(bank[6 + g % 2][:, P * i:P * i + P], XN1T[:, 512 * g + P * i:512 * g + P * i + P], wfc,
                                   start=True, stop=True)
                mm.then_inc(S["fc_full"], 1)
            pe.wait_ge(S["o1_done"], NB)
            for g in range(NT // 4):
                pe.wait_ge(S["ao_ready"], 4 * g + 4)
                if g >= 2:
                    pe.wait_ge(S["ao_evac"], g - 1)
                for i in range(4):
                    mm = pe.transpose(bank[4 + g % 2][:, P * i:P * i + P], AO[:, 4 * g + i, :], ident)
                mm.then_inc(S["ao_T"], 1)
                if g:
                    fc(g - 1)
            fc(NT // 4 - 1)
            pe.wait_ge(S["attn1_done"], NT // 4)
            ffn_tensor(pe, NBLK1, NBLK0, loads1)

        @block.scalar
        def _(act):
            for g in range(NT // 4):
                act.wait_ge(S["tok_T"], g + 1)
                act.activation(XNT[:, 512 * g:512 * g + 512], RING[g % 2][:, :], ACT.Copy).then_inc(S["tok_evac"], 1)

            def ring_out(kind, n, use, bnk, a_=None, p=None):
                act.wait_ge(S["ring_full"], use + 1)
                src = RING[bnk]
                if kind == "unit":
                    t, k = UNITS[n]
                    dst = raw[:, t, 512 * k:512 * k + 512] if k < 4 else Vt[:, p, t, 512 * (k - 4):512 * (k - 3)]
                    ins = act.activation(dst, src[:, :], ACT.Copy)
                elif kind == "qk":
                    t, k = n // 4, n % 4
                    s4 = src[:, :].rearrange("p (c n) -> p c n", c=4)
                    if k < 2:
                        ins = act.activation(qT[:, p, 4 * k:4 * k + 4, t * P:(t + 1) * P], s4, ACT.Copy, scale=qscale)
                    else:
                        ins = act.activation(kT[:, p, 4 * (k - 2):4 * (k - 2) + 4, t * P:(t + 1) * P], s4, ACT.Copy)
                else:
                    ins = act.activation(OnT[:, 4 * n:4 * n + 4], src[:, :].rearrange("p (c n) -> p c n", c=4), ACT.Copy)
                ins.then_inc(S["ring_evac"], 1)

            def probs(b, g):
                t, heads = GROUPS[g]
                n = P * (t + 1)
                act.wait_ge(S["ttr_done"], b * NG + (g + 1))
                for k, h in enumerate(heads):
                    ins = act.activation(Pb[:, g % 2, n * k:n * k + n], Sb[:, g % 2, n * k:n * k + n], ACT.Exp,
                                         bias=nm_t(t, h), scale=-1.0,
                                         accum_out=den_t(t, h))
                ins.then_inc(S["exp_done"], 1)

            def nm_t(t, h):
                return nm[:, 16 * t + h:16 * t + h + 1]

            def den_t(t, h):
                return den[:, 16 * t + h:16 * t + h + 1]

            def null_probs(b, t):
                act.wait_ge(S["nsub_done"], b * 2 + (t + 1))
                act.activation(pn[:, 32 * t:32 * t + 32], ntmp[:, 32 * t:32 * t + 32], ACT.Exp).then_inc(S["pn_done"], 1)

            def step(b, p, wn=True):
                for g in range(NG):
                    probs(b, g)
                    if wn and g < NU // 2:
                        for u in (2 * g, 2 * g + 1):
                            ring_out("unit", u, ring_use(b, ("unit", u)), ring_bank(("unit", u)), p=1 - p)
                    if g == 3:
                        null_probs(b, 0)
                    if g == 6:
                        for o in range(2):
                            ring_out("out", o, ring_use(b, ("out", 0, o), wn), ring_bank(("out", 0, o), wn))
                    if wn and g in QK_SLOTS:
                        for s in QK_SLOTS[g]:
                            ring_out("qk", s, ring_use(b, ("qk", s)), ring_bank(("qk", s)), p=1 - p)
                null_probs(b, 1)
                for o in range(2):
                    ring_out("out", o, ring_use(b, ("out", 1, o), wn), ring_bank(("out", 1, o), wn))

            for u in range(NU):
                ring_out("unit", u, ring_use(-1, ("unit", u)), ring_bank(("unit", u), start=True), p=0)
            act.wait_ge(S["nk_ready"], 1)
            for s in range(NQ):
                ring_out("qk", s, ring_use(-1, ("qk", s)), ring_bank(("qk", s), start=True), p=0)
            pairs(act, 0, NB - 3, step)
            step(NB - 2, 0)
            step(NB - 1, 1, wn=False)

            ffn_scalar(act, NBLK0, 0, loads0)

            def silu(q):
                act.wait_ge(S[f"gathered{q}"], 16 * 4)
                g = GA[:, 0, 4 * q:4 * q + 4, :]
                act.activation(g, g, ACT.Silu).then_inc(S["silu_done"], 1)
            for q in range(8):
                silu(q)

            for g in range(NT // 4):
                act.wait_ge(S["tok_T"], NT // 4 + g + 1)
                act.activation(XN1T[:, 512 * g:512 * g + 512], RING[g % 2][:, :], ACT.Copy).then_inc(S["tok_evac"], 1)
            act.wait_ge(S["gate_exp"], 1)
            act.activation(R1, R2, ACT.Exp).then_inc(S["wexp"], 1)

            def evac_qk1(b, p):
                act.wait_ge(S["qkv1_full"], b + 1)
                act.activation(qk1[:, p], bank[0][:, :], ACT.Copy).then_inc(S["qk1_evac"], 1)

            def exp1(b, p):
                act.wait_ge(S["ttr1_done"], b + 1)
                act.activation(p1b[:, p, 0:P], s1b[:, p, 0:P], ACT.Exp, bias=nm1[:, 2 * p:2 * p + 1], scale=-1.0,
                               accum_out=den1[:, 2 * p:2 * p + 1])
                act.activation(p1b[:, p, P:P + N], s1b[:, p, P:P + N], ACT.Exp, bias=nm1[:, 2 * p + 1:2 * p + 2], scale=-1.0,
                               accum_out=den1[:, 2 * p + 1:2 * p + 2]).then_inc(S["exp1_done"], 1)

            def step1(b, p, more=True):
                if more:
                    act.wait_ge(S["s1_full"], b + 1)
                    evac_qk1(b + 2, p)
                exp1(b, p)
            evac_qk1(0, 0)
            evac_qk1(1, 1)
            pairs(act, 0, NB - 3, step1)
            for b in range(NB - 2, NB):
                step1(b, b % 2, more=False)

            for g in range(NT // 4):
                act.wait_ge(S["ao_T"], g + 1)
                act.activation(XN1T[:, 512 * g:512 * g + 512], bank[4 + g % 2][:, :], ACT.Identity, bias=beta1,
                               scale=gamma1).then_inc(S["ao_evac"], 1)
            ffn_scalar(act, NBLK1, NBLK0, loads1)
            for q in range(8):
                act.wait_ge(S["gate_exp"], 2 + q)
                g = GA[:, 0, 4 * q:4 * q + 4, :]
                act.activation(g, g, ACT.Silu).then_inc(S["silu_done"], 1)

        @block.vector
        def _(v):
            link = Chain(v, S["dve_step"])
            for h in range(2):
                v.wait_ge(S[f"x_in{h}"], 16)
                i0, n = h * NT // 2, NT // 2
                layer_norm(v, link, RS_, XN, i0, n, S["xn_ready"])
                v.wait_ge(S["xn_ready"], i0 + n)
                layer_norm(v, link, XN, XN2, i0, n, S["xn2_ready"])
                v.wait_ge(S["gate_in"], 48)
                for g in range(h * 4, h * 4 + 4):
                    v.wait_ge(S["tok2_T"], g + 1)
                    v.tensor_scalar(RA[:, 512 * g:512 * g + 512], OBANK[g % 2][:, :], gamma0, None, ALU.mult)\
                     .then_inc(S["tok2_evac"], 1)
            v.wait_ge(S["w_in"], 16 * 10)
            R = 2 * H
            link(v.tensor_scalar(T1[:, 0:1], qscale, kscale, 8.0, ALU.mult, ALU.mult))
            link(v.tensor_copy(qscale, T1[:, 0:1]))
            link(v.tensor_tensor(LG0[0:R, 3000:3128], nkp, nkp, ALU.mult))
            link(v.tensor_reduce(VE[0:R, 0:1], LG0[0:R, 3000:3128], AX.X, ALU.add))
            link(v.tensor_scalar(VE[0:R, 0:1], VE[0:R, 0:1], 1e-24, None, ALU.max))
            rsqrt(v, link, RSTD[0:R, 0:1], VE[0:R, 0:1], T1[0:R, 0:1], T2[0:R, 0:1])
            v.tensor_scalar(nkp, nkp, RSTD[0:R, 0:1], None, ALU.mult).then_inc(S["nk_ready"], 1)
            v.wait_ge(S["nk_full"], 1)
            v.tensor_copy(nkT, TRB[:, 0:R]).then_inc(S["nk_evac"], 1)
            v.wait_ge(S["logits_full"], 1)
            link(v.tensor_tensor(mem0[0].rearrange("p (t e) -> p t e", e=E),
                                 MISC[:, 0:256].rearrange("p (t e) -> p t e", e=E),
                                 gateb.unsqueeze(1).to_broadcast([P, NT, E]), ALU.add))
            v.wait_ge(S["ones_ready"], 1)
            route(v, link, 0, mem0, M1_0, None)

            def sums(a_, i):
                t, k = UNITS[i]
                v.wait_ge(S["sq_done"], a_ * NQ + (i + 1))
                v.tensor_reduce(ss[:, t, 8 * k:8 * k + 8], sq[:, i % 2].rearrange("p (h d) -> p h d", d=DH),
                                AX.X, ALU.add).then_inc(S["ss_done"], 1)
                if k == 3:
                    v.wait_ge(S["ss_done"], a_ * NQ + (i + 1))
                    v.tensor_scalar(ss[:, t], ss[:, t], 1e-24, None, ALU.max).then_inc(S["den_step"], 1)
                    v.wait_ge(S["den_step"], seed_count(a_, t, 0))
                    v.tensor_scalar(xh[:, t], ss[:, t], -0.5, None, ALU.mult)
                    v.tensor_scalar(rn[:, t].bitcast(I32), ss[:, t].bitcast(I32), 1, None, ALU.logical_shift_right)\
                     .then_inc(S["den_step"], 1)
                    v.wait_ge(S["den_step"], seed_count(a_, t, 1))
                    v.tensor_scalar(rn[:, t].bitcast(I32), rn[:, t].bitcast(I32), -1.0, RSQRT_MAGIC,
                                    ALU.mult, ALU.add).then_inc(S["seed_done"], 1)

            DEN_STEP = 8

            def seed_count(a_, t, k):
                if isinstance(a_, int) and a_ == 0:
                    return 2 * t + k + 1
                return (a_ - 1) * DEN_STEP + (4 + 2 * t + k + 1)

            def den_count(b, t, k, wn):
                base = 4 + 4 if wn else 4
                return b * DEN_STEP + (base + 2 * t + k + 1)

            def null_scores(b):
                v.wait_ge(S["sn_full"], b + 1)
                v.scalar_tensor_tensor(out=nsn, in0=MISC[:, 0:64], scalar=-1.0, in1=nbias, op0=ALU.mult,
                                       op1=ALU.subtract).then_inc(S["sn_step"], 1)
                v.wait_ge(S["sn_step"], b * 2 + 1)
                v.tensor_reduce(nmn, nsn.rearrange("p (h n) -> p h n", n=2), AX.X, ALU.min).then_inc(S["sn_step"], 1)
                v.wait_ge(S["sn_step"], b * 2 + 2)

            def rows_max(b, g):
                t, heads = GROUPS[g]
                n = P * (t + 1)
                v.wait_ge(S["s_full"], b * NG + (g + 1))
                v.sem_inc(S["scores_seen"], 1)
                for k, h in enumerate(heads):
                    ins = v.tensor_tensor_reduce(out=Sb[:, g % 2, n * k:n * k + n], in0=SBANK[g % 2][:, n * k:n * k + n],
                                                 in1=alibi[:, h, N - n:N], scale=-1.0,
                                                 scalar=nmn[:, 16 * t + h:16 * t + h + 1], op0=ALU.add, op1=ALU.min,
                                                 accum_out=nm[:, 16 * t + h:16 * t + h + 1])
                ins.then_inc(S["ttr_done"], 1)

            def null_sub(b, t):
                v.wait_ge(S["ttr_done"], b * NG + (4 if t == 0 else NG))
                v.tensor_tensor(ntmp[:, 32 * t:32 * t + 32].rearrange("p (h n) -> p h n", n=2),
                                nm[:, 16 * t:16 * t + 16].unsqueeze(2).to_broadcast([P, H, 2]),
                                nsn[:, 32 * t:32 * t + 32].rearrange("p (h n) -> p h n", n=2),
                                ALU.subtract).then_inc(S["nsub_done"], 1)

            def denominators(b, t, wn):
                v.wait_ge(S["pn_done"], b * 2 + (t + 1))
                d = rden[:, 16 * t:16 * t + 16]
                v.tensor_reduce(d, pn[:, 32 * t:32 * t + 32].rearrange("p (h n) -> p h n", n=2), AX.X, ALU.add)\
                 .then_inc(S["den_step"], 1)
                v.wait_ge(S["den_step"], den_count(b, t, 0, wn))
                v.wait_ge(S["exp_done"], b * NG + (4 if t == 0 else NG))
                v.tensor_tensor(d, d, den[:, 16 * t:16 * t + 16], ALU.add).then_inc(S["den_step"], 1)
                v.wait_ge(S["den_step"], den_count(b, t, 1, wn))
                v.reciprocal(d, d).then_inc(S["rd1_done"], 1)

            def null_turned(b, t):
                v.wait_ge(S["pnT_full"], b * 2 + (t + 1))
                v.tensor_copy(pnT, MISC[0:2 * H, 0:P]).then_inc(S["pnT_evac"], 1)

            def out_norm(b, t):
                v.wait_ge(S["o_full"], b * 2 + (t + 1))
                v.wait_ge(S["rd1_done"], b * 2 + (t + 1))
                for o in range(2):
                    ins = v.tensor_tensor(On[:, 512 * o:512 * o + 512].rearrange("p (h d) -> p h d", d=DH),
                                          OBANK[o][:, :].rearrange("p (h d) -> p h d", d=DH),
                                          rden[:, 16 * t + 8 * o:16 * t + 8 * o + 8].unsqueeze(2).to_broadcast([P, 8, DH]),
                                          ALU.mult)
                ins.then_inc(S["on_done"], 1)

            def y_out(b, t):
                v.wait_ge(S["y_full"], b * 2 + (t + 1))
                v.tensor_copy(RS_[:, bass.ds(b * 2 + t, 1), :].rearrange("p t d -> p (t d)"), MISC[:, 0:D])\
                 .then_inc(S["y_evac"], 1)

            def step(b, p, wn=True):
                for g in range(NG):
                    if g + 1 < NG:
                        rows_max(b, g + 1)
                    if g == 2:
                        null_sub(b, 0)
                    if g == NG - 2:
                        null_sub(b, 1)
                    if wn and 1 <= g <= 4:
                        sums(b + 1, 2 * g - 2)
                        sums(b + 1, 2 * g - 1)
                    if g == 5:
                        denominators(b, 0, wn)
                        out_norm(b, 0)
                    v.wait_ge(S["pt_full"], b * NG + (g + 1))
                    v.tensor_copy(PTb[:, g % 2, :], TRB[:, :]).then_inc(S["pt_evac"], 1)
                    if g == 3:
                        null_turned(b, 0)
                    if g == 8:
                        y_out(b, 0)
                null_turned(b, 1)
                denominators(b, 1, wn)
                out_norm(b, 1)
                if wn:
                    null_scores(b + 1)
                    rows_max(b + 1, 0)
                y_out(b, 1)

            for i in range(NQ):
                sums(0, i)
            null_scores(0)
            rows_max(0, 0)
            pairs(v, 0, NB - 3, step)
            step(NB - 2, 0)
            step(NB - 1, 1, wn=False)

            ffn_vector(v, NBLK0, 0, loads0)

            v.wait_ge(S["y_evac"], 2 * NB)
            v.wait_ge(S["x_back"], 16)
            xr = RA[:, :].rearrange("p (t d) -> p t d", d=D)

            def combine(q, done):
                s = slice(4 * q, 4 * q + 4)
                v.wait_ge(S["silu_done"], done)
                link(v.tensor_tensor(RS_[:, s], RS_[:, s], GA[:, 0, s, :], ALU.mult))
                return v.tensor_tensor(xr[:, s], xr[:, s], RS_[:, s], ALU.add)
            for q in range(8):
                combine(q, q + 1).then_inc(S["x1_ready"], 1)
                if q % 4 == 3:
                    v.wait_ge(S["x1_ready"], q + 1)
                    layer_norm(v, link, xr, XN, (q // 4) * NT // 2, NT // 2, S["xn_ready"])

            v.wait_ge(S["logits_full"], 2)
            link(v.tensor_copy(LG, MISC[:, 0:256]))
            route(v, link, 1, mem1, M1, M2)

            def v_out(b, i3):
                v.wait_ge(S["qkv1_full"], b + 1)
                v.tensor_copy(v1[:, i3], bank[1][:, 0:N]).then_inc(S["v1_evac"], 1)

            SCL = float(D) ** -0.5

            def rows_max1(b, p):
                v.wait_ge(S["s1_full"], b + 1)
                v.sem_inc(S["scores_seen"], 1)
                v.tensor_tensor_reduce(out=s1b[:, p, 0:P], in0=bank[4][:, 0:P], in1=mask1[:, P:2 * P], scale=-SCL,
                                       scalar=-NEG, op0=ALU.add, op1=ALU.min, accum_out=nm1[:, 2 * p:2 * p + 1])
                v.tensor_tensor_reduce(out=s1b[:, p, P:P + N], in0=bank[4][:, P:P + N], in1=mask1[:, :], scale=-SCL,
                                       scalar=-NEG, op0=ALU.add, op1=ALU.min, accum_out=nm1[:, 2 * p + 1:2 * p + 2])\
                 .then_inc(S["ttr1_done"], 1)

            def residual(b, p, i3):
                v.wait_ge(S["exp1_done"], b + 1)
                v.reciprocal(rd1[:, 2 * p:2 * p + 2], den1[:, 2 * p:2 * p + 2]).then_inc(S["rd1_done"], 1)
                v.wait_ge(S["o1_full"], b + 1)
                v.wait_ge(S["rd1_done"], b + (2 * NB + 1))
                for t in range(2):
                    ins = v.scalar_tensor_tensor(out=AO[:, bass.ds(b * 2 + t, 1), :].rearrange("p t d -> p (t d)"),
                                                 in0=bank[6][:, t * D:(t + 1) * D], scalar=rd1[:, 2 * p + t:2 * p + t + 1],
                                                 in1=v1[:, i3, t * D:(t + 1) * D], op0=ALU.mult, op1=ALU.add)
                ins.then_inc(S["o1_done"], 1)

            def step1(b, p, more=2):
                if more >= 1:
                    rows_max1(b + 1, 1 - p)
                v.wait_ge(S["pt1_full"], b + 1)
                v.tensor_copy(pt1, bank[5][:, 0:384]).then_inc(S["pt1_evac"], 1)
                residual(b, p, p)
                if more >= 2:
                    v.wait_ge(S["o1_done"], b + 1)
                    v_out(b + 2, p)
            v_out(0, 0)
            v_out(1, 1)
            rows_max1(0, 0)
            pairs(v, 0, NB - 3, step1)
            for b in range(NB - 2, NB):
                step1(b, b % 2, more=NB - 1 - b)
            v.wait_ge(S["o1_done"], NB)
            for h in range(2):
                layer_norm(v, link, AO, AO, h * NT // 2, NT // 2, S["ao_ready"])
            for g in range(NT // 4):
                v.wait_ge(S["fc_full"], g + 1)
                v.tensor_tensor(RS_[:, 4 * g:4 * g + 4, :], bank[6 + g % 2][:, :].rearrange("p (t d) -> p t d", d=D),
                                bfc.unsqueeze(1).to_broadcast([P, 4, D]), ALU.add).then_inc(S["attn1_done"], 1)

            ffn_vector(v, NBLK1, NBLK0, loads1)

            for q in range(8):
                v.wait_ge(S[f"gathered{q}"], 16 * 4 * 3)
                for i in range(4 * q, 4 * q + 4):
                    ins = v.tensor_scalar(GA[:, 0, i], GA[:, 0, i], G1W[:, i:i + 1], None, ALU.mult)
                link(ins)
                for i in range(4 * q, 4 * q + 4):
                    ins = v.scalar_tensor_tensor(out=GA[:, 0, i], in0=GA[:, 1, i], scalar=G2W[:, i:i + 1],
                                                 in1=GA[:, 0, i], op0=ALU.mult, op1=ALU.add)
                ins.then_inc(S["gate_exp"], 1)
            v.wait_ge(S["attn1_done"], NT // 4)
            for q in range(8):
                combine(q, 8 + q + 1).then_inc(S["out_ready"], 1)


def constants(np):
    c = np.zeros((P, C_END), np.float32)
    p = np.arange(P)
    c[:, C_ID:C_ID + P] = np.eye(P)
    c[:, C_TRI:C_TRI + P] = p[:, None] < p[None, :]
    start = 2.0 ** (-2.0 ** (-(np.log2(H) - 3.0)))
    slopes = np.array([start * start ** i for i in range(H)], np.float32)
    for t in range(2):
        for h in range(H):
            for n in range(NNULL):
                c[:, C_NB + 32 * t + 2 * h + n] = -(t * P + p + NNULL - n) * slopes[h]
    diag = np.where(p[None, :] > p[:, None], NEG, 0.0)
    c[:, C_M1 + P:C_M1 + 2 * P] = diag
    c[:, C_W8:C_W8 + E] = E - np.arange(E)
    c[:, C_RS:C_RS + E * NT] = np.arange(E * NT) % NT != 0
    c[:, C_THR:C_THR + NTHR] = BLK * np.arange(NTHR)
    c[:, C_JJ:C_JJ + NBLK1 + 1] = np.arange(NBLK1 + 1)
    alibi = np.zeros((P, H, N), np.float32)
    dist = (p[:, None] - p[None, :]).astype(np.float32)
    for h in range(H):
        alibi[:, h, 0:P] = -(dist + P) * slopes[h]
        alibi[:, h, P:N] = np.where(dist < 0, np.float32(NEG), -dist * slopes[h])
    return c, alibi


_INS = ['L0_attn_x', 'L0_attn_gamma', 'L0_attn_w_q', 'L0_attn_w_kv', 'L0_attn_q_scale', 'L0_attn_k_scale',
        'L0_attn_w_out', 'L0_ffn_gate_W', 'L0_ffn_gate_b', 'L1_attn_Wq', 'L1_attn_Wk', 'L1_attn_Wv', 'L1_attn_Wfc',
        'L1_attn_bfc', 'L1_attn_gamma', 'L1_attn_beta', 'L1_ffn_Wg']


def kernel(**inputs):
    import numpy as np
    import concourse.bacc as _bacc
    from concourse import mybir as _mybir
    from concourse.bass_utils import run_bass_kernel_spmd as _run

    given = {n: np.ascontiguousarray(inputs[n]) for n in _INS}
    nkv = np.asarray(inputs['L0_attn_null_kv']).reshape(H, NNULL, 2, DH)
    nkp = np.zeros((2 * H, P), np.float32)
    nvb = np.zeros((2 * H, H * DH), np.float32)
    for h in range(H):
        nkp[2 * h:2 * h + 2, DH * (h % 2):DH * (h % 2) + DH] = nkv[h, :, 0]
        nvb[2 * h:2 * h + 2, DH * h:DH * h + DH] = nkv[h, :, 1]
    given["nkp"], given["nvb"] = nkp, nvb
    for l in range(2):
        w2 = np.asarray(inputs[f'L{l}_ffn_W2']).reshape(E, FC, P, D).transpose(0, 2, 1, 3).reshape(E, P, DFF)
        b1 = np.asarray(inputs[f'L{l}_ffn_b1']).reshape(E, FC, P).transpose(0, 2, 1)
        given[f"wp_{l}"] = np.ascontiguousarray(np.concatenate([np.asarray(inputs[f'L{l}_ffn_W1']), w2, b1], axis=2))
        given[f"b2_{l}"] = np.ascontiguousarray(inputs[f'L{l}_ffn_b2'])
    given["const"], given["alibi"] = constants(np)

    nc = _bacc.Bacc("TRN2", target_bir_lowering=False, num_devices=1)
    arrays, a = {}, {}
    for name, x in given.items():
        arrays[f"in_{name}"] = x
        a[name] = nc.dram_tensor(f"in_{name}", x.shape, _mybir.dt.from_np(x.dtype), kind="ExternalInput").ap()
    a["out"] = nc.dram_tensor("out_0", (NB, N, D), _mybir.dt.float32, kind="ExternalOutput").ap()
    block_kernel(nc, a)
    r = _run(nc, [arrays], core_ids=[0])
    return r.results[0]["out_0"]
```

```python
import concourse.bass as bass
from concourse import mybir
from contextlib import ExitStack

F32, I32 = mybir.dt.float32, mybir.dt.int32
ACT, ALU, AX = mybir.ActivationFunctionType, mybir.AluOpType, mybir.AxisListType

NB, N, D = 16, 256, 128
P = 128
T = NB * N
NT = T // P
H, DH = 16, 64
HC = H // 2
NNULL = 2
E, DFF = 8, 512
FC = DFF // P
BLK = 256
CAP = 2 * 2 * T // E
NBLK0 = (T + E * (BLK - 1)) // BLK
NBLK1 = (2 * T + E * (BLK - 1)) // BLK
NBUF = 4
WCOLS = 2 * DFF + FC
EPS = 1e-5
NEG = -1e30
BIG = float(1 << 20)
RSQRT_MAGIC = float(0x5F3759DF)
NTHR = T // BLK

C_ID, C_TRI, C_NB, C_M1, C_W8, C_RS, C_THR, C_JJ = 0, 128, 256, 320, 576, 584, 840, 856
C_END = C_JJ + (NBLK1 + 1)

GROUPS = [(0, [8 * (g // 2) + g % 2 + 2 * k for k in range(4)]) for g in range(4)] + \
         [(1, [4 * (g // 2) + g % 2 + 2 * k for k in range(2)]) for g in range(8)]
NG = len(GROUPS)
NU, NQ = 12, 8


RING_USES = {
    0: ([("unit", 10, 1)], []), 2: ([("unit", 11, 1)], []),
    4: ([("qk", 0, 1), ("qk", 1, 1)], [("unit", 0, 2)]),
    5: ([("qk", 2, 1), ("qk", 3, 1)], [("unit", 1, 2)]),
    6: ([("qk", 4, 1), ("qk", 5, 1)], [("out", 0, 0), ("out", 0, 1)]),
    7: ([("qk", 6, 1), ("qk", 7, 1)], []),
    8: ([("unit", 2, 2)], []), 9: ([("unit", 3, 2)], []), 10: ([("unit", 4, 2)], []), 11: ([("unit", 5, 2)], []),
    NG: ([("unit", 6, 2)], [("unit", 7, 2), ("out", 1, 0), ("out", 1, 1), ("unit", 8, 2), ("unit", 9, 2)])}


def ring_uses(g, part, more):
    return [u for u in RING_USES.get(g, ([], []))[part] if u[0] == "out" or u[2] <= more]


def ring_order(more):
    return [u for g in range(NG + 1) for part in (0, 1) for u in ring_uses(g, part, more)]


RING_FIRST = [("unit", u, 0) for u in range(8)] + [("qk", s, 0) for s in range(8)] + \
             [("unit", u, 0) for u in range(8, 12)] + [("unit", u, 1) for u in range(10)]
RING_START = len(RING_FIRST)
RING_STEP = len(ring_order(2))
UNITS = [(0, 0), (0, 1), (0, 2), (0, 3), (1, 0), (1, 1), (1, 2), (1, 3), (0, 4), (0, 5), (1, 4), (1, 5)]


def block_kernel(nc, a):
    xe = nc.dram_tensor("expert_rows", (NBLK1 * BLK, D), F32).ap()
    ye = nc.dram_tensor("expert_out", (NBLK1 * BLK, D), F32).ap()
    x_v = a["L0_attn_x"].rearrange("b (t p) d -> p (b t) d", p=P)
    out_v = a["out"].rearrange("b (t p) d -> p (b t) d", p=P)

    ctx = ExitStack()
    with ctx:
        def sb(name, shape, dt=F32):
            return ctx.enter_context(nc.sbuf_tensor(name, shape, dt))

        def sem(name):
            return ctx.enter_context(nc.semaphore(name))

        bank = [ctx.enter_context(nc.psum_tensor(f"bank{i}", [P, 512], F32)) for i in range(8)]
        RING, SBANK, OBANK, MISC, TRB = bank[0:2], bank[2:4], bank[4:6], bank[6], bank[7]

        const = sb("const", [P, C_END])
        ident, tri = const[:, C_ID:C_ID + P], const[:, C_TRI:C_TRI + P]
        nbias = const[:, C_NB:C_NB + 64]
        mask1 = const[:, C_M1:C_M1 + 256]
        ones = sb("ones", [P, P])
        XN = sb("XN", [P, NT, D])
        RA = sb("RA", [P, NT * D])
        RS_ = sb("RS_", [P, NT, D])
        small = sb("small", [P, 640])
        qscale, gamma0, gamma1, beta1 = (small[:, i:i + 1] for i in range(4))
        kscale = small[:, 4:5]
        gateb = small[:, 8:16]
        wn = small[:, 16:48]
        bfc = small[:, 48:176]
        MV = small[:, 176:240].rearrange("p (n s) -> p n s", s=2)
        VE, RSTD, T1, T2 = (small[:, 240 + 32 * i:272 + 32 * i] for i in range(4))
        G1W, G2W = small[:, 368:400], small[:, 400:432]
        ST6 = small[:, 432:624].rearrange("p (n s) -> p n s", s=6)
        gw1, gw0 = small[:, 624:632], small[:, 632:640]
        slots = sb("slots", [P, 2, NT], I32)
        owner = sb("owner", [1, NBLK1 + 1], I32)

        ARENA = 39000
        arena = sb("arena", [P, ARENA])
        at = [0]

        def take(n, rows=P):
            at[0] += n
            assert at[0] <= ARENA, at[0]
            return arena[0:rows, at[0] - n:at[0]]

        raw = take(2 * 4 * 512).rearrange("p (t n) -> p t n", t=2)
        qkn = take(2 * 4 * 512).rearrange("p (t n) -> p t n", t=2)
        sq = take(2 * 512).rearrange("p (i n) -> p i n", i=2)
        qT = take(2 * HC * N).rearrange("p (i c n) -> p i c n", i=2, c=HC)
        kT = take(2 * HC * N).rearrange("p (i c n) -> p i c n", i=2, c=HC)
        Vt = take(2 * 2 * H * DH).rearrange("p (i t n) -> p i t n", i=2, t=2)
        alibi = take(H * N).rearrange("p (h n) -> p h n", h=H)
        wqkv = take(3 * H * DH)
        wo0 = take(HC * D).rearrange("p (c n) -> p c n", c=HC)
        nvT = take(HC * 2 * H).rearrange("p (c n) -> p c n", c=HC)
        nvw = take(D, 2 * H)
        route0_at = at[0]
        Sb = take(3 * 512).rearrange("p (i n) -> p i n", i=3)
        Pb = take(3 * 512).rearrange("p (i n) -> p i n", i=3)
        PTb = take(2 * 512).rearrange("p (i n) -> p i n", i=2)
        On = take(H * DH)
        OnT = take(H * DH).rearrange("p (c n) -> p c n", c=HC)
        xa = take(2 * N).rearrange("p (i n) -> p i n", i=2)
        ss = take(64).rearrange("p (t n) -> p t n", t=2)
        rn = take(64).rearrange("p (t n) -> p t n", t=2)
        nw1, nw2, c15 = take(64), take(64), take(64)
        xh = take(64).rearrange("p (t n) -> p t n", t=2)
        nkT = take(2 * H)
        snr = take(64)
        nsn = take(64)
        nmn = take(32)
        nm = take(32)
        den = take(32)
        ntmp = take(64)
        pn = take(64)
        pns = take(64)
        rden = take(32)
        pnT = take(P, 2 * H)
        nkp = take(P, 2 * H)
        attn_end = at[0]
        XN2 = raw_flat = arena[:, 0:NT * D].rearrange("p (t n) -> p t n", t=NT)
        XNT = arena[:, NT * D:2 * NT * D]
        zeros = arena[:, 2 * NT * D:2 * NT * D + 512]

        at[0] = 0
        GA = take(2 * NT * D).rearrange("p (k t n) -> p k t n", k=2, t=NT)
        XN1T = take(NT * D)
        AO = take(NT * D).rearrange("p (t n) -> p t n", t=NT)
        wb = take(NBUF * WCOLS).rearrange("p (i n) -> p i n", i=NBUF)
        b2b = take(NBUF * D).rearrange("p (i n) -> p i n", i=NBUF)
        xb = take(NBUF * 2 * D).rearrange("p (i t n) -> p i t n", i=NBUF, t=2)
        xbT = take(2 * BLK).rearrange("p (i n) -> p i n", i=2)
        hT = take(2 * FC * BLK).rearrange("p (i n) -> p i n", i=2)
        yb = take(2 * 2 * D).rearrange("p (i n) -> p i n", i=2)
        wq1, wk1, wv1, wfc = (take(D) for _ in range(4))
        xa1 = take(2 * N).rearrange("p (i n) -> p i n", i=2)
        qk1 = take(2 * 2 * N).rearrange("p (i n) -> p i n", i=2)
        v1 = take(3 * N).rearrange("p (i n) -> p i n", i=3)
        s1b = take(2 * 384).rearrange("p (i n) -> p i n", i=2)
        p1b = take(2 * 384).rearrange("p (i n) -> p i n", i=2)
        pt1 = take(384)
        nm1, den1, rd1 = (take(4) for _ in range(3))
        LG, EQ, M1, M2, R1, R2 = (take(256) for _ in range(6))
        TOT, INC = take(512), take(512)
        MX, KM, MX2, PZ = (take(32) for _ in range(4))
        CNT = take(64)
        CMP = take(320)
        route_end = at[0]
        LG0 = arena[:, route0_at:route0_at + 3400]

        S = {n: sem(n) for n in (
            "const_in", "x_in0", "x_in1", "gate_in", "gate1_in", "w_in", "zero_done", "xe_zero", "ones_ready", "c15_ready", "dve_step",
            "xn_ready", "xn2_ready", "tok_T", "tok_evac", "tok2_T", "tok2_evac", "logits_full", "mask_ready",
            "rank_full", "nk_ready", "nk_full", "nk_evac", "wqT_full", "wqT_evac", "wn_full", "wn_evac", "slots_ready", "scattered",
            "xa_in0", "xa_in1", "ring_full", "ring_evac", "sq_done", "ss_done", "seed_done", "newton", "qn_done", "seed_step", "pn_scaled",
            "sn_full", "s_full", "scores_seen", "ttr_done", "sn_step", "exp_done", "nsub_done", "pn_done", "den_step", "pt_full",
            "pt_evac", "pnT_full", "pnT_evac", "o_full", "on_done", "y_full", "y_evac",
            *[f"rows_in{q}" for q in range(NBUF)], *[f"w_in{q}" for q in range(NBUF)], "xT_full", "xT_evac", "h_full", "gelu_done",
            "ye_full", "ye_evac", "stored0", "stored1", *[f"gathered{q}" for q in range(8)], "silu_done", "x_back", "x1_ready",
            "l1w_in", "qkv1_full", "qk1_evac", "v1_evac", "s1_full", "ttr1_done", "exp1_done", "pt1_full",
            "pt1_evac", "o1_full", "rd1_done", "o1_done", "xa1_in0", "xa1_in1", "ao_ready", "ao_T", "ao_evac",
            "fc_full", "attn1_done", "gate_exp", "out_ready", "out_done", "wexp")}

        class Chain:
            def __init__(self, eng, s):
                self.eng, self.s, self.n = eng, s, 0

            def __call__(self, ins):
                ins.then_inc(self.s, 1)
                self.n += 1
                self.eng.wait_ge(self.s, self.n)

        def ring_use(b, use, more=2):
            if isinstance(b, int) and b == -1:
                return RING_FIRST.index(use)
            base = b * RING_STEP + RING_START
            if more == 0:
                base = RING_START + (NB - 2) * RING_STEP + len(ring_order(1))
            return base + ring_order(more).index(use)

        def ring_bank(use, more=2, start=False):
            if start:
                return RING_FIRST.index(use) % 2
            return ring_use(0, use, more) % 2

        def pairs(eng, first, last, body):
            n = (last - first + 1) // 2
            if n > 0:
                with eng.Fori(0, n) as i:
                    body(i * 2 + first, first % 2)
                    body(i * 2 + (first + 1), (first + 1) % 2)
            if (last - first + 1) % 2:
                body(last, last % 2)

        def rsqrt(eng, link, out, x, t1, t2, seed=True):
            if seed:
                link(eng.tensor_scalar(t1.bitcast(I32), x.bitcast(I32), 1, None, ALU.logical_shift_right))
                link(eng.tensor_scalar(out.bitcast(I32), t1.bitcast(I32), -1.0, RSQRT_MAGIC, ALU.mult, ALU.add))
            for _ in range(3):
                link(eng.tensor_tensor(t1, out, out, ALU.mult))
                link(eng.tensor_tensor(t2, t1, x, ALU.mult))
                link(eng.tensor_scalar(t1, t2, -0.5, 1.5, ALU.mult, ALU.add))
                link(eng.tensor_tensor(out, out, t1, ALU.mult))

        def layer_norm(v, link, src, dst, i0, n, done):
            for i in range(i0, i0 + n):
                ins = v.bn_stats(ST6[:, i], src[:, i])
            link(ins)
            for i in range(i0, i0 + n):
                ins = v.bn_aggr(MV[:, i], ST6[:, i])
            link(ins)
            s = slice(i0, i0 + n)
            link(v.tensor_scalar(VE[:, s], MV[:, s, 1], EPS, None, ALU.add))
            rsqrt(v, link, RSTD[:, s], VE[:, s], T1[:, s], T2[:, s])
            for i in range(i0, i0 + n):
                v.tensor_scalar(dst[:, i], src[:, i], MV[:, i, 0:1], RSTD[:, i:i + 1],
                                ALU.subtract, ALU.mult).then_inc(done, 1)

        def route(v, link, layer, mem, M1, M2):
            LG, EQ, R1, R2, TOT, INC, MX, KM, MX2, PZ, CNT, CMP = mem
            c = lambda lo, n: const[:, lo:lo + n]
            te = lambda x: x.rearrange("p (t e) -> p t e", e=E)
            et = lambda x: x.rearrange("p (e t) -> p e t", e=E)
            w8 = c(C_W8, E).unsqueeze(1).to_broadcast([P, NT, E])
            up = lambda x: x.unsqueeze(2).to_broadcast([P, NT, E])
            nch = 1 + layer

            def first_max(M, lg, mx):
                link(v.tensor_reduce(mx, te(lg), AX.X, ALU.max))
                link(v.tensor_tensor(te(EQ), te(lg), up(mx), ALU.is_equal))
                link(v.tensor_tensor(te(EQ), te(EQ), w8, ALU.mult))
                link(v.tensor_reduce(KM, te(EQ), AX.X, ALU.max))
                v.tensor_tensor(te(M), te(EQ), up(KM), ALU.is_equal).then_inc(S["mask_ready"], 1)

            base = 0 if layer == 0 else 1
            first_max(M1, LG, MX)
            if layer:
                v.wait_ge(S["mask_ready"], base + 1)
                link(v.scalar_tensor_tensor(out=R2, in0=M1, scalar=3.0 * NEG, in1=LG, op0=ALU.mult, op1=ALU.add))
                first_max(M2, R2, MX2)
                link(v.tensor_tensor(te(R1), te(LG), up(MX), ALU.subtract))
                v.tensor_copy(R2, R1).then_inc(S["gate_exp"], 1)
                v.wait_ge(S["wexp"], 1)
                link(v.tensor_reduce(PZ, te(R1), AX.X, ALU.add))
                link(v.reciprocal(KM, PZ))
                link(v.tensor_tensor(te(R1), te(R1), up(KM), ALU.mult))
                link(v.tensor_tensor(EQ, R1, M1, ALU.mult))
                link(v.tensor_reduce(G1W, te(EQ), AX.X, ALU.add))
                v.wait_ge(S["mask_ready"], base + 2)
                link(v.tensor_tensor(EQ, R1, M2, ALU.mult))
                link(v.tensor_reduce(G2W, te(EQ), AX.X, ALU.add))
                link(v.scalar_tensor_tensor(out=PZ, in0=G1W, scalar=1e-9, in1=G2W, op0=ALU.add, op1=ALU.add))
                link(v.reciprocal(KM, PZ))
                link(v.tensor_tensor(G1W, G1W, KM, ALU.mult))
                link(v.tensor_tensor(G2W, G2W, KM, ALU.mult))
            v.wait_ge(S["rank_full"], layer + 1)
            for k in range(nch):
                tot, inc = TOT[:, 256 * k:256 * k + 256], INC[:, 256 * k:256 * k + 256]
                link(v.tensor_copy(et(tot), te(SBANK[1][:, 256 * k:256 * k + 256]).rearrange("p t e -> p e t")))
                link(v.tensor_tensor_scan(inc, c(C_RS, 256), tot, 0.0, ALU.mult, ALU.add))
                link(v.tensor_copy(CNT[:, 8 * k:8 * k + 8], et(inc)[:, :, NT - 1]))
                link(v.tensor_tensor(inc, inc, tot, ALU.subtract))
            cnt = CNT[:, 0:8]
            if layer:
                inc = INC[:, 256:512]
                link(v.tensor_tensor(et(inc), et(inc), CNT[:, 0:8].unsqueeze(2).to_broadcast([P, E, NT]), ALU.add))
                cnt = CNT[:, 16:24]
                link(v.tensor_tensor(cnt, CNT[:, 0:8], CNT[:, 8:16], ALU.add))
                link(v.tensor_scalar(cnt, cnt, float(CAP), None, ALU.min))
            cm = CMP[:, 0:E * NTHR].rearrange("p (e k) -> p e k", e=E)
            link(v.tensor_tensor(cm, cnt.unsqueeze(2).to_broadcast([P, E, NTHR]),
                                 c(C_THR, NTHR).unsqueeze(1).to_broadcast([P, E, NTHR]), ALU.is_gt))
            nblk, bend, bst = CNT[:, 24:32], CNT[:, 32:40], CNT[:, 40:48]
            link(v.tensor_reduce(nblk, cm, AX.X, ALU.add))
            link(v.tensor_tensor_scan(bend, ones[:, 0:E], nblk, 0.0, ALU.mult, ALU.add))
            link(v.tensor_tensor(bst, bend, nblk, ALU.subtract))
            link(v.tensor_scalar(bst, bst, float(BLK), None, ALU.mult))
            nj = NBLK1 + 1
            cj = CMP[0:1, 0:nj * E].rearrange("p (j e) -> p j e", e=E)
            link(v.tensor_tensor(cj, const[0:1, C_JJ:C_JJ + nj].unsqueeze(2).to_broadcast([1, nj, E]),
                                 bend[0:1].unsqueeze(1).to_broadcast([1, nj, E]), ALU.is_ge))
            link(v.tensor_reduce(EQ[0:1, 0:nj], cj, AX.X, ALU.add))
            link(v.tensor_scalar(EQ[0:1, 0:nj], EQ[0:1, 0:nj], float(E - 1), None, ALU.min))
            link(v.tensor_copy(owner[:, :], EQ[0:1, 0:nj]))
            for k in range(nch):
                M = (M1, M2)[k]
                inc = INC[:, 256 * k:256 * k + 256]
                link(v.tensor_tensor(te(R1), te(SBANK[0][:, 256 * k:256 * k + 256]),
                                     et(inc).rearrange("p e t -> p t e"), ALU.add))
                link(v.tensor_tensor(EQ, R1, M, ALU.mult))
                link(v.tensor_reduce(PZ, te(EQ), AX.X, ALU.add))
                link(v.tensor_tensor(te(EQ), te(M), bst.unsqueeze(1).to_broadcast([P, NT, E]), ALU.mult))
                link(v.tensor_reduce(KM, te(EQ), AX.X, ALU.add))
                link(v.tensor_tensor(KM, KM, PZ, ALU.add))
                if layer:
                    link(v.tensor_scalar(MX, PZ, float(CAP), None, ALU.is_lt))
                    W = (G1W, G2W)[k]
                    link(v.tensor_tensor(W, W, MX, ALU.mult))
                    link(v.tensor_scalar(MX, MX, -BIG, BIG, ALU.mult, ALU.add))
                    link(v.tensor_tensor(KM, KM, MX, ALU.add))
                v.tensor_copy(slots[:, k, :], KM).then_inc(S["slots_ready"], 1)

        def scatter_rows(pool, layer):
            pool.wait_ge(S["slots_ready"], (1, 3)[layer])
            for k in range(1 + layer):
                for i in range(NT):
                    pool.indirect_dma_start(
                        xe[:, :], bass.IndirectOffsetOnAxis(ap=slots[:, k, i:i + 1], axis=0), XN[:, i, :], None,
                        bounds_check=NBLK1 * BLK - 1, oob_is_err=False).then_inc(S["scattered"], 16)

        def gather_rows(pool, layer):
            rows = (NBLK0, NBLK1)[layer] * BLK
            for i in range(NT):
                for k in range(1 + layer):
                    pool.indirect_dma_start(
                        GA[:, k, i, :], None, ye[0:rows, :], bass.IndirectOffsetOnAxis(ap=slots[:, k, i:i + 1], axis=0),
                        bounds_check=rows - 1, oob_is_err=False).then_inc(S[f"gathered{i // 4}"], 16)

        def quads(eng, first, last, body):
            n = (last - first + 1) // NBUF
            if n > 0:
                with eng.Fori(0, n) as i:
                    for q in range(NBUF):
                        body(i * NBUF + (first + q), q, i + first // NBUF)
            for j in range(first + n * NBUF, last + 1):
                body(j, j % NBUF, j // NBUF)

        def ffn_sync(sp, layer, nblk, base):
            W, B2 = a[f"wp_{layer}"], a[f"b2_{layer}"]

            def load_rows(j, q):
                src = xe[bass.ds(j * BLK, BLK), :].rearrange("(t p) d -> p t d", p=P)
                sp.dma_start(xb[:, q], src).then_inc(S[f"rows_in{q}"], 16)

            def load_weights(j, q):
                e = sp.value_load(owner[0:1, bass.ds(j, 1)], min_val=0, max_val=E - 1)
                sp.dma_start(wb[:, q], W[bass.ds(e, 1)].rearrange("e p n -> p (e n)")).then_inc(S[f"w_in{q}"], 16)
                sp.dma_start(b2b[:, q], B2[bass.ds(e, 1)].to_broadcast([P, D])).then_inc(S[f"w_in{q}"], 16)

            def step(j, q, more=True):
                p = q % 2
                if more:
                    sp.wait_ge(S["xT_full"], j + (base + 1))
                    load_rows(j + NBUF, q)
                sp.wait_ge(S["ye_evac"], j + (base + 1))
                if more:
                    load_weights(j + NBUF, q)
                dst = ye[bass.ds(j * BLK, BLK), :].rearrange("(t p) d -> p t d", p=P)
                sp.dma_start(dst, yb[:, p].rearrange("p (t d) -> p t d", t=2)).then_inc(S[f"stored{p}"], 16)

            for j in range(NBUF):
                load_rows(j, j)
                load_weights(j, j)
            m = (nblk - NBUF) // NBUF * NBUF
            quads(sp, 0, m - 1, lambda j, q, i: step(j, q))
            for j in range(m, nblk):
                step(j, j % NBUF, more=j + NBUF < nblk)

        def ffn_tensor(pe, nblk, base, counts):
            XT, HB, YB = bank[0:2], bank[2:6], bank[6:8]

            def turn(j, q, i):
                pe.wait_ge(S[f"rows_in{q}"], (i + (counts[q] + 1)) * 16)
                for t in range(2):
                    mm = pe.transpose(XT[q % 2][:, t * P:(t + 1) * P], xb[:, q, t, :], ident)
                mm.then_inc(S["xT_full"], 1)

            def up(j, q, i):
                pe.wait_ge(S["xT_evac"], j + (base + 1))
                pe.wait_ge(S[f"w_in{q}"], (i + (counts[q] + 1)) * 32)
                for c in range(FC):
                    mm = pe.matmul(HB[2 * (q % 2) + c // 2][:, (c % 2) * BLK:(c % 2 + 1) * BLK],
                                   wb[:, q, c * P:(c + 1) * P], xbT[:, q % 2, :], start=True, stop=True)
                mm.then_inc(S["h_full"], 1)

            def down(j, q):
                p = q % 2
                pe.wait_ge(S["gelu_done"], j + (base + 1))
                if base or not isinstance(j, int) or j >= 2:
                    pe.wait_ge(S["ye_evac"], j + (base - 1))
                for t in range(2):
                    for c in range(FC):
                        mm = pe.matmul(YB[p][:, t * D:(t + 1) * D], hT[:, p, c * BLK + t * P:c * BLK + (t + 1) * P],
                                       wb[:, q, DFF + c * D:DFF + (c + 1) * D], start=(c == 0), stop=(c == FC - 1))
                mm.then_inc(S["ye_full"], 1)

            def step(j, q, i, more=2):
                if more >= 2:
                    turn(j + 2, (q + 2) % NBUF, i + (q + 2) // NBUF)
                if more >= 1:
                    up(j + 1, (q + 1) % NBUF, i + (q + 1) // NBUF)
                down(j, q)

            turn(0, 0, 0)
            turn(1, 1, 0)
            up(0, 0, 0)
            for j in range(NBUF):
                step(j, j, 0)
            m = (nblk - 2) // NBUF * NBUF
            quads(pe, NBUF, m - 1, step)
            for j in range(m, nblk):
                step(j, j % NBUF, j // NBUF, more=min(2, nblk - 1 - j))

        def ffn_scalar(act, nblk, base, counts):
            HB = bank[2:6]

            def gelu(j, q, i):
                p = q % 2
                act.wait_ge(S["h_full"], j + (base + 1))
                act.wait_ge(S[f"w_in{q}"], (i + (counts[q] + 1)) * 32)
                for c in range(FC):
                    ins = act.activation(hT[:, p, c * BLK:(c + 1) * BLK], HB[2 * p + c // 2][:, (c % 2) * BLK:(c % 2 + 1) * BLK],
                                         ACT.Gelu, bias=wb[:, q, 2 * DFF + c:2 * DFF + c + 1])
                ins.then_inc(S["gelu_done"], 1)

            quads(act, 0, nblk - 1, gelu)

        def ffn_vector(v, nblk, base, counts):
            XT, YB = bank[0:2], bank[6:8]
            before = (base + 1) // 2, base // 2

            def evac_x(j, p):
                v.wait_ge(S["xT_full"], j + (base + 1))
                v.tensor_copy(xbT[:, p, :], XT[p][:, 0:BLK]).then_inc(S["xT_evac"], 1)

            def add_b2(j, q, i):
                p = q % 2
                v.wait_ge(S["ye_full"], j + (base + 1))
                v.wait_ge(S[f"w_in{q}"], (i + (counts[q] + 1)) * 32)
                if not isinstance(j, int) or j >= 2 or base:
                    v.wait_ge(S[f"stored{p}"], (i * 2 + (q // 2 + before[p])) * 16)
                v.tensor_tensor(yb[:, p, :].rearrange("p (t d) -> p t d", t=2),
                                YB[p][:, 0:2 * D].rearrange("p (t d) -> p t d", t=2),
                                b2b[:, q].unsqueeze(1).to_broadcast([P, 2, D]), ALU.add).then_inc(S["ye_evac"], 1)

            def step(j, q, i, more=True):
                if more:
                    evac_x(j + 2, q % 2)
                add_b2(j, q, i)

            evac_x(0, 0)
            evac_x(1, 1)
            for j in range(NBUF):
                step(j, j, 0)
            m = (nblk - 2) // NBUF * NBUF
            quads(v, NBUF, m - 1, step)
            for j in range(m, nblk):
                step(j, j % NBUF, j // NBUF, more=j + 2 < nblk)

        loads0 = (0,) * NBUF
        loads1 = tuple((NBLK0 + NBUF - 1 - q) // NBUF for q in range(NBUF))

        def stores(layer):
            return (NBLK0 + 1) // 2 + layer * ((NBLK1 + 1) // 2), NBLK0 // 2 + layer * (NBLK1 // 2)

        M1_0 = LG0[:, 256 * 2:256 * 3]
        mem0 = [LG0[:, 0:256], LG0[:, 256:512], LG0[:, 768:1024], LG0[:, 1024:1280], LG0[:, 1280:1792],
                LG0[:, 1792:2304], LG0[:, 2304:2336], LG0[:, 2336:2368], LG0[:, 2368:2400], LG0[:, 2400:2432],
                LG0[:, 2432:2496], LG0[:, 2496:2816]]
        mem1 = [LG, EQ, R1, R2, TOT, INC, MX, KM, MX2, PZ, CNT, CMP]
        RB = lambda b: bass.ds(b * N, N)

        block = ctx.enter_context(nc.Block())

        @block.sync
        def _(sp):
            sp.dma_start(const[:, :], a["const"]).then_inc(S["const_in"], 16)
            for h in range(2):
                s = slice(h * NT // 2, (h + 1) * NT // 2)
                sp.dma_start(RS_[:, s], x_v[:, s]).then_inc(S[f"x_in{h}"], 16)
            sp.dma_start(gateb, a["L0_ffn_gate_b"].unsqueeze(0).to_broadcast([P, E])).then_inc(S["gate_in"], 16)
            sp.dma_start(gamma0, a["L0_attn_gamma"].unsqueeze(1)).then_inc(S["gate_in"], 16)
            sp.dma_start(gw0, a["L0_ffn_gate_W"]).then_inc(S["gate_in"], 16)
            for h in range(2):
                sp.dma_start(qscale[64 * h:64 * h + 64], a["L0_attn_q_scale"].unsqueeze(1)).then_inc(S["w_in"], 16)
                sp.dma_start(kscale[64 * h:64 * h + 64], a["L0_attn_k_scale"].unsqueeze(1)).then_inc(S["w_in"], 16)
            sp.dma_start(nkp, a["nkp"]).then_inc(S["w_in"], 16)
            sp.dma_start(wqkv[:, 0:H * DH], a["L0_attn_w_q"]).then_inc(S["w_in"], 16)
            sp.dma_start(wqkv[:, H * DH:3 * H * DH], a["L0_attn_w_kv"]).then_inc(S["w_in"], 16)
            sp.dma_start(alibi, a["alibi"]).then_inc(S["w_in"], 16)
            sp.dma_start(nvT, a["nvT"]).then_inc(S["w_in"], 16)
            sp.dma_start(wo0, a["L0_attn_w_out"].rearrange("(c p) n -> p c n", p=P)).then_inc(S["w_in"], 16)
            sp.wait_ge(S["zero_done"], 1)
            sp.dma_start(xe.rearrange("(p r) d -> p (r d)", p=P).rearrange("p (r c) -> p r c", c=512 if (NBLK1 * 2 * D) % 512 == 0 else 256),
                         zeros[:, 0:(512 if (NBLK1 * 2 * D) % 512 == 0 else 256)].unsqueeze(1).to_broadcast(
                             [P, NBLK1 * 2 * D // (512 if (NBLK1 * 2 * D) % 512 == 0 else 256), (512 if (NBLK1 * 2 * D) % 512 == 0 else 256)])).then_inc(S["xe_zero"], 16)

            def load_xa(b, p):
                sp.dma_start(xa[:, p], RA[:, RB(b)]).then_inc(S[f"xa_in{p}"], 16)

            sp.wait_ge(S["tok2_evac"], NT // 4)
            load_xa(0, 0)
            load_xa(1, 1)

            def attn_step(b, p):
                sp.wait_ge(S["sn_full"], b + 2)
                load_xa(b + 3, 1 - p)

            sp.wait_ge(S["sn_full"], 1)
            sp.wait_ge(S["ring_evac"], ring_use(-1, ("unit", NU - 1, 0)) + 1)
            load_xa(2, 0)
            pairs(sp, 0, NB - 4, attn_step)

            sp.wait_ge(S["y_evac"], 2 * NB)
            sp.wait_ge(S["scattered"], 16 * NT)
            sp.dma_start(RA[:, :].rearrange("p (t d) -> p t d", d=D), x_v).then_inc(S["x_back"], 16)
            for w, name in ((wq1, "L1_attn_Wq"), (wk1, "L1_attn_Wk"), (wv1, "L1_attn_Wv"), (wfc, "L1_attn_Wfc")):
                sp.dma_start(w, a[name]).then_inc(S["l1w_in"], 16)
            sp.dma_start(gamma1, a["L1_attn_gamma"].unsqueeze(1)).then_inc(S["l1w_in"], 16)
            sp.dma_start(beta1, a["L1_attn_beta"].unsqueeze(1)).then_inc(S["l1w_in"], 16)
            sp.dma_start(bfc, a["L1_attn_bfc"].unsqueeze(0).to_broadcast([P, D])).then_inc(S["l1w_in"], 16)
            sp.dma_start(gw1, a["L1_ffn_Wg"]).then_inc(S["gate1_in"], 16)
            ffn_sync(sp, 0, NBLK0, 0)

            sp.wait_ge(S["tok_evac"], 2 * (NT // 4))

            def load_xa1(b, p):
                sp.dma_start(xa1[:, p], XN1T[:, RB(b)]).then_inc(S[f"xa1_in{p}"], 16)

            load_xa1(0, 0)
            load_xa1(1, 1)

            def attn1_step(b, p):
                sp.wait_ge(S["qkv1_full"], b + 1)
                load_xa1(b + 2, p)

            pairs(sp, 0, NB - 3, attn1_step)

            sp.wait_ge(S["scattered"], 16 * 3 * NT)
            ffn_sync(sp, 1, NBLK1, NBLK0)
            for q in range(8):
                s = slice(4 * q, 4 * q + 4)
                sp.wait_ge(S["out_ready"], q + 1)
                sp.dma_start(out_v[:, s], RA[:, 512 * q:512 * q + 512].rearrange("p (t d) -> p t d", d=D))\
                  .then_inc(S["out_done"], 16)
            sp.wait_ge(S["out_done"], 16 * 8)

        @block.gpsimd
        def _(pool):
            pool.memset(zeros, 0.0).then_inc(S["zero_done"], 1)
            pool.memset(ones[:, :], 1.0).then_inc(S["ones_ready"], 1)
            pool.memset(c15, 1.5).then_inc(S["c15_ready"], 1)
            pool.wait_ge(S["c15_ready"], 1)

            def squares(a_, use):
                for i in range(NQ):
                    t, k = UNITS[i]
                    pool.wait_ge(S["ring_evac"], use(i) + 1)
                    if i >= 2:
                        pool.wait_ge(S["ss_done"], a_ * NQ + (i - 1))
                    r = raw[:, t, 512 * k:512 * k + 512]
                    pool.tensor_tensor(sq[:, i % 2], r, r, ALU.mult).then_inc(S["sq_done"], 1)

            def normalise(a_):
                pool.wait_ge(S["seed_done"], a_ + 1)
                y, n = rn[:, :, :].rearrange("p t n -> p (t n)"), 0
                x = xh[:, :, :].rearrange("p t n -> p (t n)")
                for _ in range(3):
                    for out, i0, i1, op in ((nw1, y, y, ALU.mult), (nw2, nw1, x, ALU.mult),
                                            (nw1, nw2, c15, ALU.add), (y, y, nw1, ALU.mult)):
                        pool.tensor_tensor(out, i0, i1, op).then_inc(S["newton"], 1)
                        n += 1
                        pool.wait_ge(S["newton"], a_ * 12 + n)
                for t in range(2):
                    for k in range(4):
                        pool.tensor_tensor(qkn[:, t, 512 * k:512 * k + 512].rearrange("p (h d) -> p h d", d=DH),
                                           raw[:, t, 512 * k:512 * k + 512].rearrange("p (h d) -> p h d", d=DH),
                                           rn[:, t, 8 * k:8 * k + 8].unsqueeze(2).to_broadcast([P, 8, DH]),
                                           ALU.mult).then_inc(S["qn_done"], 1)

            squares(0, lambda i: ring_use(-1, ("unit", i, 0)))
            normalise(0)
            squares(1, lambda i: ring_use(-1, ("unit", i, 1)))

            def step(b, p):
                normalise(b + 1)
                squares(b + 2, lambda i: ring_use(b, ("unit", i, 2)))

            pairs(pool, 0, NB - 3, step)
            normalise(NB - 1)
            pool.wait_ge(S["xe_zero"], 16)
            scatter_rows(pool, 0)

            for p in range(2):
                pool.wait_ge(S[f"stored{p}"], 16 * stores(0)[p])
            gather_rows(pool, 0)
            scatter_rows(pool, 1)
            pool.wait_ge(S["silu_done"], 8)
            pool.wait_ge(S["x1_ready"], 8)
            pool.memset(GA[:, :, :, :].rearrange("p k t n -> p (k t n)"), 0.0).then_inc(S["zero_done"], 1)
            pool.wait_ge(S["zero_done"], 2)
            for p in range(2):
                pool.wait_ge(S[f"stored{p}"], 16 * stores(1)[p])
            gather_rows(pool, 1)

        @block.tensor
        def _(pe):
            def gate_logits(layer, first, gw, XT):
                def logits(g):
                    pe.wait_ge(S["tok_evac"], first + g + 1)
                    for i in range(4 * g, 4 * g + 4):
                        mm = pe.matmul(MISC[:, E * i:E * i + E], XT[:, P * i:P * i + P], gw, start=True, stop=True)
                    return mm
                for g in range(NT // 4):
                    pe.wait_ge(S["xn_ready"], layer * NT + 4 * g + 4)
                    if g >= 2:
                        pe.wait_ge(S["tok_evac"], first + g - 1)
                    for i in range(4):
                        mm = pe.transpose(RING[g % 2][:, P * i:P * i + P], XN[:, 4 * g + i, :], ident)
                    mm.then_inc(S["tok_T"], 1)
                    if layer == 0:
                        pe.wait_ge(S["xn2_ready"], 4 * g + 4)
                        if g >= 2:
                            pe.wait_ge(S["tok2_evac"], g - 1)
                        for i in range(4):
                            mm = pe.transpose(OBANK[g % 2][:, P * i:P * i + P], XN2[:, 4 * g + i, :], ident)
                        mm.then_inc(S["tok2_T"], 1)
                    if g:
                        logits(g - 1)
                logits(NT // 4 - 1).then_inc(S["logits_full"], 1)

            def ranks(layer, M1, M2):
                pe.wait_ge(S["mask_ready"], (1, 3)[layer])
                for k, M in enumerate((M1, M2)[:1 + layer]):
                    pe.matmul(SBANK[0][:, 256 * k:256 * k + 256], tri, M, start=True, stop=True)
                    mm = pe.matmul(SBANK[1][:, 256 * k:256 * k + 256], ones[:, :], M, start=True, stop=True)
                mm.then_inc(S["rank_full"], 1)

            pe.wait_ge(S["const_in"], 16)
            pe.wait_ge(S["ones_ready"], 1)
            pe.wait_ge(S["gate_in"], 48)
            gate_logits(0, 0, gw0, XNT)
            pe.wait_ge(S["nk_ready"], 1)
            pe.wait_ge(S["w_in"], 16 * 10)
            pe.wait_ge(S["tok2_evac"], NT // 4)
            pe.transpose(TRB[:, 0:2 * H], nkp, ident[0:2 * H, 0:2 * H])
            for c in range(HC):
                mm = pe.matmul(TRB[0:2 * H, P:2 * P], nvT[:, c], wo0[:, c], start=(c == 0), stop=(c == HC - 1))
            mm.then_inc(S["nk_full"], 1)
            for c in range(HC):
                mm = pe.transpose(OBANK[c // 4][:, P * (c % 4):P * (c % 4) + P], wqkv[:, P * c:P * c + P], ident)
            mm.then_inc(S["wqT_full"], 1)
            pe.wait_ge(S["nk_evac"], 1)
            pe.wait_ge(S["wqT_evac"], 1)
            for c in range(HC):
                mm = pe.matmul(TRB[:, 4 * c:4 * c + 4], OnT[:, c], nkT[:, 4 * c:4 * c + 4], start=True, stop=True)
            mm.then_inc(S["wn_full"], 1)
            ranks(0, M1_0, None)
            pe.wait_ge(S["tok2_evac"], NT // 4)

            def ring_in(use, bnk, b, p, more=2):
                n = ring_use(b, use, more)
                if not isinstance(n, int) or n >= 2:
                    pe.wait_ge(S["ring_evac"], n - 1)
                if use[0] == "unit":
                    t, k = UNITS[use[1]]
                    mm = pe.matmul(RING[bnk][:, :], xa[:, p, t * P:(t + 1) * P], wqkv[:, 512 * k:512 * k + 512],
                                   start=True, stop=True)
                elif use[0] == "qk":
                    t, k = use[1] // 4, use[1] % 4
                    pe.wait_ge(S["qn_done"], b * NQ + (use[1] + 1 + NQ))
                    for c in range(4):
                        mm = pe.transpose(RING[bnk][:, P * c:P * c + P], qkn[:, t, 512 * k + P * c:512 * k + P * c + P],
                                          ident)
                else:
                    pe.wait_ge(S["on_done"], b * 2 + (use[1] + 1))
                    for c in range(4):
                        mm = pe.transpose(RING[bnk][:, P * c:P * c + P],
                                          On[:, 512 * use[2] + P * c:512 * use[2] + P * c + P], ident)
                mm.then_inc(S["ring_full"], 1)

            def scores(p, g):
                t, heads = GROUPS[g]
                n = P * (t + 1)
                for k, h in enumerate(heads):
                    r = 64 * (h % 2)
                    mm = pe.matmul(SBANK[g % 2][:, n * k:n * k + n], qT[r:r + 64, p, h // 2, t * P:(t + 1) * P],
                                   kT[r:r + 64, p, h // 2, 0:n], start=True, stop=True)
                mm.then_inc(S["s_full"], 1)

            def null_scores(p):
                for t in range(2):
                    mm = pe.matmul(MISC[:, 32 * t:32 * t + 32], xa[:, p, t * P:(t + 1) * P], wn, start=True, stop=True)
                mm.then_inc(S["sn_full"], 1)

            def turn_p(b, g):
                pe.wait_ge(S["exp_done"], b * NG + (g + 1))
                for k in range(4):
                    mm = pe.transpose(TRB[:, P * k:P * k + P], Pb[:, g % 3, P * k:P * k + P], ident)
                mm.then_inc(S["pt_full"], 1)

            def weigh(b, p, g):
                t, heads = GROUPS[g]
                pe.wait_ge(S["pt_evac"], b * NG + (g + 1))
                for k, h in enumerate(heads):
                    for j in range(t + 1):
                        o = OBANK[h // 8][:, DH * (h % 8):DH * (h % 8) + DH]
                        mm = pe.matmul(o, PTb[:, g % 2, P * ((t + 1) * k + j):P * ((t + 1) * k + j) + P],
                                       Vt[:, p, j, DH * h:DH * h + DH], start=(h % 8 == 0 and j == 0), stop=(j == t),
                                       skip_group_check=True)
                if g in (3, NG - 1):
                    mm.then_inc(S["o_full"], 1)

            def turn_null(b, t):
                pe.wait_ge(S["pn_scaled"], b * 2 + (t + 1))
                pe.transpose(MISC[0:2 * H, 0:P], pns[:, 32 * t:32 * t + 32], ident).then_inc(S["pnT_full"], 1)

            def project(b, t, more):
                pe.wait_ge(S["pnT_evac"], b * 2 + (t + 1))
                pe.matmul(MISC[:, 0:D], pnT, nvw, start=True, stop=False)
                pe.wait_ge(S["ring_evac"], ring_use(b, ("out", t, 1), more) + 1)
                for c in range(HC):
                    mm = pe.matmul(MISC[:, 0:D], OnT[:, c], wo0[:, c], start=False, stop=(c == HC - 1))
                mm.then_inc(S["y_full"], 1)

            def step(b, p, i, more=2):
                def ring(g, part):
                    for use in ring_uses(g, part, more):
                        if use == ("unit", 0, 2):
                            pe.wait_ge(S[f"xa_in{p}"], (i + 2) * 16)
                        ring_in(use, ring_bank(use, more), b, (p + use[2]) % 2, more)
                for g in range(NG):
                    if g == NG - 3 and more:
                        pe.wait_ge(S["ring_evac"], ring_use(b, ("qk", NQ - 1, 1), more) + 1)
                        pe.wait_ge(S["y_evac"], b * 2 + 1)
                        null_scores(1 - p)
                    if g + 2 < NG or more:
                        pe.wait_ge(S["ttr_done"], b * NG + (g + 1))
                        if g + 2 < NG:
                            scores(p, g + 2)
                        else:
                            scores(1 - p, g + 2 - NG)
                    if g == 6:
                        turn_null(b, 0)
                    ring(g, 0)
                    if g == 7:
                        project(b, 0, more)
                    if g == 5:
                        pe.wait_ge(S["on_done"], b * 2 + 1)
                    if g:
                        weigh(b, p, g - 1)
                    ring(g, 1)
                    turn_p(b, g)
                ring(NG, 0)
                weigh(b, p, NG - 1)
                for use in ring_uses(NG, 1, more):
                    if use == ("out", 1, 0):
                        turn_null(b, 1)
                    ring_in(use, ring_bank(use, more), b, (p + use[2]) % 2, more)
                project(b, 1, more)

            pe.wait_ge(S["w_in"], 16 * 10)
            for use in RING_FIRST:
                if use == ("unit", 0, use[2]):
                    pe.wait_ge(S[f"xa_in{use[2]}"], 16)
                if use == ("unit", 8, 0):
                    pe.wait_ge(S["wn_evac"], 1)
                    pe.wait_ge(S["ring_evac"], ring_use(-1, ("qk", NQ - 1, 0)) + 1)
                    null_scores(0)
                    scores(0, 0)
                    scores(0, 1)
                ring_in(use, ring_bank(use, start=True), -1, use[2])
            with pe.Fori(0, (NB - 2) // 2) as i:
                step(i * 2, 0, i)
                step(i * 2 + 1, 1, i)
            for b in range(NB - 2, NB):
                step(b, b % 2, b // 2, more=NB - 1 - b)

            pe.wait_ge(S["y_evac"], 2 * NB)
            ffn_tensor(pe, NBLK0, 0, loads0)

            pe.wait_ge(S["gate1_in"], 16)
            pe.wait_ge(S["ye_evac"], NBLK0)
            gate_logits(1, NT // 4, gw1, XN1T)
            ranks(1, M1, M2)
            pe.wait_ge(S["l1w_in"], 16 * 7)

            QK, VB, SC, PT, OB = bank[0], bank[1], bank[4], bank[5], bank[6]

            def qkv1(b, p, n):
                pe.wait_ge(S[f"xa1_in{p}"], n)
                pe.matmul(QK[:, 0:N], wq1, xa1[:, p], start=True, stop=True)
                pe.matmul(QK[:, N:2 * N], wk1, xa1[:, p], start=True, stop=True)
                for t in range(2):
                    mm = pe.matmul(VB[:, t * D:(t + 1) * D], xa1[:, p, t * P:(t + 1) * P], wv1, start=True, stop=True)
                mm.then_inc(S["qkv1_full"], 1)

            def scores1(b, p):
                pe.wait_ge(S["qk1_evac"], b + 1)
                pe.matmul(SC[:, 0:P], qk1[:, p, 0:P], qk1[:, p, N:N + P], start=True, stop=True)
                pe.matmul(SC[:, P:P + N], qk1[:, p, P:N], qk1[:, p, N:2 * N], start=True, stop=True)\
                  .then_inc(S["s1_full"], 1)

            def weigh1(b, p):
                pe.wait_ge(S["exp1_done"], b + 1)
                for k in range(3):
                    mm = pe.transpose(PT[:, P * k:P * k + P], p1b[:, p, P * k:P * k + P], ident)
                mm.then_inc(S["pt1_full"], 1)
                pe.wait_ge(S["pt1_evac"], b + 1)
                for t, k, j in ((0, 0, 0), (1, 1, 0), (1, 2, 1)):
                    mm = pe.matmul(OB[:, t * D:(t + 1) * D], pt1[:, P * k:P * k + P],
                                   v1[:, p, j * D:(j + 1) * D], start=(j == 0), stop=(j == t))
                mm.then_inc(S["o1_full"], 1)

            def step1(b, p, i, more=2):
                if more >= 2:
                    pe.wait_ge(S["v1_evac"], b + 2)
                    pe.wait_ge(S["qk1_evac"], b + 2)
                    qkv1(b + 2, p, (i + 2) * 16)
                if more >= 1:
                    pe.wait_ge(S["ttr1_done"], b + 1)
                    scores1(b + 1, 1 - p)
                pe.wait_ge(S["v1_evac"], b + 1)
                weigh1(b, p)

            qkv1(0, 0, 16)
            pe.wait_ge(S["v1_evac"], 1)
            pe.wait_ge(S["qk1_evac"], 1)
            qkv1(1, 1, 16)
            scores1(0, 0)
            with pe.Fori(0, (NB - 2) // 2) as i:
                step1(i * 2, 0, i)
                step1(i * 2 + 1, 1, i)
            for b in range(NB - 2, NB):
                step1(b, b % 2, b // 2, more=NB - 1 - b)

            def fc(g):
                pe.wait_ge(S["ao_evac"], g + 1)
                if g >= 2:
                    pe.wait_ge(S["attn1_done"], g - 1)
                for i in range(4):
                    mm = pe.matmul(bank[6 + g % 2][:, P * i:P * i + P], XN1T[:, 512 * g + P * i:512 * g + P * i + P], wfc,
                                   start=True, stop=True)
                mm.then_inc(S["fc_full"], 1)
            pe.wait_ge(S["o1_done"], NB)
            for g in range(NT // 4):
                pe.wait_ge(S["ao_ready"], 4 * g + 4)
                if g >= 2:
                    pe.wait_ge(S["ao_evac"], g - 1)
                for i in range(4):
                    mm = pe.transpose(bank[4 + g % 2][:, P * i:P * i + P], AO[:, 4 * g + i, :], ident)
                mm.then_inc(S["ao_T"], 1)
                if g:
                    fc(g - 1)
            fc(NT // 4 - 1)
            pe.wait_ge(S["attn1_done"], NT // 4)
            ffn_tensor(pe, NBLK1, NBLK0, loads1)

        @block.scalar
        def _(act):
            for g in range(NT // 4):
                act.wait_ge(S["tok_T"], g + 1)
                act.activation(XNT[:, 512 * g:512 * g + 512], RING[g % 2][:, :], ACT.Copy).then_inc(S["tok_evac"], 1)

            def ring_out(use, n_use, bnk, p):
                act.wait_ge(S["ring_full"], n_use + 1)
                src = RING[bnk]
                kind, n = use[0], use[1]
                if kind == "unit":
                    t, k = UNITS[n]
                    dst = raw[:, t, 512 * k:512 * k + 512] if k < 4 else Vt[:, p, t, 512 * (k - 4):512 * (k - 3)]
                    ins = act.activation(dst, src[:, :], ACT.Copy)
                elif kind == "qk":
                    t, k = n // 4, n % 4
                    s4 = src[:, :].rearrange("p (c n) -> p c n", c=4)
                    if k < 2:
                        ins = act.activation(qT[:, p, 4 * k:4 * k + 4, t * P:(t + 1) * P], s4, ACT.Copy, scale=qscale)
                    else:
                        ins = act.activation(kT[:, p, 4 * (k - 2):4 * (k - 2) + 4, t * P:(t + 1) * P], s4, ACT.Copy)
                else:
                    n = use[2]
                    ins = act.activation(OnT[:, 4 * n:4 * n + 4], src[:, :].rearrange("p (c n) -> p c n", c=4), ACT.Copy)
                ins.then_inc(S["ring_evac"], 1)

            def probs(b, g):
                t, heads = GROUPS[g]
                n = P * (t + 1)
                act.wait_ge(S["ttr_done"], b * NG + (g + 1))
                for k, h in enumerate(heads):
                    ins = act.activation(Pb[:, g % 3, n * k:n * k + n], Sb[:, g % 3, n * k:n * k + n], ACT.Exp,
                                         bias=nm_t(t, h), scale=-1.0,
                                         accum_out=den_t(t, h))
                ins.then_inc(S["exp_done"], 1)

            def nm_t(t, h):
                return nm[:, 16 * t + h:16 * t + h + 1]

            def den_t(t, h):
                return den[:, 16 * t + h:16 * t + h + 1]

            def null_probs(b, t):
                act.wait_ge(S["nsub_done"], b * 2 + (t + 1))
                act.activation(pn[:, 32 * t:32 * t + 32], ntmp[:, 32 * t:32 * t + 32], ACT.Exp).then_inc(S["pn_done"], 1)

            def step(b, p, more=2):
                def ring(g):
                    for use in ring_uses(g, 0, more) + ring_uses(g, 1, more):
                        ring_out(use, ring_use(b, use, more), ring_bank(use, more), (p + use[2]) % 2)
                for g in range(NG):
                    probs(b, g)
                    if g == 3:
                        null_probs(b, 0)
                    if g == NG - 2:
                        null_probs(b, 1)
                    ring(g)
                ring(NG)

            act.wait_ge(S["wqT_full"], 1)
            for o in range(2):
                ins = act.activation(OnT[:, 4 * o:4 * o + 4], OBANK[o][:, :].rearrange("p (c n) -> p c n", c=4), ACT.Copy)
            ins.then_inc(S["wqT_evac"], 1)
            for use in RING_FIRST:
                if use == ("qk", 0, 0):
                    act.wait_ge(S["nk_ready"], 1)
                ring_out(use, ring_use(-1, use), ring_bank(use, start=True), use[2])
            pairs(act, 0, NB - 3, step)
            for b in range(NB - 2, NB):
                step(b, b % 2, more=NB - 1 - b)

            ffn_scalar(act, NBLK0, 0, loads0)

            def silu(q):
                act.wait_ge(S[f"gathered{q}"], 16 * 4)
                g = GA[:, 0, 4 * q:4 * q + 4, :]
                act.activation(g, g, ACT.Silu).then_inc(S["silu_done"], 1)
            for q in range(8):
                silu(q)

            for g in range(NT // 4):
                act.wait_ge(S["tok_T"], NT // 4 + g + 1)
                act.activation(XN1T[:, 512 * g:512 * g + 512], RING[g % 2][:, :], ACT.Copy).then_inc(S["tok_evac"], 1)
            act.wait_ge(S["gate_exp"], 1)
            act.activation(R1, R2, ACT.Exp).then_inc(S["wexp"], 1)

            def evac_qk1(b, p):
                act.wait_ge(S["qkv1_full"], b + 1)
                act.activation(qk1[:, p], bank[0][:, :], ACT.Copy).then_inc(S["qk1_evac"], 1)

            def exp1(b, p):
                act.wait_ge(S["ttr1_done"], b + 1)
                act.activation(p1b[:, p, 0:P], s1b[:, p, 0:P], ACT.Exp, bias=nm1[:, 2 * p:2 * p + 1], scale=-1.0,
                               accum_out=den1[:, 2 * p:2 * p + 1])
                act.activation(p1b[:, p, P:P + N], s1b[:, p, P:P + N], ACT.Exp, bias=nm1[:, 2 * p + 1:2 * p + 2], scale=-1.0,
                               accum_out=den1[:, 2 * p + 1:2 * p + 2]).then_inc(S["exp1_done"], 1)

            def step1(b, p, more=True):
                if more:
                    act.wait_ge(S["s1_full"], b + 1)
                    evac_qk1(b + 2, p)
                exp1(b, p)
            evac_qk1(0, 0)
            evac_qk1(1, 1)
            pairs(act, 0, NB - 3, step1)
            for b in range(NB - 2, NB):
                step1(b, b % 2, more=False)

            for g in range(NT // 4):
                act.wait_ge(S["ao_T"], g + 1)
                act.activation(XN1T[:, 512 * g:512 * g + 512], bank[4 + g % 2][:, :], ACT.Identity, bias=beta1,
                               scale=gamma1).then_inc(S["ao_evac"], 1)
            ffn_scalar(act, NBLK1, NBLK0, loads1)
            for q in range(8):
                act.wait_ge(S["gate_exp"], 2 + q)
                g = GA[:, 0, 4 * q:4 * q + 4, :]
                act.activation(g, g, ACT.Silu).then_inc(S["silu_done"], 1)

        @block.vector
        def _(v):
            link = Chain(v, S["dve_step"])
            for h in range(2):
                v.wait_ge(S[f"x_in{h}"], 16)
                i0, n = h * NT // 2, NT // 2
                layer_norm(v, link, RS_, XN, i0, n, S["xn_ready"])
                v.wait_ge(S["xn_ready"], i0 + n)
                layer_norm(v, link, XN, XN2, i0, n, S["xn2_ready"])
                v.wait_ge(S["gate_in"], 48)
                for g in range(h * 4, h * 4 + 4):
                    v.wait_ge(S["tok2_T"], g + 1)
                    v.tensor_scalar(RA[:, 512 * g:512 * g + 512], OBANK[g % 2][:, :], gamma0, None, ALU.mult)\
                     .then_inc(S["tok2_evac"], 1)
            v.wait_ge(S["w_in"], 16 * 10)
            R = 2 * H
            link(v.tensor_scalar(T1[:, 0:1], qscale, kscale, 8.0, ALU.mult, ALU.mult))
            link(v.tensor_copy(qscale, T1[:, 0:1]))
            link(v.tensor_tensor(LG0[0:R, 3000:3128], nkp, nkp, ALU.mult))
            link(v.tensor_reduce(VE[0:R, 0:1], LG0[0:R, 3000:3128], AX.X, ALU.add))
            link(v.tensor_scalar(VE[0:R, 0:1], VE[0:R, 0:1], 1e-24, None, ALU.max))
            rsqrt(v, link, RSTD[0:R, 0:1], VE[0:R, 0:1], T1[0:R, 0:1], T2[0:R, 0:1])
            v.tensor_scalar(nkp, nkp, RSTD[0:R, 0:1], None, ALU.mult).then_inc(S["nk_ready"], 1)
            v.wait_ge(S["nk_full"], 1)
            v.tensor_scalar(nkT, TRB[:, 0:R], qscale, None, ALU.mult)
            v.tensor_copy(nvw, TRB[0:R, P:2 * P]).then_inc(S["nk_evac"], 1)
            v.wait_ge(S["wn_full"], 1)
            v.tensor_copy(wn, TRB[:, 0:R]).then_inc(S["wn_evac"], 1)
            v.wait_ge(S["logits_full"], 1)
            link(v.tensor_tensor(mem0[0].rearrange("p (t e) -> p t e", e=E),
                                 MISC[:, 0:256].rearrange("p (t e) -> p t e", e=E),
                                 gateb.unsqueeze(1).to_broadcast([P, NT, E]), ALU.add))
            v.wait_ge(S["ones_ready"], 1)
            route(v, link, 0, mem0, M1_0, None)

            def sums(a_, i):
                t, k = UNITS[i]
                v.wait_ge(S["sq_done"], a_ * NQ + (i + 1))
                v.tensor_reduce(ss[:, t, 8 * k:8 * k + 8], sq[:, i % 2].rearrange("p (h d) -> p h d", d=DH),
                                AX.X, ALU.add).then_inc(S["ss_done"], 1)

            def seeds(a_):
                x, y, half = (m[:, :, :].rearrange("p t n -> p (t n)") for m in (ss, rn, xh))
                v.wait_ge(S["ss_done"], (a_ + 1) * NQ)
                v.tensor_scalar(x, x, 1e-24, None, ALU.max).then_inc(S["seed_step"], 1)
                v.wait_ge(S["seed_step"], a_ * 2 + 1)
                v.tensor_scalar(half, x, -0.5, None, ALU.mult)
                v.tensor_scalar(y.bitcast(I32), x.bitcast(I32), 1, None, ALU.logical_shift_right)\
                 .then_inc(S["seed_step"], 1)
                v.wait_ge(S["seed_step"], a_ * 2 + 2)
                v.tensor_scalar(y.bitcast(I32), y.bitcast(I32), -1.0, RSQRT_MAGIC,
                                ALU.mult, ALU.add).then_inc(S["seed_done"], 1)

            def null_scores(b):
                v.wait_ge(S["sn_full"], b + 1)
                v.wait_ge(S["newton"], b * 12 + 12)
                for t in range(2):
                    ins = v.tensor_tensor(snr[:, 32 * t:32 * t + 32].rearrange("p (h n) -> p h n", n=2),
                                          MISC[:, 32 * t:32 * t + 32].rearrange("p (h n) -> p h n", n=2),
                                          rn[:, t, 0:H].unsqueeze(2).to_broadcast([P, H, 2]), ALU.mult)
                ins.then_inc(S["sn_step"], 1)
                v.wait_ge(S["sn_step"], b * 3 + 1)
                v.scalar_tensor_tensor(out=nsn, in0=snr, scalar=-1.0, in1=nbias, op0=ALU.mult,
                                       op1=ALU.subtract).then_inc(S["sn_step"], 1)
                v.wait_ge(S["sn_step"], b * 3 + 2)
                v.tensor_reduce(nmn, nsn.rearrange("p (h n) -> p h n", n=2), AX.X, ALU.min).then_inc(S["sn_step"], 1)
                v.wait_ge(S["sn_step"], b * 3 + 3)

            def rows_max(b, g):
                t, heads = GROUPS[g]
                n = P * (t + 1)
                v.wait_ge(S["s_full"], b * NG + (g + 1))
                v.sem_inc(S["scores_seen"], 1)
                for k, h in enumerate(heads):
                    ins = v.tensor_tensor_reduce(out=Sb[:, g % 3, n * k:n * k + n], in0=SBANK[g % 2][:, n * k:n * k + n],
                                                 in1=alibi[:, h, N - n:N], scale=-1.0,
                                                 scalar=nmn[:, 16 * t + h:16 * t + h + 1], op0=ALU.add, op1=ALU.min,
                                                 accum_out=nm[:, 16 * t + h:16 * t + h + 1])
                ins.then_inc(S["ttr_done"], 1)

            def null_sub(b, t):
                v.wait_ge(S["ttr_done"], b * NG + (4 if t == 0 else NG))
                v.tensor_tensor(ntmp[:, 32 * t:32 * t + 32].rearrange("p (h n) -> p h n", n=2),
                                nm[:, 16 * t:16 * t + 16].unsqueeze(2).to_broadcast([P, H, 2]),
                                nsn[:, 32 * t:32 * t + 32].rearrange("p (h n) -> p h n", n=2),
                                ALU.subtract).then_inc(S["nsub_done"], 1)

            def denominators(b, t):
                v.wait_ge(S["pn_done"], b * 2 + (t + 1))
                d = rden[:, 16 * t:16 * t + 16]
                v.tensor_reduce(d, pn[:, 32 * t:32 * t + 32].rearrange("p (h n) -> p h n", n=2), AX.X, ALU.add)\
                 .then_inc(S["den_step"], 1)
                v.wait_ge(S["den_step"], b * 4 + (2 * t + 1))
                v.wait_ge(S["exp_done"], b * NG + (4 if t == 0 else NG))
                v.tensor_tensor(d, d, den[:, 16 * t:16 * t + 16], ALU.add).then_inc(S["den_step"], 1)
                v.wait_ge(S["den_step"], b * 4 + (2 * t + 2))
                v.reciprocal(d, d).then_inc(S["rd1_done"], 1)
                v.wait_ge(S["rd1_done"], b * 2 + (t + 1))
                v.tensor_tensor(pns[:, 32 * t:32 * t + 32].rearrange("p (h n) -> p h n", n=2),
                                pn[:, 32 * t:32 * t + 32].rearrange("p (h n) -> p h n", n=2),
                                d.unsqueeze(2).to_broadcast([P, H, 2]), ALU.mult).then_inc(S["pn_scaled"], 1)

            def null_turned(b, t):
                v.wait_ge(S["pnT_full"], b * 2 + (t + 1))
                v.tensor_copy(pnT, MISC[0:2 * H, 0:P]).then_inc(S["pnT_evac"], 1)

            def out_norm(b, t):
                v.wait_ge(S["o_full"], b * 2 + (t + 1))
                v.wait_ge(S["rd1_done"], b * 2 + (t + 1))
                for o in range(2):
                    ins = v.tensor_tensor(On[:, 512 * o:512 * o + 512].rearrange("p (h d) -> p h d", d=DH),
                                          OBANK[o][:, :].rearrange("p (h d) -> p h d", d=DH),
                                          rden[:, 16 * t + 8 * o:16 * t + 8 * o + 8].unsqueeze(2).to_broadcast([P, 8, DH]),
                                          ALU.mult)
                ins.then_inc(S["on_done"], 1)

            def y_out(b, t):
                v.wait_ge(S["y_full"], b * 2 + (t + 1))
                v.tensor_copy(RS_[:, bass.ds(b * 2 + t, 1), :].rearrange("p t d -> p (t d)"), MISC[:, 0:D])\
                 .then_inc(S["y_evac"], 1)

            def step(b, p, more=2):
                for g in range(NG):
                    if g == 5:
                        denominators(b, 0)
                        out_norm(b, 0)
                    if g == 8:
                        y_out(b, 0)
                    if g + 2 < NG:
                        rows_max(b, g + 2)
                    elif more:
                        if g + 2 == NG:
                            v.wait_ge(S["nsub_done"], b * 2 + 2)
                            null_scores(b + 1)
                        rows_max(b + 1, g + 2 - NG)
                    if g == 2:
                        null_sub(b, 0)
                    if g == NG - 3:
                        null_sub(b, 1)
                    if g == 6:
                        null_turned(b, 0)
                    if more == 2 and g in SUMS:
                        sums(b + 2, SUMS[g])
                    v.wait_ge(S["pt_full"], b * NG + (g + 1))
                    v.tensor_copy(PTb[:, g % 2, :], TRB[:, :]).then_inc(S["pt_evac"], 1)
                denominators(b, 1)
                out_norm(b, 1)
                if more == 2:
                    for i in (4, 5):
                        sums(b + 2, i)
                null_turned(b, 1)
                if more == 2:
                    for i in (6, 7):
                        sums(b + 2, i)
                    seeds(b + 2)
                y_out(b, 1)

            SUMS = {6: 0, 7: 1, 10: 2, 11: 3}
            for i in range(NQ):
                sums(0, i)
            seeds(0)
            null_scores(0)
            rows_max(0, 0)
            rows_max(0, 1)
            for i in range(NQ):
                sums(1, i)
            seeds(1)
            pairs(v, 0, NB - 3, step)
            for b in range(NB - 2, NB):
                step(b, b % 2, more=NB - 1 - b)

            ffn_vector(v, NBLK0, 0, loads0)

            v.wait_ge(S["y_evac"], 2 * NB)
            v.wait_ge(S["x_back"], 16)
            xr = RA[:, :].rearrange("p (t d) -> p t d", d=D)

            def combine(q, done):
                s = slice(4 * q, 4 * q + 4)
                v.wait_ge(S["silu_done"], done)
                link(v.tensor_tensor(RS_[:, s], RS_[:, s], GA[:, 0, s, :], ALU.mult))
                return v.tensor_tensor(xr[:, s], xr[:, s], RS_[:, s], ALU.add)
            for q in range(8):
                combine(q, q + 1).then_inc(S["x1_ready"], 1)
                if q % 4 == 3:
                    v.wait_ge(S["x1_ready"], q + 1)
                    layer_norm(v, link, xr, XN, (q // 4) * NT // 2, NT // 2, S["xn_ready"])

            v.wait_ge(S["logits_full"], 2)
            link(v.tensor_copy(LG, MISC[:, 0:256]))
            route(v, link, 1, mem1, M1, M2)

            def v_out(b, i3):
                v.wait_ge(S["qkv1_full"], b + 1)
                v.tensor_copy(v1[:, i3], bank[1][:, 0:N]).then_inc(S["v1_evac"], 1)

            SCL = float(D) ** -0.5

            def rows_max1(b, p):
                v.wait_ge(S["s1_full"], b + 1)
                v.sem_inc(S["scores_seen"], 1)
                v.tensor_tensor_reduce(out=s1b[:, p, 0:P], in0=bank[4][:, 0:P], in1=mask1[:, P:2 * P], scale=-SCL,
                                       scalar=-NEG, op0=ALU.add, op1=ALU.min, accum_out=nm1[:, 2 * p:2 * p + 1])
                v.tensor_tensor_reduce(out=s1b[:, p, P:P + N], in0=bank[4][:, P:P + N], in1=mask1[:, :], scale=-SCL,
                                       scalar=-NEG, op0=ALU.add, op1=ALU.min, accum_out=nm1[:, 2 * p + 1:2 * p + 2])\
                 .then_inc(S["ttr1_done"], 1)

            def residual(b, p, i3):
                v.wait_ge(S["exp1_done"], b + 1)
                v.reciprocal(rd1[:, 2 * p:2 * p + 2], den1[:, 2 * p:2 * p + 2]).then_inc(S["rd1_done"], 1)
                v.wait_ge(S["o1_full"], b + 1)
                v.wait_ge(S["rd1_done"], b + (2 * NB + 1))
                for t in range(2):
                    ins = v.scalar_tensor_tensor(out=AO[:, bass.ds(b * 2 + t, 1), :].rearrange("p t d -> p (t d)"),
                                                 in0=bank[6][:, t * D:(t + 1) * D], scalar=rd1[:, 2 * p + t:2 * p + t + 1],
                                                 in1=v1[:, i3, t * D:(t + 1) * D], op0=ALU.mult, op1=ALU.add)
                ins.then_inc(S["o1_done"], 1)

            def step1(b, p, more=2):
                if more >= 1:
                    rows_max1(b + 1, 1 - p)
                v.wait_ge(S["pt1_full"], b + 1)
                v.tensor_copy(pt1, bank[5][:, 0:384]).then_inc(S["pt1_evac"], 1)
                residual(b, p, p)
                if more >= 2:
                    v.wait_ge(S["o1_done"], b + 1)
                    v_out(b + 2, p)
            v_out(0, 0)
            v_out(1, 1)
            rows_max1(0, 0)
            pairs(v, 0, NB - 3, step1)
            for b in range(NB - 2, NB):
                step1(b, b % 2, more=NB - 1 - b)
            v.wait_ge(S["o1_done"], NB)
            for h in range(2):
                layer_norm(v, link, AO, AO, h * NT // 2, NT // 2, S["ao_ready"])
            for g in range(NT // 4):
                v.wait_ge(S["fc_full"], g + 1)
                v.tensor_tensor(RS_[:, 4 * g:4 * g + 4, :], bank[6 + g % 2][:, :].rearrange("p (t d) -> p t d", d=D),
                                bfc.unsqueeze(1).to_broadcast([P, 4, D]), ALU.add).then_inc(S["attn1_done"], 1)

            ffn_vector(v, NBLK1, NBLK0, loads1)

            for q in range(8):
                v.wait_ge(S[f"gathered{q}"], 16 * 4 * 3)
                for i in range(4 * q, 4 * q + 4):
                    ins = v.tensor_scalar(GA[:, 0, i], GA[:, 0, i], G1W[:, i:i + 1], None, ALU.mult)
                link(ins)
                for i in range(4 * q, 4 * q + 4):
                    ins = v.scalar_tensor_tensor(out=GA[:, 0, i], in0=GA[:, 1, i], scalar=G2W[:, i:i + 1],
                                                 in1=GA[:, 0, i], op0=ALU.mult, op1=ALU.add)
                ins.then_inc(S["gate_exp"], 1)
            v.wait_ge(S["attn1_done"], NT // 4)
            for q in range(8):
                combine(q, 8 + q + 1).then_inc(S["out_ready"], 1)


def constants(np):
    c = np.zeros((P, C_END), np.float32)
    p = np.arange(P)
    c[:, C_ID:C_ID + P] = np.eye(P)
    c[:, C_TRI:C_TRI + P] = p[:, None] < p[None, :]
    start = 2.0 ** (-2.0 ** (-(np.log2(H) - 3.0)))
    slopes = np.array([start * start ** i for i in range(H)], np.float32)
    for t in range(2):
        for h in range(H):
            for n in range(NNULL):
                c[:, C_NB + 32 * t + 2 * h + n] = -(t * P + p + NNULL - n) * slopes[h]
    diag = np.where(p[None, :] > p[:, None], NEG, 0.0)
    c[:, C_M1 + P:C_M1 + 2 * P] = diag
    c[:, C_W8:C_W8 + E] = E - np.arange(E)
    c[:, C_RS:C_RS + E * NT] = np.arange(E * NT) % NT != 0
    c[:, C_THR:C_THR + NTHR] = BLK * np.arange(NTHR)
    c[:, C_JJ:C_JJ + NBLK1 + 1] = np.arange(NBLK1 + 1)
    alibi = np.zeros((P, H, N), np.float32)
    dist = (p[:, None] - p[None, :]).astype(np.float32)
    for h in range(H):
        alibi[:, h, 0:P] = -(dist + P) * slopes[h]
        alibi[:, h, P:N] = np.where(dist < 0, np.float32(NEG), -dist * slopes[h])
    return c, alibi


_INS = ['L0_attn_x', 'L0_attn_gamma', 'L0_attn_w_q', 'L0_attn_w_kv', 'L0_attn_q_scale', 'L0_attn_k_scale',
        'L0_attn_w_out', 'L0_ffn_gate_W', 'L0_ffn_gate_b', 'L1_attn_Wq', 'L1_attn_Wk', 'L1_attn_Wv', 'L1_attn_Wfc',
        'L1_attn_bfc', 'L1_attn_gamma', 'L1_attn_beta', 'L1_ffn_Wg']


def kernel(**inputs):
    import numpy as np
    import concourse.bacc as _bacc
    from concourse import mybir as _mybir
    from concourse.bass_utils import run_bass_kernel_spmd as _run

    given = {n: np.ascontiguousarray(inputs[n]) for n in _INS}
    nkv = np.asarray(inputs['L0_attn_null_kv']).reshape(H, NNULL, 2, DH)
    nkp = np.zeros((2 * H, P), np.float32)
    nvT = np.zeros((P, HC, 2 * H), np.float32)
    for h in range(H):
        half = slice(DH * (h % 2), DH * (h % 2) + DH)
        nkp[2 * h:2 * h + 2, half] = nkv[h, :, 0]
        nvT[half, h // 2, 2 * h:2 * h + 2] = nkv[h, :, 1].T
    given["nkp"], given["nvT"] = nkp, nvT
    for l in range(2):
        w2 = np.asarray(inputs[f'L{l}_ffn_W2']).reshape(E, FC, P, D).transpose(0, 2, 1, 3).reshape(E, P, DFF)
        b1 = np.asarray(inputs[f'L{l}_ffn_b1']).reshape(E, FC, P).transpose(0, 2, 1)
        given[f"wp_{l}"] = np.ascontiguousarray(np.concatenate([np.asarray(inputs[f'L{l}_ffn_W1']), w2, b1], axis=2))
        given[f"b2_{l}"] = np.ascontiguousarray(inputs[f'L{l}_ffn_b2'])
    given["const"], given["alibi"] = constants(np)

    nc = _bacc.Bacc("TRN2", target_bir_lowering=False, num_devices=1)
    arrays, a = {}, {}
    for name, x in given.items():
        arrays[f"in_{name}"] = x
        a[name] = nc.dram_tensor(f"in_{name}", x.shape, _mybir.dt.from_np(x.dtype), kind="ExternalInput").ap()
    a["out"] = nc.dram_tensor("out_0", (NB, N, D), _mybir.dt.float32, kind="ExternalOutput").ap()
    block_kernel(nc, a)
    r = _run(nc, [arrays], core_ids=[0])
    return r.results[0]["out_0"]
```

```python
import concourse.bass as bass
from concourse import mybir
from contextlib import ExitStack

F32, I32 = mybir.dt.float32, mybir.dt.int32
ACT, ALU, AX = mybir.ActivationFunctionType, mybir.AluOpType, mybir.AxisListType

NB, N, D = 16, 256, 128
P = 128
T = NB * N
NT = T // P
H, DH = 16, 64
HC = H // 2
NNULL = 2
E, DFF = 8, 512
FC = DFF // P
BLK = 256
CAP = 2 * 2 * T // E
NBLK0 = (T + E * (BLK - 1)) // BLK
NBLK1 = (2 * T + E * (BLK - 1)) // BLK
NBUF = 4
WCOLS = 2 * DFF + FC
EPS = 1e-5
NEG = -1e30
BIG = float(1 << 20)
RSQRT_MAGIC = float(0x5F3759DF)
NTHR = T // BLK

C_ID, C_TRI, C_NB, C_M1, C_W8, C_RS, C_THR, C_JJ = 0, 128, 256, 320, 576, 584, 840, 856
C_END = C_JJ + (NBLK1 + 1)

GROUPS = [(0, [8 * (g // 2) + g % 2 + 2 * k for k in range(4)]) for g in range(4)] + \
         [(1, [4 * (g // 2) + g % 2 + 2 * k for k in range(2)]) for g in range(8)]
NG = len(GROUPS)
NU, NQ = 12, 8


RING_USES = {
    0: ([("unit", 10, 1)], []), 2: ([("unit", 11, 1)], []),
    4: ([("qk", 0, 1), ("qk", 1, 1)], [("unit", 0, 2)]),
    5: ([("qk", 2, 1), ("qk", 3, 1)], [("unit", 1, 2)]),
    6: ([("qk", 4, 1), ("qk", 5, 1)], [("out", 0, 0), ("out", 0, 1)]),
    7: ([("qk", 6, 1), ("qk", 7, 1)], []),
    8: ([("unit", 2, 2)], []), 9: ([("unit", 3, 2)], []), 10: ([("unit", 4, 2)], []), 11: ([("unit", 5, 2)], []),
    NG: ([("unit", 6, 2)], [("unit", 7, 2), ("unit", 8, 2), ("out", 1, 0), ("out", 1, 1), ("unit", 9, 2)])}


def ring_uses(g, part, more):
    return [u for u in RING_USES.get(g, ([], []))[part] if u[0] == "out" or u[2] <= more]


def ring_order(more):
    return [u for g in range(NG + 1) for part in (0, 1) for u in ring_uses(g, part, more)]


RING_FIRST = [("unit", u, 0) for u in range(8)] + [("qk", s, 0) for s in range(8)] + \
             [("unit", u, 1) for u in range(8)] + [("unit", u, 0) for u in range(8, 12)] + \
             [("unit", u, 1) for u in (8, 9)]
RING_START = len(RING_FIRST)
RING_STEP = len(ring_order(2))
UNITS = [(0, 0), (0, 1), (0, 2), (0, 3), (1, 0), (1, 1), (1, 2), (1, 3), (0, 4), (0, 5), (1, 4), (1, 5)]


def block_kernel(nc, a):
    xe = nc.dram_tensor("expert_rows", (NBLK1 * BLK, D), F32).ap()
    ye = nc.dram_tensor("expert_out", (NBLK1 * BLK, D), F32).ap()
    x_v = a["L0_attn_x"].rearrange("b (t p) d -> p (b t) d", p=P)
    out_v = a["out"].rearrange("b (t p) d -> p (b t) d", p=P)

    ctx = ExitStack()
    with ctx:
        def sb(name, shape, dt=F32):
            return ctx.enter_context(nc.sbuf_tensor(name, shape, dt))

        def sem(name):
            return ctx.enter_context(nc.semaphore(name))

        bank = [ctx.enter_context(nc.psum_tensor(f"bank{i}", [P, 512], F32)) for i in range(8)]
        RING, SBANK, OBANK, MISC, TRB = bank[0:2], bank[2:4], bank[4:6], bank[6], bank[7]

        const = sb("const", [P, C_END])
        ident, tri = const[:, C_ID:C_ID + P], const[:, C_TRI:C_TRI + P]
        nbias = const[:, C_NB:C_NB + 64]
        mask1 = const[:, C_M1:C_M1 + 256]
        ones = sb("ones", [P, P])
        XN = sb("XN", [P, NT, D])
        RA = sb("RA", [P, NT * D])
        RS_ = sb("RS_", [P, NT, D])
        small = sb("small", [P, 640])
        qscale, gamma0, gamma1, beta1 = (small[:, i:i + 1] for i in range(4))
        kscale = small[:, 4:5]
        gateb = small[:, 8:16]
        wn = small[:, 16:48]
        bfc = small[:, 48:176]
        MV = small[:, 176:240].rearrange("p (n s) -> p n s", s=2)
        VE, RSTD, T1, T2 = (small[:, 240 + 32 * i:272 + 32 * i] for i in range(4))
        G1W, G2W = small[:, 368:400], small[:, 400:432]
        ST6 = small[:, 432:624].rearrange("p (n s) -> p n s", s=6)
        gw1, gw0 = small[:, 624:632], small[:, 632:640]
        slots = sb("slots", [P, 2, NT], I32)
        owner = sb("owner", [1, NBLK1 + 1], I32)

        ARENA = 39000
        arena = sb("arena", [P, ARENA])
        at = [0]

        def take(n, rows=P):
            at[0] += n
            assert at[0] <= ARENA, at[0]
            return arena[0:rows, at[0] - n:at[0]]

        raw = take(2 * 4 * 512).rearrange("p (t n) -> p t n", t=2)
        qkn = take(2 * 4 * 512).rearrange("p (t n) -> p t n", t=2)
        sq = take(2 * 512).rearrange("p (i n) -> p i n", i=2)
        ffn_room = at[0]
        qT = take(2 * HC * N).rearrange("p (i c n) -> p i c n", i=2, c=HC)
        kT = take(2 * HC * N).rearrange("p (i c n) -> p i c n", i=2, c=HC)
        Vt = take(2 * 2 * H * DH).rearrange("p (i t n) -> p i t n", i=2, t=2)
        alibi = take(H * N).rearrange("p (h n) -> p h n", h=H)
        wqkv = take(3 * H * DH)
        wo0 = take(HC * D).rearrange("p (c n) -> p c n", c=HC)
        nvT = take(HC * 2 * H).rearrange("p (c n) -> p c n", c=HC)
        nvw = take(D, 2 * H)
        Sb = take(3 * 512).rearrange("p (i n) -> p i n", i=3)
        Pb = take(3 * 512).rearrange("p (i n) -> p i n", i=3)
        PTb = take(2 * 512).rearrange("p (i n) -> p i n", i=2)
        On = take(H * DH)
        OnT = take(H * DH).rearrange("p (c n) -> p c n", c=HC)
        xa = take(2 * N).rearrange("p (i n) -> p i n", i=2)
        ss = take(64).rearrange("p (t n) -> p t n", t=2)
        rn = take(64).rearrange("p (t n) -> p t n", t=2)
        nw1, nw2, c15 = take(64), take(64), take(64)
        xh = take(64).rearrange("p (t n) -> p t n", t=2)
        nkT = take(2 * H)
        snr = take(64)
        nsn = take(64)
        nmn = take(32)
        nm = take(32)
        den = take(32)
        ntmp = take(64)
        pn = take(64)
        pns = take(64)
        rden = take(32)
        pnT = take(P, 2 * H)
        nkp = take(P, 2 * H)
        XN2 = qT[:, :, :, :].rearrange("p i c n -> p (i c n)").rearrange("p (t n) -> p t n", t=NT)
        XNT = kT[:, :, :, :].rearrange("p i c n -> p (i c n)")
        zeros = PTb[:, 0, :]

        at[0] = 0
        wb = take(NBUF * WCOLS).rearrange("p (i n) -> p i n", i=NBUF)
        b2b = take(NBUF * D).rearrange("p (i n) -> p i n", i=NBUF)
        xb = take(NBUF * 2 * D).rearrange("p (i t n) -> p i t n", i=NBUF, t=2)
        xbT = take(2 * BLK).rearrange("p (i n) -> p i n", i=2)
        hT = take(2 * FC * BLK).rearrange("p (i n) -> p i n", i=2)
        yb = take(2 * 2 * D).rearrange("p (i n) -> p i n", i=2)
        assert at[0] <= ffn_room
        GA = take(2 * NT * D).rearrange("p (k t n) -> p k t n", k=2, t=NT)
        XN1T = take(NT * D)
        AO = take(NT * D).rearrange("p (t n) -> p t n", t=NT)
        wq1, wk1, wv1, wfc = (take(D) for _ in range(4))
        xa1 = take(2 * N).rearrange("p (i n) -> p i n", i=2)
        qk1 = take(2 * 2 * N).rearrange("p (i n) -> p i n", i=2)
        v1 = take(2 * N).rearrange("p (i n) -> p i n", i=2)
        s1b = take(2 * 384).rearrange("p (i n) -> p i n", i=2)
        p1b = take(2 * 384).rearrange("p (i n) -> p i n", i=2)
        pt1 = take(384)
        nm1, den1, rd1 = (take(4) for _ in range(3))
        LG, EQ, M1, M2, R1, R2 = (take(256) for _ in range(6))
        TOT, INC = take(512), take(512)
        MX, KM, MX2, PZ, KEPT1, KEPT2 = (take(32) for _ in range(6))
        CNT = take(64)
        CMP = take(320)
        LG0 = RS_[:, :, :].rearrange("p t d -> p (t d)")[:, 1024:]

        S = {n: sem(n) for n in (
            "const_in", "x_in0", "x_in1", "gate_in", "w_in", "zero_done", "xe_zero", "ones_ready", "c15_ready",
            "dve_step", "stats_ready", "xn_ready", "xn2_ready", "xn2b_ready", "tok_T", "tok_evac", "tok2_T", "tok2_evac",
            "logits_full",
            "mask_ready", "rank_full", "rank_evac", "owner_ready", "slots_ready", "scattered",
            *[f"gathered{q}" for q in range(8)], "gate_exp", "wexp",
            "scale_ready", "nk_ready", "nk_full", "nk_evac", "wqT_full", "wqT_evac", "wn_full", "wn_evac",
            "xa_in0", "xa_in1", "ring_full", "ring_evac", "sq_done", "ss_done", "seed_step", "seed_done", "newton",
            "qn_done",
            "sn_full", "sn_step", "s_full", "scores_seen", "ttr_done", "exp_done", "nsub_done", "pn_done", "den_step",
            "rd1_done", "pn_scaled", "pt_full", "pt_evac", "pnT_full", "pnT_evac", "o_full", "on_done", "y_full",
            "y_evac",
            *[f"rows_in{q}" for q in range(NBUF)], *[f"w_in{q}" for q in range(NBUF)], "xT_full", "xT_evac", "h_full",
            "gelu_done", "ye_full", "ye_evac", "stored0", "stored1",
            "silu_done", "gated", "x_back", "x1_ready", "out_ready", "out_done",
            "gate1_in", "l1w_in", "xa1_in0", "xa1_in1", "qkv1_full", "qk1_evac", "v1_evac", "s1_full", "ttr1_done",
            "exp1_done", "pt1_full", "pt1_evac", "o1_full", "o1_done", "ao_ready", "ao_T", "ao_evac", "fc_full",
            "attn1_done")}

        class Chain:
            def __init__(self, eng, s):
                self.eng, self.s, self.n = eng, s, 0

            def __call__(self, ins):
                ins.then_inc(self.s, 1)
                self.n += 1
                self.eng.wait_ge(self.s, self.n)

        def ring_use(b, use, more=2):
            if isinstance(b, int) and b == -1:
                return RING_FIRST.index(use)
            base = b * RING_STEP + RING_START
            if more == 0:
                base = RING_START + (NB - 2) * RING_STEP + len(ring_order(1))
            return base + ring_order(more).index(use)

        def ring_bank(use, more=2, start=False):
            if start:
                return RING_FIRST.index(use) % 2
            return ring_use(0, use, more) % 2

        def pairs(eng, first, last, body):
            n = (last - first + 1) // 2
            if n > 0:
                with eng.Fori(0, n) as i:
                    body(i * 2 + first, first % 2)
                    body(i * 2 + (first + 1), (first + 1) % 2)
            if (last - first + 1) % 2:
                body(last, last % 2)

        def rsqrt(eng, link, out, x, t1, t2):
            link(eng.tensor_scalar(t1.bitcast(I32), x.bitcast(I32), 1, None, ALU.logical_shift_right))
            link(eng.tensor_scalar(out.bitcast(I32), t1.bitcast(I32), -1.0, RSQRT_MAGIC, ALU.mult, ALU.add))
            for _ in range(3):
                link(eng.tensor_tensor(t1, out, out, ALU.mult))
                link(eng.tensor_tensor(t2, t1, x, ALU.mult))
                link(eng.tensor_scalar(t1, t2, -0.5, 1.5, ALU.mult, ALU.add))
                link(eng.tensor_tensor(out, out, t1, ALU.mult))

        NMR = VE

        def norm_stats(v, link, src, i0, n):
            for i in range(i0, i0 + n):
                ins = v.bn_stats(ST6[:, i], src[:, i])
            link(ins)
            for i in range(i0, i0 + n):
                ins = v.bn_aggr(MV[:, i], ST6[:, i])
            link(ins)
            s = slice(i0, i0 + n)
            link(v.tensor_scalar(VE[:, s], MV[:, s, 1], EPS, None, ALU.add))
            rsqrt(v, link, RSTD[:, s], VE[:, s], T1[:, s], T2[:, s])
            v.scalar_tensor_tensor(out=NMR[:, s], in0=MV[:, s, 0], scalar=-1.0, in1=RSTD[:, s], op0=ALU.mult,
                                   op1=ALU.mult).then_inc(S["stats_ready"], 1)

        def normalise_tiles(act, src, dst, i0, n, stats, done):
            act.wait_ge(S["stats_ready"], stats)
            for i in range(i0, i0 + n):
                act.activation(dst[:, i], src[:, i], ACT.Identity, bias=NMR[:, i:i + 1], scale=RSTD[:, i:i + 1])\
                   .then_inc(done, 1)

        te = lambda x: x.rearrange("p (t e) -> p t e", e=E)
        et = lambda x: x.rearrange("p (e t) -> p e t", e=E)
        cc = lambda lo, n: const[:, lo:lo + n]

        def masks(v, link, layer, mem, M1, M2):
            LG, EQ, R1, R2, TOT, INC, MX, KM, MX2, PZ, CNT, CMP = mem
            w8 = cc(C_W8, E).unsqueeze(1).to_broadcast([P, NT, E])
            up = lambda x: x.unsqueeze(2).to_broadcast([P, NT, E])

            def first_max(M, lg, mx):
                link(v.tensor_reduce(mx, te(lg), AX.X, ALU.max))
                link(v.tensor_tensor(te(EQ), te(lg), up(mx), ALU.is_equal))
                link(v.tensor_tensor(te(EQ), te(EQ), w8, ALU.mult))
                link(v.tensor_reduce(KM, te(EQ), AX.X, ALU.max))
                v.tensor_tensor(te(M), te(EQ), up(KM), ALU.is_equal).then_inc(S["mask_ready"], 1)

            first_max(M1, LG, MX)
            if layer:
                v.wait_ge(S["mask_ready"], 2)
                link(v.scalar_tensor_tensor(out=R2, in0=M1, scalar=3.0 * NEG, in1=LG, op0=ALU.mult, op1=ALU.add))
                first_max(M2, R2, MX2)

        def totals(v, link, layer, mem, keep=None):
            TOT = mem[4]
            v.wait_ge(S["rank_full"], layer + 1)
            if keep is not None:
                v.tensor_copy(keep, SBANK[0][:, 0:256])
            for k in range(1 + layer):
                ins = v.tensor_copy(et(TOT[:, 256 * k:256 * k + 256]),
                                    te(SBANK[1][:, 256 * k:256 * k + 256]).rearrange("p t e -> p e t"))
            ins.then_inc(S["rank_evac"], 1)
            v.wait_ge(S["rank_evac"], layer + 1)

        def counts(v, link, layer, mem):
            LG, EQ, R1, R2, TOT, INC, MX, KM, MX2, PZ, CNT, CMP = mem
            for k in range(1 + layer):
                tot, inc = TOT[:, 256 * k:256 * k + 256], INC[:, 256 * k:256 * k + 256]
                link(v.tensor_tensor_scan(inc, cc(C_RS, 256), tot, 0.0, ALU.mult, ALU.add))
                link(v.tensor_copy(CNT[:, 8 * k:8 * k + 8], et(inc)[:, :, NT - 1]))
                link(v.tensor_tensor(inc, inc, tot, ALU.subtract))
            if layer:
                inc, cnt = INC[:, 256:512], CNT[:, 16:24]
                link(v.tensor_tensor(et(inc), et(inc), CNT[:, 0:8].unsqueeze(2).to_broadcast([P, E, NT]), ALU.add))
                link(v.tensor_tensor(cnt, CNT[:, 0:8], CNT[:, 8:16], ALU.add))
                link(v.tensor_scalar(cnt, cnt, float(CAP), None, ALU.min))

        def blocks(v, link, layer, mem):
            CNT, CMP = mem[10:12]
            cnt = CNT[:, 16:24] if layer else CNT[:, 0:8]
            nblk, bend, bst = CNT[:, 24:32], CNT[:, 32:40], CNT[:, 40:48]
            cm = CMP[:, 0:E * NTHR].rearrange("p (e k) -> p e k", e=E)
            link(v.tensor_tensor(cm, cnt.unsqueeze(2).to_broadcast([P, E, NTHR]),
                                 cc(C_THR, NTHR).unsqueeze(1).to_broadcast([P, E, NTHR]), ALU.is_gt))
            link(v.tensor_reduce(nblk, cm, AX.X, ALU.add))
            link(v.tensor_tensor_scan(bend, ones[:, 0:E], nblk, 0.0, ALU.mult, ALU.add))
            link(v.tensor_tensor(bst, bend, nblk, ALU.subtract))
            link(v.tensor_scalar(bst, bst, float(BLK), None, ALU.mult))

        def owners(v, link, layer, mem):
            EQ, CNT, CMP = mem[1], mem[10], mem[11]
            nj = NBLK1 + 1
            cj = CMP[0:1, 0:nj * E].rearrange("p (j e) -> p j e", e=E)
            link(v.tensor_tensor(cj, const[0:1, C_JJ:C_JJ + nj].unsqueeze(2).to_broadcast([1, nj, E]),
                                 CNT[0:1, 32:40].unsqueeze(1).to_broadcast([1, nj, E]), ALU.is_ge))
            link(v.tensor_reduce(EQ[0:1, 0:nj], cj, AX.X, ALU.add))
            link(v.tensor_scalar(EQ[0:1, 0:nj], EQ[0:1, 0:nj], float(E - 1), None, ALU.min))
            v.tensor_copy(owner[:, :], EQ[0:1, 0:nj]).then_inc(S["owner_ready"], 1)
            v.wait_ge(S["owner_ready"], layer + 1)

        def rows(v, link, layer, mem, M1, M2, before):
            LG, EQ, R1, R2, TOT, INC, MX, KM, MX2, PZ, CNT, CMP = mem
            for k in range(1 + layer):
                M = (M1, M2)[k]
                inc = INC[:, 256 * k:256 * k + 256]
                link(v.tensor_tensor(te(R1), te(before[:, 256 * k:256 * k + 256]),
                                     et(inc).rearrange("p e t -> p t e"), ALU.add))
                link(v.tensor_tensor(EQ, R1, M, ALU.mult))
                link(v.tensor_reduce(PZ, te(EQ), AX.X, ALU.add))
                link(v.tensor_tensor(te(EQ), te(M), CNT[:, 40:48].unsqueeze(1).to_broadcast([P, NT, E]), ALU.mult))
                link(v.tensor_reduce(KM, te(EQ), AX.X, ALU.add))
                link(v.tensor_tensor(KM, KM, PZ, ALU.add))
                if layer:
                    kept = (KEPT1, KEPT2)[k]
                    link(v.tensor_scalar(kept, PZ, float(CAP), None, ALU.is_lt))
                    link(v.tensor_scalar(MX2, kept, -BIG, BIG, ALU.mult, ALU.add))
                    link(v.tensor_tensor(KM, KM, MX2, ALU.add))
                v.tensor_copy(slots[:, k, :], KM).then_inc(S["slots_ready"], 1)

        def gates(v, link, mem, M1, M2):
            LG, EQ, R1, R2, TOT, INC, MX, KM, MX2, PZ, CNT, CMP = mem
            up = lambda x: x.unsqueeze(2).to_broadcast([P, NT, E])
            v.wait_ge(S["slots_ready"], 3)
            v.tensor_tensor(te(R2), te(LG), up(MX), ALU.subtract).then_inc(S["gate_exp"], 1)
            v.wait_ge(S["wexp"], 1)
            link(v.tensor_reduce(PZ, te(R1), AX.X, ALU.add))
            link(v.reciprocal(KM, PZ))
            link(v.tensor_tensor(te(R1), te(R1), up(KM), ALU.mult))
            for W, M in ((G1W, M1), (G2W, M2)):
                link(v.tensor_tensor(EQ, R1, M, ALU.mult))
                link(v.tensor_reduce(W, te(EQ), AX.X, ALU.add))
            link(v.scalar_tensor_tensor(out=PZ, in0=G1W, scalar=1e-9, in1=G2W, op0=ALU.add, op1=ALU.add))
            link(v.reciprocal(KM, PZ))
            for W, kept in ((G1W, KEPT1), (G2W, KEPT2)):
                link(v.tensor_tensor(W, W, KM, ALU.mult))
                link(v.tensor_tensor(W, W, kept, ALU.mult))

        def scatter_rows(pool, layer, tiles=range(NT)):
            for k in range(1 + layer):
                pool.wait_ge(S["slots_ready"], 1 + layer + k)
                for i in tiles:
                    pool.indirect_dma_start(
                        xe[:, :], bass.IndirectOffsetOnAxis(ap=slots[:, k, i:i + 1], axis=0), XN[:, i, :], None,
                        bounds_check=NBLK1 * BLK - 1, oob_is_err=False).then_inc(S["scattered"], 16)

        def gather_rows(pool, layer):
            rows = (NBLK0, NBLK1)[layer] * BLK
            for i in range(NT):
                for k in range(1 + layer):
                    pool.indirect_dma_start(
                        (GA[:, k, i, :] if layer else XN[:, i, :]), None, ye[0:rows, :],
                        bass.IndirectOffsetOnAxis(ap=slots[:, k, i:i + 1], axis=0),
                        bounds_check=rows - 1, oob_is_err=False).then_inc(S[f"gathered{i // 4}"], 16)

        def quads(eng, first, last, body):
            n = (last - first + 1) // NBUF
            if n > 0:
                with eng.Fori(0, n) as i:
                    for q in range(NBUF):
                        body(i * NBUF + (first + q), q, i + first // NBUF)
            for j in range(first + n * NBUF, last + 1):
                body(j, j % NBUF, j // NBUF)

        def ffn_sync(sp, layer, nblk, base, scattered):
            W, B2 = a[f"wp_{layer}"], a[f"b2_{layer}"]

            def load_rows(j, q):
                src = xe[bass.ds(j * BLK, BLK), :].rearrange("(t p) d -> p t d", p=P)
                sp.dma_start(xb[:, q], src).then_inc(S[f"rows_in{q}"], 16)

            def load_weights(j, q):
                e = sp.value_load(owner[0:1, bass.ds(j, 1)], min_val=0, max_val=E - 1)
                sp.dma_start(wb[:, q], W[bass.ds(e, 1)].rearrange("e p n -> p (e n)")).then_inc(S[f"w_in{q}"], 16)
                sp.dma_start(b2b[:, q], B2[bass.ds(e, 1)].to_broadcast([P, D])).then_inc(S[f"w_in{q}"], 16)

            def step(j, q, more=True):
                p = q % 2
                if more:
                    sp.wait_ge(S["xT_full"], j + (base + 1))
                    load_rows(j + NBUF, q)
                sp.wait_ge(S["ye_evac"], j + (base + 1))
                if more:
                    load_weights(j + NBUF, q)
                dst = ye[bass.ds(j * BLK, BLK), :].rearrange("(t p) d -> p t d", p=P)
                sp.dma_start(dst, yb[:, p].rearrange("p (t d) -> p t d", t=2)).then_inc(S[f"stored{p}"], 16)

            sp.wait_ge(S["owner_ready"], layer + 1)
            for j in range(NBUF):
                load_weights(j, j)
            sp.wait_ge(S["scattered"], scattered)
            for j in range(NBUF):
                load_rows(j, j)
            m = (nblk - NBUF) // NBUF * NBUF
            quads(sp, 0, m - 1, lambda j, q, i: step(j, q))
            for j in range(m, nblk):
                step(j, j % NBUF, more=j + NBUF < nblk)

        def ffn_tensor(pe, nblk, base, counts):
            XT, HB, YB = bank[0:2], bank[2:6], bank[6:8]

            def turn(j, q, i):
                pe.wait_ge(S[f"rows_in{q}"], (i + (counts[q] + 1)) * 16)
                for t in range(2):
                    mm = pe.transpose(XT[q % 2][:, t * P:(t + 1) * P], xb[:, q, t, :], ident)
                mm.then_inc(S["xT_full"], 1)

            def up(j, q, i):
                pe.wait_ge(S["xT_evac"], j + (base + 1))
                pe.wait_ge(S[f"w_in{q}"], (i + (counts[q] + 1)) * 32)
                for c in range(FC):
                    mm = pe.matmul(HB[2 * (q % 2) + c // 2][:, (c % 2) * BLK:(c % 2 + 1) * BLK],
                                   wb[:, q, c * P:(c + 1) * P], xbT[:, q % 2, :], start=True, stop=True)
                mm.then_inc(S["h_full"], 1)

            def down(j, q):
                p = q % 2
                pe.wait_ge(S["gelu_done"], j + (base + 1))
                if base or not isinstance(j, int) or j >= 2:
                    pe.wait_ge(S["ye_evac"], j + (base - 1))
                for t in range(2):
                    for c in range(FC):
                        mm = pe.matmul(YB[p][:, t * D:(t + 1) * D], hT[:, p, c * BLK + t * P:c * BLK + (t + 1) * P],
                                       wb[:, q, DFF + c * D:DFF + (c + 1) * D], start=(c == 0), stop=(c == FC - 1))
                mm.then_inc(S["ye_full"], 1)

            def step(j, q, i, more=2):
                if more >= 2:
                    turn(j + 2, (q + 2) % NBUF, i + (q + 2) // NBUF)
                if more >= 1:
                    up(j + 1, (q + 1) % NBUF, i + (q + 1) // NBUF)
                down(j, q)

            turn(0, 0, 0)
            turn(1, 1, 0)
            up(0, 0, 0)
            for j in range(NBUF):
                step(j, j, 0)
            m = (nblk - 2) // NBUF * NBUF
            quads(pe, NBUF, m - 1, step)
            for j in range(m, nblk):
                step(j, j % NBUF, j // NBUF, more=min(2, nblk - 1 - j))

        def ffn_scalar(act, nblk, base, counts):
            HB = bank[2:6]

            def gelu(j, q, i):
                p = q % 2
                act.wait_ge(S["h_full"], j + (base + 1))
                act.wait_ge(S[f"w_in{q}"], (i + (counts[q] + 1)) * 32)
                for c in range(FC):
                    ins = act.activation(hT[:, p, c * BLK:(c + 1) * BLK], HB[2 * p + c // 2][:, (c % 2) * BLK:(c % 2 + 1) * BLK],
                                         ACT.Gelu, bias=wb[:, q, 2 * DFF + c:2 * DFF + c + 1])
                ins.then_inc(S["gelu_done"], 1)

            quads(act, 0, nblk - 1, gelu)

        def ffn_vector(v, nblk, base, counts):
            XT, YB = bank[0:2], bank[6:8]
            before = (base + 1) // 2, base // 2

            def evac_x(j, p):
                v.wait_ge(S["xT_full"], j + (base + 1))
                v.tensor_copy(xbT[:, p, :], XT[p][:, 0:BLK]).then_inc(S["xT_evac"], 1)

            def add_b2(j, q, i):
                p = q % 2
                v.wait_ge(S["ye_full"], j + (base + 1))
                v.wait_ge(S[f"w_in{q}"], (i + (counts[q] + 1)) * 32)
                if not isinstance(j, int) or j >= 2 or base:
                    v.wait_ge(S[f"stored{p}"], (i * 2 + (q // 2 + before[p])) * 16)
                v.tensor_tensor(yb[:, p, :].rearrange("p (t d) -> p t d", t=2),
                                YB[p][:, 0:2 * D].rearrange("p (t d) -> p t d", t=2),
                                b2b[:, q].unsqueeze(1).to_broadcast([P, 2, D]), ALU.add).then_inc(S["ye_evac"], 1)

            def step(j, q, i, more=True):
                if more:
                    evac_x(j + 2, q % 2)
                add_b2(j, q, i)

            evac_x(0, 0)
            evac_x(1, 1)
            for j in range(NBUF):
                step(j, j, 0)
            m = (nblk - 2) // NBUF * NBUF
            quads(v, NBUF, m - 1, step)
            for j in range(m, nblk):
                step(j, j % NBUF, j // NBUF, more=j + 2 < nblk)

        loads0 = (0,) * NBUF
        loads1 = tuple((NBLK0 + NBUF - 1 - q) // NBUF for q in range(NBUF))

        def stores(layer):
            return (NBLK0 + 1) // 2 + layer * ((NBLK1 + 1) // 2), NBLK0 // 2 + layer * (NBLK1 // 2)

        M1_0 = LG0[:, 256 * 2:256 * 3]
        mem0 = [LG0[:, 0:256], LG0[:, 256:512], LG0[:, 768:1024], LG0[:, 1024:1280], LG0[:, 1280:1792],
                LG0[:, 1792:2304], LG0[:, 2304:2336], LG0[:, 2336:2368], LG0[:, 2368:2400], LG0[:, 2400:2432],
                LG0[:, 2432:2496], LG0[:, 2496:2816]]
        RANK0 = LG0[:, 2816:3072]
        mem1 = [LG, EQ, R1, R2, TOT, INC, MX, KM, MX2, PZ, CNT, CMP]
        xr = RA[:, :].rearrange("p (t d) -> p t d", d=D)
        NORM1 = (range(0, 12), range(12, 24), range(24, NT))
        RB = lambda b: bass.ds(b * N, N)

        block = ctx.enter_context(nc.Block())

        @block.sync
        def _(sp):
            sp.dma_start(const[:, :], a["const"]).then_inc(S["const_in"], 16)
            for h in range(2):
                s = slice(h * NT // 2, (h + 1) * NT // 2)
                sp.dma_start(RS_[:, s], x_v[:, s]).then_inc(S[f"x_in{h}"], 16)
            sp.dma_start(gateb, a["L0_ffn_gate_b"].unsqueeze(0).to_broadcast([P, E])).then_inc(S["gate_in"], 16)
            sp.dma_start(gamma0, a["L0_attn_gamma"].unsqueeze(1)).then_inc(S["gate_in"], 16)
            sp.dma_start(gw0, a["L0_ffn_gate_W"]).then_inc(S["gate_in"], 16)
            for h in range(2):
                sp.dma_start(qscale[64 * h:64 * h + 64], a["L0_attn_q_scale"].unsqueeze(1)).then_inc(S["w_in"], 16)
                sp.dma_start(kscale[64 * h:64 * h + 64], a["L0_attn_k_scale"].unsqueeze(1)).then_inc(S["w_in"], 16)
            sp.dma_start(nkp, a["nkp"]).then_inc(S["w_in"], 16)
            sp.dma_start(wqkv[:, 0:H * DH], a["L0_attn_w_q"]).then_inc(S["w_in"], 16)
            sp.dma_start(wqkv[:, H * DH:3 * H * DH], a["L0_attn_w_kv"]).then_inc(S["w_in"], 16)
            sp.dma_start(alibi, a["alibi"]).then_inc(S["w_in"], 16)
            sp.dma_start(nvT, a["nvT"]).then_inc(S["w_in"], 16)
            sp.dma_start(wo0, a["L0_attn_w_out"].rearrange("(c p) n -> p c n", p=P)).then_inc(S["w_in"], 16)
            sp.wait_ge(S["zero_done"], 1)
            sp.dma_start(xe.rearrange("(p r c) d -> p r (c d)", p=P, c=2),
                         zeros[:, 0:2 * D].unsqueeze(1).to_broadcast([P, NBLK1, 2 * D])).then_inc(S["xe_zero"], 16)

            def load_xa(b, p):
                sp.dma_start(xa[:, p], RA[:, RB(b)]).then_inc(S[f"xa_in{p}"], 16)

            sp.wait_ge(S["tok2_evac"], 1)
            load_xa(0, 0)
            load_xa(1, 1)

            def attn_step(b, p):
                sp.wait_ge(S["sn_full"], b + 2)
                load_xa(b + 3, 1 - p)

            sp.wait_ge(S["tok2_evac"], NT // 4)
            sp.wait_ge(S["sn_full"], 1)
            sp.wait_ge(S["ring_evac"], ring_use(-1, ("unit", NU - 1, 0)) + 1)
            load_xa(2, 0)
            pairs(sp, 0, NB - 4, attn_step)

            sp.wait_ge(S["ring_evac"], ring_use(NB - 2, ("qk", NQ - 1, 1), 1) + 1)
            ffn_sync(sp, 0, NBLK0, 0, 16 * NT)
            sp.dma_start(RA[:, :].rearrange("p (t d) -> p t d", d=D), x_v).then_inc(S["x_back"], 16)
            sp.dma_start(gamma1, a["L1_attn_gamma"].unsqueeze(1)).then_inc(S["l1w_in"], 16)
            sp.dma_start(beta1, a["L1_attn_beta"].unsqueeze(1)).then_inc(S["l1w_in"], 16)
            sp.dma_start(bfc, a["L1_attn_bfc"].unsqueeze(0).to_broadcast([P, D])).then_inc(S["l1w_in"], 16)
            sp.dma_start(gw1, a["L1_ffn_Wg"]).then_inc(S["gate1_in"], 16)
            sp.wait_ge(S["y_evac"], 2 * NB)
            for w, name in ((wq1, "L1_attn_Wq"), (wk1, "L1_attn_Wk"), (wv1, "L1_attn_Wv"), (wfc, "L1_attn_Wfc")):
                sp.dma_start(w, a[name]).then_inc(S["l1w_in"], 16)

            sp.wait_ge(S["tok_evac"], 2 * (NT // 4))

            def load_xa1(b, p):
                sp.dma_start(xa1[:, p], XN1T[:, RB(b)]).then_inc(S[f"xa1_in{p}"], 16)

            load_xa1(0, 0)
            load_xa1(1, 1)

            def attn1_step(b, p):
                sp.wait_ge(S["qkv1_full"], b + 1)
                load_xa1(b + 2, p)

            pairs(sp, 0, NB - 3, attn1_step)

            ffn_sync(sp, 1, NBLK1, NBLK0, 16 * 3 * NT)
            for q in range(8):
                s = slice(4 * q, 4 * q + 4)
                sp.wait_ge(S["out_ready"], q + 1)
                sp.dma_start(out_v[:, s], RA[:, 512 * q:512 * q + 512].rearrange("p (t d) -> p t d", d=D))\
                  .then_inc(S["out_done"], 16)
            sp.wait_ge(S["out_done"], 16 * 8)

        @block.gpsimd
        def _(pool):
            pool.memset(zeros, 0.0).then_inc(S["zero_done"], 1)
            pool.memset(ones[:, :], 1.0).then_inc(S["ones_ready"], 1)
            pool.memset(c15, 1.5).then_inc(S["c15_ready"], 1)
            pool.wait_ge(S["c15_ready"], 1)

            def squares(a_, use):
                for i in range(NQ):
                    t, k = UNITS[i]
                    pool.wait_ge(S["ring_evac"], use(i) + 1)
                    if i >= 2:
                        pool.wait_ge(S["ss_done"], a_ * NQ + (i - 1))
                    r = raw[:, t, 512 * k:512 * k + 512]
                    pool.tensor_tensor(sq[:, i % 2], r, r, ALU.mult).then_inc(S["sq_done"], 1)

            def normalise(a_):
                pool.wait_ge(S["seed_done"], a_ + 1)
                y, n = rn[:, :, :].rearrange("p t n -> p (t n)"), 0
                x = xh[:, :, :].rearrange("p t n -> p (t n)")
                for _ in range(3):
                    for out, i0, i1, op in ((nw1, y, y, ALU.mult), (nw2, nw1, x, ALU.mult),
                                            (nw1, nw2, c15, ALU.add), (y, y, nw1, ALU.mult)):
                        pool.tensor_tensor(out, i0, i1, op).then_inc(S["newton"], 1)
                        n += 1
                        pool.wait_ge(S["newton"], a_ * 12 + n)
                for t in range(2):
                    for k in range(4):
                        pool.tensor_tensor(qkn[:, t, 512 * k:512 * k + 512].rearrange("p (h d) -> p h d", d=DH),
                                           raw[:, t, 512 * k:512 * k + 512].rearrange("p (h d) -> p h d", d=DH),
                                           rn[:, t, 8 * k:8 * k + 8].unsqueeze(2).to_broadcast([P, 8, DH]),
                                           ALU.mult).then_inc(S["qn_done"], 1)

            squares(0, lambda i: ring_use(-1, ("unit", i, 0)))
            normalise(0)
            squares(1, lambda i: ring_use(-1, ("unit", i, 1)))

            def step(b, p):
                normalise(b + 1)
                squares(b + 2, lambda i: ring_use(b, ("unit", i, 2)))

            pairs(pool, 0, NB - 5, step)
            pool.wait_ge(S["xe_zero"], 16)
            for b, tiles in ((NB - 4, range(0, 8)), (NB - 3, range(8, 16))):
                normalise(b + 1)
                scatter_rows(pool, 0, tiles)
                squares(b + 2, lambda i: ring_use(b, ("unit", i, 2)))
            normalise(NB - 1)
            scatter_rows(pool, 0, range(16, NT))

            for p in range(2):
                pool.wait_ge(S[f"stored{p}"], 16 * stores(0)[p])
            gather_rows(pool, 0)
            pool.wait_ge(S["y_evac"], 2 * NB)
            for q in range(8):
                sl = slice(4 * q, 4 * q + 4)
                pool.wait_ge(S["silu_done"], q + 1)
                pool.tensor_tensor(RS_[:, sl], RS_[:, sl], XN[:, sl], ALU.mult).then_inc(S["gated"], 1)
            scatter_rows(pool, 1)
            pool.memset(GA[:, :, :, :].rearrange("p k t n -> p (k t n)"), 0.0).then_inc(S["zero_done"], 1)
            pool.wait_ge(S["zero_done"], 2)
            for p in range(2):
                pool.wait_ge(S[f"stored{p}"], 16 * stores(1)[p])
            gather_rows(pool, 1)

        @block.tensor
        def _(pe):
            def gate_logits(layer, first, gw, XT, turned, groups):
                def logits(g):
                    pe.wait_ge(S["tok_evac"], first + g + 1)
                    for i in range(4 * g, 4 * g + 4):
                        mm = pe.matmul(MISC[:, E * i:E * i + E], XT[:, P * i:P * i + P], gw, start=True, stop=True)
                    return mm
                for g in groups:
                    pe.wait_ge(S["xn_ready"], layer * NT + 4 * g + 4)
                    if g >= 2:
                        pe.wait_ge(S["tok_evac"], first + g - 1)
                    for i in range(4):
                        mm = pe.transpose(turned[g % 2][:, P * i:P * i + P], XN[:, 4 * g + i, :], ident)
                    mm.then_inc(S["tok_T"], 1)
                    if layer == 0:
                        if g < NT // 8:
                            pe.wait_ge(S["xn2_ready"], 4 * g + 4)
                        else:
                            pe.wait_ge(S["xn2b_ready"], 4 * g + 4 - NT // 2)
                        if g >= 2:
                            pe.wait_ge(S["tok2_evac"], g - 1)
                        for i in range(4):
                            mm = pe.transpose(OBANK[g % 2][:, P * i:P * i + P], XN2[:, 4 * g + i, :], ident)
                        mm.then_inc(S["tok2_T"], 1)
                    if g > groups[0]:
                        logits(g - 1)
                mm = logits(groups[-1])
                if groups[-1] == NT // 4 - 1:
                    mm.then_inc(S["logits_full"], 1)

            def ranks(layer, M1, M2):
                pe.wait_ge(S["mask_ready"], (1, 3)[layer])
                for k, M in enumerate((M1, M2)[:1 + layer]):
                    pe.matmul(SBANK[0][:, 256 * k:256 * k + 256], tri, M, start=True, stop=True)
                    mm = pe.matmul(SBANK[1][:, 256 * k:256 * k + 256], ones[:, :], M, start=True, stop=True)
                mm.then_inc(S["rank_full"], 1)

            pe.wait_ge(S["const_in"], 16)
            pe.wait_ge(S["ones_ready"], 1)
            pe.wait_ge(S["gate_in"], 48)
            gate_logits(0, 0, gw0, XNT, SBANK, range(1))

            def ring_in(use, bnk, b, p, more=2):
                n = ring_use(b, use, more)
                if not isinstance(n, int) or n >= 2:
                    pe.wait_ge(S["ring_evac"], n - 1)
                if use[0] == "unit":
                    t, k = UNITS[use[1]]
                    mm = pe.matmul(RING[bnk][:, :], xa[:, p, t * P:(t + 1) * P], wqkv[:, 512 * k:512 * k + 512],
                                   start=True, stop=True)
                elif use[0] == "qk":
                    t, k = use[1] // 4, use[1] % 4
                    pe.wait_ge(S["qn_done"], b * NQ + (use[1] + 1 + NQ))
                    for c in range(4):
                        mm = pe.transpose(RING[bnk][:, P * c:P * c + P], qkn[:, t, 512 * k + P * c:512 * k + P * c + P],
                                          ident)
                else:
                    pe.wait_ge(S["on_done"], b * 2 + (use[1] + 1))
                    for c in range(4):
                        mm = pe.transpose(RING[bnk][:, P * c:P * c + P],
                                          On[:, 512 * use[2] + P * c:512 * use[2] + P * c + P], ident)
                mm.then_inc(S["ring_full"], 1)

            def scores(p, g):
                t, heads = GROUPS[g]
                n = P * (t + 1)
                for k, h in enumerate(heads):
                    r = 64 * (h % 2)
                    mm = pe.matmul(SBANK[g % 2][:, n * k:n * k + n], qT[r:r + 64, p, h // 2, t * P:(t + 1) * P],
                                   kT[r:r + 64, p, h // 2, 0:n], start=True, stop=True)
                mm.then_inc(S["s_full"], 1)

            def null_scores(p):
                for t in range(2):
                    mm = pe.matmul(MISC[:, 32 * t:32 * t + 32], xa[:, p, t * P:(t + 1) * P], wn, start=True, stop=True)
                mm.then_inc(S["sn_full"], 1)

            def turn_p(b, g):
                pe.wait_ge(S["exp_done"], b * NG + (g + 1))
                for k in range(4):
                    mm = pe.transpose(TRB[:, P * k:P * k + P], Pb[:, g % 3, P * k:P * k + P], ident)
                mm.then_inc(S["pt_full"], 1)

            def weigh(b, p, g):
                t, heads = GROUPS[g]
                pe.wait_ge(S["pt_evac"], b * NG + (g + 1))
                for k, h in enumerate(heads):
                    for j in range(t + 1):
                        o = OBANK[h // 8][:, DH * (h % 8):DH * (h % 8) + DH]
                        mm = pe.matmul(o, PTb[:, g % 2, P * ((t + 1) * k + j):P * ((t + 1) * k + j) + P],
                                       Vt[:, p, j, DH * h:DH * h + DH], start=(h % 8 == 0 and j == 0), stop=(j == t),
                                       skip_group_check=True)
                if g in (3, NG - 1):
                    mm.then_inc(S["o_full"], 1)

            def turn_null(b, t):
                pe.wait_ge(S["pn_scaled"], b * 2 + (t + 1))
                pe.transpose(MISC[0:2 * H, 0:P], pns[:, 32 * t:32 * t + 32], ident).then_inc(S["pnT_full"], 1)

            def project(b, t, more):
                pe.wait_ge(S["pnT_evac"], b * 2 + (t + 1))
                pe.matmul(MISC[:, 0:D], pnT, nvw, start=True, stop=False)
                pe.wait_ge(S["ring_evac"], ring_use(b, ("out", t, 1), more) + 1)
                for c in range(HC):
                    mm = pe.matmul(MISC[:, 0:D], OnT[:, c], wo0[:, c], start=False, stop=(c == HC - 1))
                mm.then_inc(S["y_full"], 1)

            def step(b, p, i, more=2):
                def ring(g, part):
                    for use in ring_uses(g, part, more):
                        if use == ("unit", 0, 2):
                            pe.wait_ge(S[f"xa_in{p}"], (i + 2) * 16)
                        ring_in(use, ring_bank(use, more), b, (p + use[2]) % 2, more)
                for g in range(NG):
                    if g == NG - 3 and more:
                        pe.wait_ge(S["ring_evac"], ring_use(b, ("qk", NQ - 1, 1), more) + 1)
                        pe.wait_ge(S["y_evac"], b * 2 + 1)
                        null_scores(1 - p)
                    if g + 2 < NG or more:
                        pe.wait_ge(S["ttr_done"], b * NG + (g + 1))
                        if g + 2 < NG:
                            scores(p, g + 2)
                        else:
                            scores(1 - p, g + 2 - NG)
                    if g == 6:
                        turn_null(b, 0)
                    ring(g, 0)
                    if g == 7:
                        project(b, 0, more)
                    if g == 5:
                        pe.wait_ge(S["on_done"], b * 2 + 1)
                    if g:
                        weigh(b, p, g - 1)
                    ring(g, 1)
                    turn_p(b, g)
                ring(NG, 0)
                weigh(b, p, NG - 1)
                for use in ring_uses(NG, 1, more):
                    if use == ("out", 1, 0):
                        turn_null(b, 1)
                    ring_in(use, ring_bank(use, more), b, (p + use[2]) % 2, more)
                project(b, 1, more)

            pe.wait_ge(S["w_in"], 16 * 10)
            for use in RING_FIRST:
                if use == ("qk", 0, 0):
                    gate_logits(0, 0, gw0, XNT, SBANK, range(1, NT // 4))
                if use == ("unit", 0, use[2]):
                    pe.wait_ge(S[f"xa_in{use[2]}"], 16)
                if use == ("unit", 0, 1):
                    pe.wait_ge(S["nk_ready"], 1)
                    pe.transpose(TRB[:, 0:2 * H], nkp, ident[0:2 * H, 0:2 * H])
                    for c in range(HC):
                        mm = pe.matmul(TRB[0:2 * H, P:2 * P], nvT[:, c], wo0[:, c], start=(c == 0), stop=(c == HC - 1))
                    mm.then_inc(S["nk_full"], 1)
                    ranks(0, M1_0, None)
                    pe.wait_ge(S["tok2_evac"], NT // 4)
                    for c in range(HC):
                        mm = pe.transpose(OBANK[c // 4][:, P * (c % 4):P * (c % 4) + P], wqkv[:, P * c:P * c + P], ident)
                    mm.then_inc(S["wqT_full"], 1)
                if use == ("unit", 8, 0):
                    pe.wait_ge(S["nk_evac"], 1)
                    pe.wait_ge(S["wqT_evac"], 1)
                    for c in range(HC):
                        mm = pe.matmul(TRB[:, 4 * c:4 * c + 4], OnT[:, c], nkT[:, 4 * c:4 * c + 4], start=True, stop=True)
                    mm.then_inc(S["wn_full"], 1)
                    pe.wait_ge(S["wn_evac"], 1)
                    pe.wait_ge(S["rank_evac"], 1)
                    pe.wait_ge(S["ring_evac"], ring_use(-1, ("qk", NQ - 1, 0)) + 1)
                    null_scores(0)
                    scores(0, 0)
                    scores(0, 1)
                ring_in(use, ring_bank(use, start=True), -1, use[2])
            with pe.Fori(0, (NB - 2) // 2) as i:
                step(i * 2, 0, i)
                step(i * 2 + 1, 1, i)
            step(NB - 2, 0, (NB - 2) // 2, more=1)
            pe.wait_ge(S["y_evac"], 2 * (NB - 1))
            pe.wait_ge(S["ttr_done"], (NB - 1) * NG + 2)
            ffn_tensor(pe, NBLK0, 0, loads0)
            pe.wait_ge(S["ye_evac"], NBLK0)
            step(NB - 1, 1, (NB - 1) // 2, more=0)

            pe.wait_ge(S["gate1_in"], 16)
            pe.wait_ge(S["y_evac"], 2 * NB)
            gate_logits(1, NT // 4, gw1, XN1T, RING, range(NT // 4))
            ranks(1, M1, M2)
            pe.wait_ge(S["l1w_in"], 16 * 7)

            QK, VB, SC, PT, OB = bank[0:2], bank[4:6], bank[6], bank[7], bank[2]

            def qkv1(b, p, n):
                pe.wait_ge(S[f"xa1_in{p}"], n)
                pe.matmul(QK[p][:, 0:N], wq1, xa1[:, p], start=True, stop=True)
                pe.matmul(QK[p][:, N:2 * N], wk1, xa1[:, p], start=True, stop=True)
                for t in range(2):
                    mm = pe.matmul(VB[p][:, t * D:(t + 1) * D], xa1[:, p, t * P:(t + 1) * P], wv1, start=True, stop=True)
                mm.then_inc(S["qkv1_full"], 1)

            def scores1(b, p):
                pe.wait_ge(S["qk1_evac"], b + 1)
                pe.matmul(SC[:, 0:P], qk1[:, p, 0:P], qk1[:, p, N:N + P], start=True, stop=True)
                pe.matmul(SC[:, P:P + N], qk1[:, p, P:N], qk1[:, p, N:2 * N], start=True, stop=True)\
                  .then_inc(S["s1_full"], 1)

            def step1(b, p, i, more=2):
                if more >= 1:
                    pe.wait_ge(S["ttr1_done"], b + 1)
                    scores1(b + 1, 1 - p)
                pe.wait_ge(S["exp1_done"], b + 1)
                for k in range(3):
                    mm = pe.transpose(PT[:, P * k:P * k + P], p1b[:, p, P * k:P * k + P], ident)
                mm.then_inc(S["pt1_full"], 1)
                if more >= 2:
                    pe.wait_ge(S["v1_evac"], b + 1)
                    pe.wait_ge(S["qk1_evac"], b + 1)
                    qkv1(b + 2, p, (i + 2) * 16)
                pe.wait_ge(S["v1_evac"], b + 1)
                pe.wait_ge(S["pt1_evac"], b + 1)
                for t, k, j in ((0, 0, 0), (1, 1, 0), (1, 2, 1)):
                    mm = pe.matmul(OB[:, t * D:(t + 1) * D], pt1[:, P * k:P * k + P],
                                   v1[:, p, j * D:(j + 1) * D], start=(j == 0), stop=(j == t))
                mm.then_inc(S["o1_full"], 1)

            qkv1(0, 0, 16)
            qkv1(1, 1, 16)
            scores1(0, 0)
            with pe.Fori(0, (NB - 2) // 2) as i:
                step1(i * 2, 0, i)
                step1(i * 2 + 1, 1, i)
            for b in range(NB - 2, NB):
                step1(b, b % 2, b // 2, more=NB - 1 - b)

            pe.wait_ge(S["o1_done"], NB)
            ffn_tensor(pe, NBLK1, NBLK0, loads1)

            def fc(g):
                pe.wait_ge(S["ao_evac"], g + 1)
                if g >= 2:
                    pe.wait_ge(S["attn1_done"], g - 1)
                for i in range(4):
                    mm = pe.matmul(bank[6 + g % 2][:, P * i:P * i + P], XN1T[:, 512 * g + P * i:512 * g + P * i + P], wfc,
                                   start=True, stop=True)
                mm.then_inc(S["fc_full"], 1)
            pe.wait_ge(S["ye_evac"], NBLK0 + NBLK1)
            for g in range(NT // 4):
                pe.wait_ge(S["ao_ready"], 4 * g + 4)
                if g >= 2:
                    pe.wait_ge(S["ao_evac"], g - 1)
                for i in range(4):
                    mm = pe.transpose(bank[4 + g % 2][:, P * i:P * i + P], AO[:, 4 * g + i, :], ident)
                mm.then_inc(S["ao_T"], 1)
                if g:
                    fc(g - 1)
            fc(NT // 4 - 1)

        @block.scalar
        def _(act):
            normalise_tiles(act, RS_, XN, 0, NT // 2, 1, S["xn_ready"])
            normalise_tiles(act, RS_, XN, NT // 2, NT // 2, 2, S["xn_ready"])
            normalise_tiles(act, XN, XN2, 0, NT // 2, 3, S["xn2_ready"])
            act.wait_ge(S["gate_in"], 48)

            def tokens_out(groups):
                for g in groups:
                    act.wait_ge(S["tok_T"], g + 1)
                    act.activation(XNT[:, 512 * g:512 * g + 512], SBANK[g % 2][:, :], ACT.Copy).then_inc(S["tok_evac"], 1)
                    act.wait_ge(S["tok2_T"], g + 1)
                    act.activation(RA[:, 512 * g:512 * g + 512], OBANK[g % 2][:, :], ACT.Copy, scale=gamma0)\
                       .then_inc(S["tok2_evac"], 1)
            tokens_out(range(1))

            def ring_out(use, n_use, bnk, p):
                act.wait_ge(S["ring_full"], n_use + 1)
                src = RING[bnk]
                kind, n = use[0], use[1]
                if kind == "unit":
                    t, k = UNITS[n]
                    dst = raw[:, t, 512 * k:512 * k + 512] if k < 4 else Vt[:, p, t, 512 * (k - 4):512 * (k - 3)]
                    ins = act.activation(dst, src[:, :], ACT.Copy)
                elif kind == "qk":
                    t, k = n // 4, n % 4
                    s4 = src[:, :].rearrange("p (c n) -> p c n", c=4)
                    if k < 2:
                        ins = act.activation(qT[:, p, 4 * k:4 * k + 4, t * P:(t + 1) * P], s4, ACT.Copy, scale=qscale)
                    else:
                        ins = act.activation(kT[:, p, 4 * (k - 2):4 * (k - 2) + 4, t * P:(t + 1) * P], s4, ACT.Copy)
                else:
                    n = use[2]
                    ins = act.activation(OnT[:, 4 * n:4 * n + 4], src[:, :].rearrange("p (c n) -> p c n", c=4), ACT.Copy)
                ins.then_inc(S["ring_evac"], 1)

            def probs(b, g):
                t, heads = GROUPS[g]
                n = P * (t + 1)
                act.wait_ge(S["ttr_done"], b * NG + (g + 1))
                for k, h in enumerate(heads):
                    ins = act.activation(Pb[:, g % 3, n * k:n * k + n], Sb[:, g % 3, n * k:n * k + n], ACT.Exp,
                                         bias=nm_t(t, h), scale=-1.0,
                                         accum_out=den_t(t, h))
                ins.then_inc(S["exp_done"], 1)

            def nm_t(t, h):
                return nm[:, 16 * t + h:16 * t + h + 1]

            def den_t(t, h):
                return den[:, 16 * t + h:16 * t + h + 1]

            def null_probs(b, t):
                act.wait_ge(S["nsub_done"], b * 2 + (t + 1))
                act.activation(pn[:, 32 * t:32 * t + 32], ntmp[:, 32 * t:32 * t + 32], ACT.Exp).then_inc(S["pn_done"], 1)

            def step(b, p, more=2):
                def ring(g):
                    for use in ring_uses(g, 0, more) + ring_uses(g, 1, more):
                        ring_out(use, ring_use(b, use, more), ring_bank(use, more), (p + use[2]) % 2)
                for g in range(NG):
                    probs(b, g)
                    if g == 3:
                        null_probs(b, 0)
                    if g == NG - 2:
                        null_probs(b, 1)
                    ring(g)
                ring(NG)

            for use in RING_FIRST:
                if use == ("unit", 0, 1):
                    act.wait_ge(S["wqT_full"], 1)
                    for o in range(2):
                        ins = act.activation(OnT[:, 4 * o:4 * o + 4], OBANK[o][:, :].rearrange("p (c n) -> p c n", c=4),
                                             ACT.Copy)
                    ins.then_inc(S["wqT_evac"], 1)
                if use == ("qk", 0, 0):
                    tokens_out(range(1, NT // 4))
                    act.wait_ge(S["scale_ready"], 1)
                ring_out(use, ring_use(-1, use), ring_bank(use, start=True), use[2])
            pairs(act, 0, NB - 3, step)
            step(NB - 2, 0, more=1)
            ffn_scalar(act, NBLK0, 0, loads0)
            step(NB - 1, 1, more=0)

            def silu(q):
                act.wait_ge(S[f"gathered{q}"], 16 * 4)
                g = XN[:, 4 * q:4 * q + 4, :]
                act.activation(g, g, ACT.Silu).then_inc(S["silu_done"], 1)
            for q in range(8):
                silu(q)

            for k, tiles in enumerate(NORM1):
                normalise_tiles(act, xr, XN, tiles[0], len(tiles), 5 + k, S["xn_ready"])
                for g in range(tiles[0] // 4, (tiles[-1] + 1) // 4):
                    act.wait_ge(S["tok_T"], NT // 4 + g + 1)
                    act.activation(XN1T[:, 512 * g:512 * g + 512], RING[g % 2][:, :], ACT.Copy)\
                       .then_inc(S["tok_evac"], 1)
            def evac_qk1(b, p):
                act.wait_ge(S["qkv1_full"], b + 1)
                act.activation(qk1[:, p], bank[p][:, :], ACT.Copy).then_inc(S["qk1_evac"], 1)

            def exp1(b, p):
                act.wait_ge(S["ttr1_done"], b + 1)
                act.activation(p1b[:, p, 0:P], s1b[:, p, 0:P], ACT.Exp, bias=nm1[:, 2 * p:2 * p + 1], scale=-1.0,
                               accum_out=den1[:, 2 * p:2 * p + 1])
                act.activation(p1b[:, p, P:P + N], s1b[:, p, P:P + N], ACT.Exp, bias=nm1[:, 2 * p + 1:2 * p + 2], scale=-1.0,
                               accum_out=den1[:, 2 * p + 1:2 * p + 2]).then_inc(S["exp1_done"], 1)

            def step1(b, p, more=2):
                if more >= 1:
                    exp1(b + 1, 1 - p)
                if more >= 2:
                    act.wait_ge(S["s1_full"], b + 1)
                    evac_qk1(b + 2, p)
            evac_qk1(0, 0)
            evac_qk1(1, 1)
            exp1(0, 0)
            pairs(act, 0, NB - 3, step1)
            step1(NB - 2, 0, more=1)
            ffn_scalar(act, NBLK1, NBLK0, loads1)
            act.wait_ge(S["gate_exp"], 1)
            act.activation(R1, R2, ACT.Exp).then_inc(S["wexp"], 1)

            for g in range(NT // 4):
                if g % 4 == 0:
                    normalise_tiles(act, AO, AO, 4 * g, NT // 2, 5 + len(NORM1) + g // 4, S["ao_ready"])
                act.wait_ge(S["ao_T"], g + 1)
                act.activation(XN1T[:, 512 * g:512 * g + 512], bank[4 + g % 2][:, :], ACT.Identity, bias=beta1,
                               scale=gamma1).then_inc(S["ao_evac"], 1)
            for q in range(8):
                act.wait_ge(S["gate_exp"], 2 + q)
                g = GA[:, 0, 4 * q:4 * q + 4, :]
                act.activation(g, g, ACT.Silu).then_inc(S["silu_done"], 1)

        @block.vector
        def _(v):
            link = Chain(v, S["dve_step"])
            def sums(a_, i):
                t, k = UNITS[i]
                v.wait_ge(S["sq_done"], a_ * NQ + (i + 1))
                v.tensor_reduce(ss[:, t, 8 * k:8 * k + 8], sq[:, i % 2].rearrange("p (h d) -> p h d", d=DH),
                                AX.X, ALU.add).then_inc(S["ss_done"], 1)

            def seeds(a_):
                x, y, half = (m[:, :, :].rearrange("p t n -> p (t n)") for m in (ss, rn, xh))
                v.wait_ge(S["ss_done"], (a_ + 1) * NQ)
                v.tensor_scalar(x, x, 1e-24, None, ALU.max).then_inc(S["seed_step"], 1)
                v.wait_ge(S["seed_step"], a_ * 2 + 1)
                v.tensor_scalar(half, x, -0.5, None, ALU.mult)
                v.tensor_scalar(y.bitcast(I32), x.bitcast(I32), 1, None, ALU.logical_shift_right)\
                 .then_inc(S["seed_step"], 1)
                v.wait_ge(S["seed_step"], a_ * 2 + 2)
                v.tensor_scalar(y.bitcast(I32), y.bitcast(I32), -1.0, RSQRT_MAGIC,
                                ALU.mult, ALU.add).then_inc(S["seed_done"], 1)

            for h in range(2):
                v.wait_ge(S[f"x_in{h}"], 16)
                norm_stats(v, link, RS_, h * NT // 2, NT // 2)
            for h in range(2):
                v.wait_ge(S["xn_ready"], (h + 1) * NT // 2)
                norm_stats(v, link, XN, h * NT // 2, NT // 2)
            for i in range(NT // 2, NT):
                v.tensor_scalar(XN2[:, i], XN[:, i], MV[:, i, 0:1], RSTD[:, i:i + 1], ALU.subtract, ALU.mult)\
                 .then_inc(S["xn2b_ready"], 1)
            for i in range(NQ):
                sums(0, i)
            seeds(0)
            v.wait_ge(S["w_in"], 16 * 10)
            link(v.tensor_scalar(T1[:, 0:1], qscale, kscale, 8.0, ALU.mult, ALU.mult))
            v.tensor_copy(qscale, T1[:, 0:1]).then_inc(S["scale_ready"], 1)
            v.wait_ge(S["scale_ready"], 1)
            R = 2 * H
            nk2 = RS_[0:R, 0, :]
            link(v.tensor_tensor(nk2, nkp, nkp, ALU.mult))
            link(v.tensor_reduce(VE[0:R, 0:1], nk2, AX.X, ALU.add))
            link(v.tensor_scalar(VE[0:R, 0:1], VE[0:R, 0:1], 1e-24, None, ALU.max))
            rsqrt(v, link, RSTD[0:R, 0:1], VE[0:R, 0:1], T1[0:R, 0:1], T2[0:R, 0:1])
            v.tensor_scalar(nkp, nkp, RSTD[0:R, 0:1], None, ALU.mult).then_inc(S["nk_ready"], 1)
            v.wait_ge(S["logits_full"], 1)
            v.wait_ge(S["gate_in"], 48)
            link(v.tensor_tensor(mem0[0].rearrange("p (t e) -> p t e", e=E),
                                 MISC[:, 0:256].rearrange("p (t e) -> p t e", e=E),
                                 gateb.unsqueeze(1).to_broadcast([P, NT, E]), ALU.add))
            masks(v, link, 0, mem0, M1_0, None)
            v.wait_ge(S["nk_full"], 1)
            v.tensor_scalar(nkT, TRB[:, 0:R], qscale, None, ALU.mult)
            v.tensor_copy(nvw, TRB[0:R, P:2 * P]).then_inc(S["nk_evac"], 1)

            def null_scores(b):
                v.wait_ge(S["sn_full"], b + 1)
                v.wait_ge(S["newton"], b * 12 + 12)
                for t in range(2):
                    ins = v.tensor_tensor(snr[:, 32 * t:32 * t + 32].rearrange("p (h n) -> p h n", n=2),
                                          MISC[:, 32 * t:32 * t + 32].rearrange("p (h n) -> p h n", n=2),
                                          rn[:, t, 0:H].unsqueeze(2).to_broadcast([P, H, 2]), ALU.mult)
                ins.then_inc(S["sn_step"], 1)
                v.wait_ge(S["sn_step"], b * 3 + 1)
                v.scalar_tensor_tensor(out=nsn, in0=snr, scalar=-1.0, in1=nbias, op0=ALU.mult,
                                       op1=ALU.subtract).then_inc(S["sn_step"], 1)
                v.wait_ge(S["sn_step"], b * 3 + 2)
                v.tensor_reduce(nmn, nsn.rearrange("p (h n) -> p h n", n=2), AX.X, ALU.min).then_inc(S["sn_step"], 1)
                v.wait_ge(S["sn_step"], b * 3 + 3)

            def rows_max(b, g):
                t, heads = GROUPS[g]
                n = P * (t + 1)
                v.wait_ge(S["s_full"], b * NG + (g + 1))
                v.sem_inc(S["scores_seen"], 1)
                for k, h in enumerate(heads):
                    ins = v.tensor_tensor_reduce(out=Sb[:, g % 3, n * k:n * k + n], in0=SBANK[g % 2][:, n * k:n * k + n],
                                                 in1=alibi[:, h, N - n:N], scale=-1.0,
                                                 scalar=nmn[:, 16 * t + h:16 * t + h + 1], op0=ALU.add, op1=ALU.min,
                                                 accum_out=nm[:, 16 * t + h:16 * t + h + 1])
                ins.then_inc(S["ttr_done"], 1)

            def null_sub(b, t):
                v.wait_ge(S["ttr_done"], b * NG + (4 if t == 0 else NG))
                v.tensor_tensor(ntmp[:, 32 * t:32 * t + 32].rearrange("p (h n) -> p h n", n=2),
                                nm[:, 16 * t:16 * t + 16].unsqueeze(2).to_broadcast([P, H, 2]),
                                nsn[:, 32 * t:32 * t + 32].rearrange("p (h n) -> p h n", n=2),
                                ALU.subtract).then_inc(S["nsub_done"], 1)

            def denominators(b, t):
                v.wait_ge(S["pn_done"], b * 2 + (t + 1))
                d = rden[:, 16 * t:16 * t + 16]
                v.tensor_reduce(d, pn[:, 32 * t:32 * t + 32].rearrange("p (h n) -> p h n", n=2), AX.X, ALU.add)\
                 .then_inc(S["den_step"], 1)
                v.wait_ge(S["den_step"], b * 4 + (2 * t + 1))
                v.wait_ge(S["exp_done"], b * NG + (4 if t == 0 else NG))
                v.tensor_tensor(d, d, den[:, 16 * t:16 * t + 16], ALU.add).then_inc(S["den_step"], 1)
                v.wait_ge(S["den_step"], b * 4 + (2 * t + 2))
                v.reciprocal(d, d).then_inc(S["rd1_done"], 1)
                v.wait_ge(S["rd1_done"], b * 2 + (t + 1))
                v.tensor_tensor(pns[:, 32 * t:32 * t + 32].rearrange("p (h n) -> p h n", n=2),
                                pn[:, 32 * t:32 * t + 32].rearrange("p (h n) -> p h n", n=2),
                                d.unsqueeze(2).to_broadcast([P, H, 2]), ALU.mult).then_inc(S["pn_scaled"], 1)

            def null_turned(b, t):
                v.wait_ge(S["pnT_full"], b * 2 + (t + 1))
                v.tensor_copy(pnT, MISC[0:2 * H, 0:P]).then_inc(S["pnT_evac"], 1)

            def out_norm(b, t):
                v.wait_ge(S["o_full"], b * 2 + (t + 1))
                v.wait_ge(S["rd1_done"], b * 2 + (t + 1))
                for o in range(2):
                    ins = v.tensor_tensor(On[:, 512 * o:512 * o + 512].rearrange("p (h d) -> p h d", d=DH),
                                          OBANK[o][:, :].rearrange("p (h d) -> p h d", d=DH),
                                          rden[:, 16 * t + 8 * o:16 * t + 8 * o + 8].unsqueeze(2).to_broadcast([P, 8, DH]),
                                          ALU.mult)
                ins.then_inc(S["on_done"], 1)

            def y_out(b, t):
                v.wait_ge(S["y_full"], b * 2 + (t + 1))
                v.tensor_copy(RS_[:, bass.ds(b * 2 + t, 1), :].rearrange("p t d -> p (t d)"), MISC[:, 0:D])\
                 .then_inc(S["y_evac"], 1)

            def step(b, p, more=2, routing=False):
                for g in range(NG):
                    if routing and g == 1:
                        v.wait_ge(S["ones_ready"], 1)
                        counts(v, link, 0, mem0)
                    if routing and g == 2:
                        blocks(v, link, 0, mem0)
                    if routing and g == 4:
                        owners(v, link, 0, mem0)
                    if routing and g == 8:
                        rows(v, link, 0, mem0, M1_0, None, RANK0)
                    if g == 8:
                        y_out(b, 0)
                    if g + 2 < NG:
                        rows_max(b, g + 2)
                    elif more:
                        if g + 2 == NG:
                            v.wait_ge(S["nsub_done"], b * 2 + 2)
                            null_scores(b + 1)
                        rows_max(b + 1, g + 2 - NG)
                    if g == 2:
                        null_sub(b, 0)
                    if g == NG - 3:
                        null_sub(b, 1)
                    if g == 6:
                        null_turned(b, 0)
                    if more == 2 and g in SUMS:
                        sums(b + 2, SUMS[g])
                    if g == 4:
                        denominators(b, 0)
                        out_norm(b, 0)
                    v.wait_ge(S["pt_full"], b * NG + (g + 1))
                    v.tensor_copy(PTb[:, g % 2, :], TRB[:, :]).then_inc(S["pt_evac"], 1)
                denominators(b, 1)
                out_norm(b, 1)
                if more == 2:
                    for i in (4, 5):
                        sums(b + 2, i)
                null_turned(b, 1)
                if more == 2:
                    for i in (6, 7):
                        sums(b + 2, i)
                    seeds(b + 2)
                y_out(b, 1)

            SUMS = {6: 0, 7: 1, 10: 2, 11: 3}
            totals(v, link, 0, mem0, keep=RANK0)
            for i in range(NQ):
                sums(1, i)
            v.wait_ge(S["wn_full"], 1)
            v.tensor_copy(wn, TRB[:, 0:R]).then_inc(S["wn_evac"], 1)
            null_scores(0)
            rows_max(0, 0)
            rows_max(0, 1)
            seeds(1)
            step(0, 0, routing=True)
            step(1, 1)
            pairs(v, 2, NB - 3, step)
            step(NB - 2, 0, more=1)
            ffn_vector(v, NBLK0, 0, loads0)
            step(NB - 1, 1, more=0)

            v.wait_ge(S["x_back"], 16)
            for q in range(8):
                sl = slice(4 * q, 4 * q + 4)
                v.wait_ge(S["gated"], q + 1)
                v.tensor_tensor(xr[:, sl], xr[:, sl], RS_[:, sl], ALU.add).then_inc(S["x1_ready"], 1)
                for tiles in NORM1:
                    if tiles[-1] == 4 * q + 3:
                        v.wait_ge(S["x1_ready"], q + 1)
                        norm_stats(v, link, xr, tiles[0], len(tiles))

            v.wait_ge(S["logits_full"], 2)
            link(v.tensor_copy(LG, MISC[:, 0:256]))
            masks(v, link, 1, mem1, M1, M2)
            totals(v, link, 1, mem1)
            counts(v, link, 1, mem1)
            blocks(v, link, 1, mem1)
            rows(v, link, 1, mem1, M1, M2, SBANK[0])
            owners(v, link, 1, mem1)

            def v_out(b, i3):
                v.wait_ge(S["qkv1_full"], b + 1)
                v.tensor_copy(v1[:, i3], bank[4 + i3][:, 0:N]).then_inc(S["v1_evac"], 1)

            SCL = float(D) ** -0.5

            def rows_max1(b, p):
                v.wait_ge(S["s1_full"], b + 1)
                v.sem_inc(S["scores_seen"], 1)
                v.tensor_tensor_reduce(out=s1b[:, p, 0:P], in0=bank[6][:, 0:P], in1=mask1[:, P:2 * P], scale=-SCL,
                                       scalar=-NEG, op0=ALU.add, op1=ALU.min, accum_out=nm1[:, 2 * p:2 * p + 1])
                v.tensor_tensor_reduce(out=s1b[:, p, P:P + N], in0=bank[6][:, P:P + N], in1=mask1[:, :], scale=-SCL,
                                       scalar=-NEG, op0=ALU.add, op1=ALU.min, accum_out=nm1[:, 2 * p + 1:2 * p + 2])\
                 .then_inc(S["ttr1_done"], 1)

            def residual(b, p, i3):
                v.wait_ge(S["exp1_done"], b + 1)
                v.reciprocal(rd1[:, 2 * p:2 * p + 2], den1[:, 2 * p:2 * p + 2]).then_inc(S["rd1_done"], 1)
                v.wait_ge(S["o1_full"], b + 1)
                v.wait_ge(S["rd1_done"], b + (2 * NB + 1))
                for t in range(2):
                    ins = v.scalar_tensor_tensor(out=AO[:, bass.ds(b * 2 + t, 1), :].rearrange("p t d -> p (t d)"),
                                                 in0=bank[2][:, t * D:(t + 1) * D], scalar=rd1[:, 2 * p + t:2 * p + t + 1],
                                                 in1=v1[:, i3, t * D:(t + 1) * D], op0=ALU.mult, op1=ALU.add)
                ins.then_inc(S["o1_done"], 1)

            def step1(b, p, more=2):
                if more >= 1:
                    rows_max1(b + 1, 1 - p)
                v.wait_ge(S["pt1_full"], b + 1)
                v.tensor_copy(pt1, bank[7][:, 0:384]).then_inc(S["pt1_evac"], 1)
                residual(b, p, p)
                if more >= 2:
                    v.wait_ge(S["o1_done"], b + 1)
                    v_out(b + 2, p)
            v_out(0, 0)
            v_out(1, 1)
            rows_max1(0, 0)
            pairs(v, 0, NB - 3, step1)
            for b in range(NB - 2, NB):
                step1(b, b % 2, more=NB - 1 - b)
            v.wait_ge(S["o1_done"], NB)

            ffn_vector(v, NBLK1, NBLK0, loads1)
            gates(v, link, mem1, M1, M2)

            for h in range(2):
                norm_stats(v, link, AO, h * NT // 2, NT // 2)
            for g in range(NT // 4):
                v.wait_ge(S["fc_full"], g + 1)
                v.tensor_tensor(RS_[:, 4 * g:4 * g + 4, :], bank[6 + g % 2][:, :].rearrange("p (t d) -> p t d", d=D),
                                bfc.unsqueeze(1).to_broadcast([P, 4, D]), ALU.add).then_inc(S["attn1_done"], 1)

            def mix(q):
                v.wait_ge(S[f"gathered{q}"], 16 * 4 * 3)
                for i in range(4 * q, 4 * q + 4):
                    ins = v.tensor_scalar(GA[:, 0, i], GA[:, 0, i], G1W[:, i:i + 1], None, ALU.mult)
                link(ins)
                for i in range(4 * q, 4 * q + 4):
                    ins = v.scalar_tensor_tensor(out=GA[:, 0, i], in0=GA[:, 1, i], scalar=G2W[:, i:i + 1],
                                                 in1=GA[:, 0, i], op0=ALU.mult, op1=ALU.add)
                ins.then_inc(S["gate_exp"], 1)

            def combine(q):
                sl = slice(4 * q, 4 * q + 4)
                v.wait_ge(S["silu_done"], 8 + q + 1)
                link(v.tensor_tensor(RS_[:, sl], RS_[:, sl], GA[:, 0, sl, :], ALU.mult))
                v.tensor_tensor(xr[:, sl], xr[:, sl], RS_[:, sl], ALU.add).then_inc(S["out_ready"], 1)

            v.wait_ge(S["attn1_done"], NT // 4)
            for q in range(8):
                mix(q)
                if q:
                    combine(q - 1)
            combine(7)


def constants(np):
    c = np.zeros((P, C_END), np.float32)
    p = np.arange(P)
    c[:, C_ID:C_ID + P] = np.eye(P)
    c[:, C_TRI:C_TRI + P] = p[:, None] < p[None, :]
    start = 2.0 ** (-2.0 ** (-(np.log2(H) - 3.0)))
    slopes = np.array([start * start ** i for i in range(H)], np.float32)
    for t in range(2):
        for h in range(H):
            for n in range(NNULL):
                c[:, C_NB + 32 * t + 2 * h + n] = -(t * P + p + NNULL - n) * slopes[h]
    diag = np.where(p[None, :] > p[:, None], NEG, 0.0)
    c[:, C_M1 + P:C_M1 + 2 * P] = diag
    c[:, C_W8:C_W8 + E] = E - np.arange(E)
    c[:, C_RS:C_RS + E * NT] = np.arange(E * NT) % NT != 0
    c[:, C_THR:C_THR + NTHR] = BLK * np.arange(NTHR)
    c[:, C_JJ:C_JJ + NBLK1 + 1] = np.arange(NBLK1 + 1)
    alibi = np.zeros((P, H, N), np.float32)
    dist = (p[:, None] - p[None, :]).astype(np.float32)
    for h in range(H):
        alibi[:, h, 0:P] = -(dist + P) * slopes[h]
        alibi[:, h, P:N] = np.where(dist < 0, np.float32(NEG), -dist * slopes[h])
    return c, alibi


_INS = ['L0_attn_x', 'L0_attn_gamma', 'L0_attn_w_q', 'L0_attn_w_kv', 'L0_attn_q_scale', 'L0_attn_k_scale',
        'L0_attn_w_out', 'L0_ffn_gate_W', 'L0_ffn_gate_b', 'L1_attn_Wq', 'L1_attn_Wk', 'L1_attn_Wv', 'L1_attn_Wfc',
        'L1_attn_bfc', 'L1_attn_gamma', 'L1_attn_beta', 'L1_ffn_Wg']


def kernel(**inputs):
    import numpy as np
    import concourse.bacc as _bacc
    from concourse import mybir as _mybir
    from concourse.bass_utils import run_bass_kernel_spmd as _run

    given = {n: np.ascontiguousarray(inputs[n]) for n in _INS}
    nkv = np.asarray(inputs['L0_attn_null_kv']).reshape(H, NNULL, 2, DH)
    nkp = np.zeros((2 * H, P), np.float32)
    nvT = np.zeros((P, HC, 2 * H), np.float32)
    for h in range(H):
        half = slice(DH * (h % 2), DH * (h % 2) + DH)
        nkp[2 * h:2 * h + 2, half] = nkv[h, :, 0]
        nvT[half, h // 2, 2 * h:2 * h + 2] = nkv[h, :, 1].T
    given["nkp"], given["nvT"] = nkp, nvT
    for l in range(2):
        w2 = np.asarray(inputs[f'L{l}_ffn_W2']).reshape(E, FC, P, D).transpose(0, 2, 1, 3).reshape(E, P, DFF)
        b1 = np.asarray(inputs[f'L{l}_ffn_b1']).reshape(E, FC, P).transpose(0, 2, 1)
        given[f"wp_{l}"] = np.ascontiguousarray(np.concatenate([np.asarray(inputs[f'L{l}_ffn_W1']), w2, b1], axis=2))
        given[f"b2_{l}"] = np.ascontiguousarray(inputs[f'L{l}_ffn_b2'])
    given["const"], given["alibi"] = constants(np)

    nc = _bacc.Bacc("TRN2", target_bir_lowering=False, num_devices=1)
    arrays, a = {}, {}
    for name, x in given.items():
        arrays[f"in_{name}"] = x
        a[name] = nc.dram_tensor(f"in_{name}", x.shape, _mybir.dt.from_np(x.dtype), kind="ExternalInput").ap()
    a["out"] = nc.dram_tensor("out_0", (NB, N, D), _mybir.dt.float32, kind="ExternalOutput").ap()
    block_kernel(nc, a)
    r = _run(nc, [arrays], core_ids=[0])
    return r.results[0]["out_0"]
```
